# Optimizing a Trainium2 kernel written in Bass

```python
import numpy as np
import jax
import jax.numpy as jnp

def _softmax(x, axis=-1):
    return jax.nn.softmax(x, axis=axis)

def _gelu(x):
    return jax.nn.gelu(x, approximate=True)

def _silu(x):
    return jax.nn.silu(x)

def _sigmoid(x):
    return jax.nn.sigmoid(x)

def _layernorm(x, axis=-1, eps=1e-05):
    m = jnp.mean(x, axis=axis, keepdims=True)
    v = jnp.var(x, axis=axis, keepdims=True)
    return (x - m) / jnp.sqrt(v + eps)

def _scatter_add(tgt, idx, src, axis=0):
    return tgt.at[idx].add(src)

def _segment_sum(src, seg, n):
    return jax.ops.segment_sum(src, seg, n)
kernel_name = 'mk_gnn_preln_d4_gnn_r16_eeaaab'

def setup_inputs(seed: int=0):
    np.random.seed(seed)
    _w = jnp.asarray

    def _rec_inputs():
        import jax
        import jax.numpy as jnp
        _gk = jax.random.key(seed)
        x = -0.000202 + 1 * jax.random.normal(jax.random.fold_in(_gk, 1), (3125, 128), jnp.float32)
        src = jax.random.randint(jax.random.fold_in(_gk, 2), (100000,), 0, 3125, jnp.int32)
        dst = jax.random.randint(jax.random.fold_in(_gk, 3), (100000,), 0, 3125, jnp.int32)
        _o = jnp.argsort(dst, stable=True)
        src = src[_o]
        dst = dst[_o]
        edge_attr_4 = jax.random.uniform(jax.random.fold_in(_gk, 12), (100000, 4), jnp.float32, 0.0, 1)
        edge_type_16 = jax.random.randint(jax.random.fold_in(_gk, 14), (100000,), 0, 16, jnp.int32)
        edge_weight = jax.random.uniform(jax.random.fold_in(_gk, 15), (100000,), jnp.float32, 0.0, 1)
        return (x, src, dst, edge_attr_4, edge_type_16, edge_weight)
    x, src, dst, edge_attr_4, edge_type_16, edge_weight = _rec_inputs()

    def _L0_gnn_setup():
        import jax, jax.numpy as jnp
        import numpy as np
        D = 128
        STEPS = 2
        N = 3125
        E = 31250

        def _mlp2(h, W1, b1, W2, b2):
            return jax.nn.relu(h @ W1 + b1) @ W2 + b2
        key = jax.random.key(seed)
        ks = jax.random.split(key, 16)
        s = 1.0 / np.sqrt(2 * D)
        t = 1.0 / np.sqrt(D)
        inp = {'x': jax.random.normal(ks[0], (N, D), dtype=jnp.float32), 'edge_index': jax.random.randint(ks[1], (2, E), 0, N, dtype=jnp.int64), 'msg_W1': jax.random.uniform(ks[2], (2 * D, D), jnp.float32, -s, s), 'msg_b1': jnp.zeros((D,), jnp.float32), 'msg_W2': jax.random.uniform(ks[3], (D, D), jnp.float32, -t, t), 'msg_b2': jnp.zeros((D,), jnp.float32), 'upd_W1': jax.random.uniform(ks[4], (2 * D, D), jnp.float32, -s, s), 'upd_b1': jnp.zeros((D,), jnp.float32), 'upd_W2': jax.random.uniform(ks[5], (D, D), jnp.float32, -t, t), 'upd_b2': jnp.zeros((D,), jnp.float32), 'att_W1': jax.random.uniform(ks[6], (2 * D, D), jnp.float32, -s, s), 'att_b1': jnp.zeros((D,), jnp.float32), 'att_W2': jax.random.uniform(ks[7], (D, 1), jnp.float32, -t, t), 'att_b2': jnp.zeros((1,), jnp.float32), 'glb_W': jax.random.uniform(ks[8], (D, D), jnp.float32, -t, t), 'glb_b': jnp.zeros((D,), jnp.float32)}
        return inp
    _L0_gnn_all = _L0_gnn_setup()
    _L0_gnn_in = {k: v for k, v in _L0_gnn_all.items() if k in ('msg_W1', 'msg_b1', 'msg_W2', 'msg_b2', 'upd_W1', 'upd_b1', 'upd_W2', 'upd_b2', 'att_W1', 'att_b1', 'att_W2', 'att_b2', 'glb_W', 'glb_b')}
    del _L0_gnn_all

    def _L1_gnn_setup():
        import jax, jax.numpy as jnp
        import numpy as np
        N = 6250
        E = 40000
        D = 128

        def _weighted_mean_agg(ft, w, src, dst, n_nodes):
            m = ft[src] * w[:, None]
            msum = jax.ops.segment_sum(m, dst, num_segments=n_nodes)
            wsum = jax.ops.segment_sum(w, dst, num_segments=n_nodes)
            safe = jnp.where(wsum > 0, wsum, 1.0)
            return jnp.where((wsum > 0)[:, None], msum / safe[:, None], 0.0)
        key = jax.random.key(seed)
        ks = jax.random.split(key, 10)
        s = 1.0 / np.sqrt(D)
        feat = jax.random.normal(ks[0], (N, D), jnp.float32)
        w = jax.random.uniform(ks[1], (E,), jnp.float32)
        src = jax.random.randint(ks[2], (E,), 0, N, dtype=jnp.int32)
        dst = jax.random.randint(ks[3], (E,), 0, N, dtype=jnp.int32)
        W1 = jax.random.uniform(ks[4], (D, D), jnp.float32, -s, s)
        W2 = jax.random.uniform(ks[5], (D, D), jnp.float32, -s, s)
        sg = 1.0 / np.sqrt(D)
        w_ih = jax.random.uniform(ks[6], (3 * D, 2 * D), jnp.float32, -sg, sg)
        w_hh = jax.random.uniform(ks[7], (3 * D, D), jnp.float32, -sg, sg)
        b_ih = jax.random.uniform(ks[8], (3 * D,), jnp.float32, -sg, sg)
        b_hh = jax.random.uniform(ks[9], (3 * D,), jnp.float32, -sg, sg)
        return {'feat': feat, 'w': w, 'src': src, 'dst': dst, 'W1': W1, 'W2': W2, 'w_ih': w_ih, 'w_hh': w_hh, 'b_ih': b_ih, 'b_hh': b_hh}
    _L1_gnn_all = _L1_gnn_setup()
    _L1_gnn_in = {k: v for k, v in _L1_gnn_all.items() if k in ('W1', 'W2', 'w_ih', 'w_hh', 'b_ih', 'b_hh')}
    del _L1_gnn_all

    def _L2_gnn_setup():
        import jax, jax.numpy as jnp
        import numpy as np
        N_NODES = 6250
        N_EDGES = 100000
        HIDDEN = 128
        N_ETYPES = 4
        N_STEPS = 4

        def _gru_cell(x, h, W_ih, W_hh, b_ih, b_hh):
            gi = x @ W_ih.T + b_ih
            gh = h @ W_hh.T + b_hh
            ir, iz, inn = jnp.split(gi, 3, axis=1)
            hr, hz, hn = jnp.split(gh, 3, axis=1)
            r = jax.nn.sigmoid(ir + hr)
            z = jax.nn.sigmoid(iz + hz)
            n = jnp.tanh(inn + r * hn)
            return (1.0 - z) * n + z * h
        key = jax.random.key(seed)
        ks = jax.random.split(key, 10)
        s = 1.0 / np.sqrt(HIDDEN)
        node_feat = jax.random.normal(ks[0], (N_NODES, HIDDEN), dtype=jnp.float32)
        edge_index = jax.random.randint(ks[1], (2, N_EDGES), 0, N_NODES)
        edge_feat = jax.random.uniform(ks[2], (N_EDGES, N_ETYPES), dtype=jnp.float32)
        W_edge = jax.random.uniform(ks[3], (N_ETYPES, HIDDEN, HIDDEN), minval=-s, maxval=s, dtype=jnp.float32)
        b_edge = jax.random.uniform(ks[4], (N_ETYPES, HIDDEN), minval=-s, maxval=s, dtype=jnp.float32)
        W_ih = jax.random.uniform(ks[5], (3 * HIDDEN, HIDDEN), minval=-s, maxval=s, dtype=jnp.float32)
        W_hh = jax.random.uniform(ks[6], (3 * HIDDEN, HIDDEN), minval=-s, maxval=s, dtype=jnp.float32)
        b_ih = jax.random.uniform(ks[7], (3 * HIDDEN,), minval=-s, maxval=s, dtype=jnp.float32)
        b_hh = jax.random.uniform(ks[8], (3 * HIDDEN,), minval=-s, maxval=s, dtype=jnp.float32)
        return {'node_feat': node_feat, 'edge_index': edge_index, 'edge_feat': edge_feat, 'W_edge': W_edge, 'b_edge': b_edge, 'W_ih': W_ih, 'W_hh': W_hh, 'b_ih': b_ih, 'b_hh': b_hh}
    _L2_gnn_all = _L2_gnn_setup()
    _L2_gnn_in = {k: v for k, v in _L2_gnn_all.items() if k in ('W_edge', 'b_edge', 'W_ih', 'W_hh', 'b_ih', 'b_hh')}
    del _L2_gnn_all

    def _L3_gnn_setup():
        import jax, jax.numpy as jnp
        import numpy as np
        NUM_NODES = 3125
        IN_DIM = 128
        OUT_DIM = 128
        NUM_RELATIONS = 16
        NUM_BASES = 8
        NUM_EDGES = 37500
        key = jax.random.key(seed)
        k_x, k_ei, k_et, k_b, k_c, k_s = jax.random.split(key, 6)
        x = jax.random.normal(k_x, (NUM_NODES, IN_DIM), dtype=jnp.float32)
        edge_index = jax.random.randint(k_ei, (2, NUM_EDGES), 0, NUM_NODES, dtype=jnp.int32)
        edge_type = jax.random.randint(k_et, (NUM_EDGES,), 0, NUM_RELATIONS, dtype=jnp.int32)

        def xavier(k, shape, fan_in, fan_out):
            lim = float(np.sqrt(6.0 / (fan_in + fan_out)))
            return jax.random.uniform(k, shape, dtype=jnp.float32, minval=-lim, maxval=lim)
        bases = xavier(k_b, (NUM_BASES, IN_DIM, OUT_DIM), IN_DIM, OUT_DIM)
        coefficients = xavier(k_c, (NUM_RELATIONS, NUM_BASES), NUM_BASES, NUM_RELATIONS)
        self_loop = xavier(k_s, (IN_DIM, OUT_DIM), IN_DIM, OUT_DIM)
        return {'x': x, 'edge_index': edge_index, 'edge_type': edge_type, 'bases': bases, 'coefficients': coefficients, 'self_loop': self_loop}
    _L3_gnn_all = _L3_gnn_setup()
    _L3_gnn_in = {k: v for k, v in _L3_gnn_all.items() if k in ('bases', 'coefficients', 'self_loop')}
    del _L3_gnn_all
    return {'x': x, 'src': src, 'dst': dst, 'edge_attr_4': edge_attr_4, 'edge_type_16': edge_type_16, 'edge_weight': edge_weight, 'L0_gnn_msg_W1': _L0_gnn_in['msg_W1'], 'L0_gnn_msg_b1': _L0_gnn_in['msg_b1'], 'L0_gnn_msg_W2': _L0_gnn_in['msg_W2'], 'L0_gnn_msg_b2': _L0_gnn_in['msg_b2'], 'L0_gnn_upd_W1': _L0_gnn_in['upd_W1'], 'L0_gnn_upd_b1': _L0_gnn_in['upd_b1'], 'L0_gnn_upd_W2': _L0_gnn_in['upd_W2'], 'L0_gnn_upd_b2': _L0_gnn_in['upd_b2'], 'L0_gnn_att_W1': _L0_gnn_in['att_W1'], 'L0_gnn_att_b1': _L0_gnn_in['att_b1'], 'L0_gnn_att_W2': _L0_gnn_in['att_W2'], 'L0_gnn_att_b2': _L0_gnn_in['att_b2'], 'L0_gnn_glb_W': _L0_gnn_in['glb_W'], 'L0_gnn_glb_b': _L0_gnn_in['glb_b'], 'L1_gnn_W1': _L1_gnn_in['W1'], 'L1_gnn_W2': _L1_gnn_in['W2'], 'L1_gnn_w_ih': _L1_gnn_in['w_ih'], 'L1_gnn_w_hh': _L1_gnn_in['w_hh'], 'L1_gnn_b_ih': _L1_gnn_in['b_ih'], 'L1_gnn_b_hh': _L1_gnn_in['b_hh'], 'L2_gnn_W_edge': _L2_gnn_in['W_edge'], 'L2_gnn_b_edge': _L2_gnn_in['b_edge'], 'L2_gnn_W_ih': _L2_gnn_in['W_ih'], 'L2_gnn_W_hh': _L2_gnn_in['W_hh'], 'L2_gnn_b_ih': _L2_gnn_in['b_ih'], 'L2_gnn_b_hh': _L2_gnn_in['b_hh'], 'L3_gnn_bases': _L3_gnn_in['bases'], 'L3_gnn_coefficients': _L3_gnn_in['coefficients'], 'L3_gnn_self_loop': _L3_gnn_in['self_loop']}

def reference(x, src, dst, edge_attr_4, edge_type_16, edge_weight, L0_gnn_msg_W1, L0_gnn_msg_b1, L0_gnn_msg_W2, L0_gnn_msg_b2, L0_gnn_upd_W1, L0_gnn_upd_b1, L0_gnn_upd_W2, L0_gnn_upd_b2, L0_gnn_att_W1, L0_gnn_att_b1, L0_gnn_att_W2, L0_gnn_att_b2, L0_gnn_glb_W, L0_gnn_glb_b, L1_gnn_W1, L1_gnn_W2, L1_gnn_w_ih, L1_gnn_w_hh, L1_gnn_b_ih, L1_gnn_b_hh, L2_gnn_W_edge, L2_gnn_b_edge, L2_gnn_W_ih, L2_gnn_W_hh, L2_gnn_b_ih, L2_gnn_b_hh, L3_gnn_bases, L3_gnn_coefficients, L3_gnn_self_loop):
    import jax
    import jax.numpy as jnp

    def _L0_gnn_ref(x, edge_index, msg_W1, msg_b1, msg_W2, msg_b2, upd_W1, upd_b1, upd_W2, upd_b2, att_W1, att_b1, att_W2, att_b2, glb_W, glb_b):
        import jax, jax.numpy as jnp
        import numpy as np
        D = 128
        STEPS = 2
        N = 3125
        E = 31250

        def _mlp2(h, W1, b1, W2, b2):
            return jax.nn.relu(h @ W1 + b1) @ W2 + b2
        num_nodes = x.shape[0]
        src, dst = (edge_index[0], edge_index[1])
        global_repr = jax.nn.relu(jnp.mean(x, axis=0, keepdims=True) @ glb_W + glb_b)
        h = x
        for _ in range(STEPS):
            edge_feat = jnp.concatenate([h[src], h[dst]], axis=-1)
            messages = _mlp2(edge_feat, msg_W1, msg_b1, msg_W2, msg_b2)
            att = jax.nn.sigmoid(_mlp2(edge_feat, att_W1, att_b1, att_W2, att_b2))
            weighted = messages * att
            aggregated = jax.ops.segment_sum(weighted, dst, num_segments=num_nodes)
            combined = jnp.concatenate([h, aggregated], axis=-1)
            new_h = _mlp2(combined, upd_W1, upd_b1, upd_W2, upd_b2)
            h = new_h + h + global_repr
        return h

    def _L1_gnn_ref(feat, w, src, dst, W1, W2, w_ih, w_hh, b_ih, b_hh):
        import jax, jax.numpy as jnp
        import numpy as np
        N = 6250
        E = 40000
        D = 128

        def _weighted_mean_agg(ft, w, src, dst, n_nodes):
            m = ft[src] * w[:, None]
            msum = jax.ops.segment_sum(m, dst, num_segments=n_nodes)
            wsum = jax.ops.segment_sum(w, dst, num_segments=n_nodes)
            safe = jnp.where(wsum > 0, wsum, 1.0)
            return jnp.where((wsum > 0)[:, None], msum / safe[:, None], 0.0)
        n = feat.shape[0]
        neigh1 = _weighted_mean_agg(feat, w, src, dst, n)
        neigh2 = _weighted_mean_agg(feat, w, dst, src, n)
        hn = jnp.concatenate([neigh1 @ W1.T, neigh2 @ W2.T], axis=1)
        gi = hn @ w_ih.T + b_ih
        gh = feat @ w_hh.T + b_hh
        i_r, i_z, i_n = jnp.split(gi, 3, axis=1)
        h_r, h_z, h_n = jnp.split(gh, 3, axis=1)
        r = jax.nn.sigmoid(i_r + h_r)
        z = jax.nn.sigmoid(i_z + h_z)
        nn_ = jnp.tanh(i_n + r * h_n)
        return nn_ + z * (feat - nn_)

    def _L2_gnn_ref(node_feat, edge_index, edge_feat, W_edge, b_edge, W_ih, W_hh, b_ih, b_hh):
        import jax, jax.numpy as jnp
        import numpy as np
        N_NODES = 6250
        N_EDGES = 100000
        HIDDEN = 128
        N_ETYPES = 4
        N_STEPS = 4

        def _gru_cell(x, h, W_ih, W_hh, b_ih, b_hh):
            gi = x @ W_ih.T + b_ih
            gh = h @ W_hh.T + b_hh
            ir, iz, inn = jnp.split(gi, 3, axis=1)
            hr, hz, hn = jnp.split(gh, 3, axis=1)
            r = jax.nn.sigmoid(ir + hr)
            z = jax.nn.sigmoid(iz + hz)
            n = jnp.tanh(inn + r * hn)
            return (1.0 - z) * n + z * h
        etypes = jnp.argmax(edge_feat, axis=1)
        src, dst = (edge_index[0], edge_index[1])
        N = node_feat.shape[0]
        h = node_feat
        for _ in range(N_STEPS):
            trans = jnp.einsum('nd,tod->tno', h, W_edge) + b_edge[:, None, :]
            msg = trans[etypes, src]
            a = jax.ops.segment_sum(msg, dst, num_segments=N)
            h = _gru_cell(a, h, W_ih, W_hh, b_ih, b_hh)
        return h

    def _L3_gnn_ref(x, edge_index, edge_type, bases, coefficients, self_loop):
        import jax, jax.numpy as jnp
        import numpy as np
        NUM_NODES = 3125
        IN_DIM = 128
        OUT_DIM = 128
        NUM_RELATIONS = 16
        NUM_BASES = 8
        NUM_EDGES = 37500
        num_nodes = x.shape[0]
        W = jnp.einsum('rb,bio->rio', coefficients, bases)
        src, dst = (edge_index[0], edge_index[1])
        deg = jax.ops.segment_sum(jnp.ones_like(dst, dtype=x.dtype), dst, num_segments=num_nodes)
        deg_inv = 1.0 / jnp.maximum(deg, 1.0)
        xW = jnp.einsum('ni,rio->rno', x, W)
        msg = xW[edge_type, src] * deg_inv[dst][:, None]
        agg = jax.ops.segment_sum(msg, dst, num_segments=num_nodes)
        return agg + x @ self_loop
    edge_index = jnp.stack([src, dst])
    h = jnp.maximum(_layernorm(x, axis=-1), 0.0)
    x = x + _L0_gnn_ref(h, edge_index, L0_gnn_msg_W1, L0_gnn_msg_b1, L0_gnn_msg_W2, L0_gnn_msg_b2, L0_gnn_upd_W1, L0_gnn_upd_b1, L0_gnn_upd_W2, L0_gnn_upd_b2, L0_gnn_att_W1, L0_gnn_att_b1, L0_gnn_att_W2, L0_gnn_att_b2, L0_gnn_glb_W, L0_gnn_glb_b)
    h = jnp.maximum(_layernorm(x, axis=-1), 0.0)
    x = x + _L1_gnn_ref(h, edge_weight, src, dst, L1_gnn_W1, L1_gnn_W2, L1_gnn_w_ih, L1_gnn_w_hh, L1_gnn_b_ih, L1_gnn_b_hh)
    h = jnp.maximum(_layernorm(x, axis=-1), 0.0)
    x = x + _L2_gnn_ref(h, edge_index, edge_attr_4, L2_gnn_W_edge, L2_gnn_b_edge, L2_gnn_W_ih, L2_gnn_W_hh, L2_gnn_b_ih, L2_gnn_b_hh)
    h = jnp.maximum(_layernorm(x, axis=-1), 0.0)
    x = x + _L3_gnn_ref(h, edge_index, edge_type_16, L3_gnn_bases, L3_gnn_coefficients, L3_gnn_self_loop)
    return x

_drawn_inputs = setup_inputs


def setup_inputs(seed=0):
    import zlib

    import numpy as np

    out = dict(_drawn_inputs(seed))
    spreads = {'L0_gnn_msg_b1': (0.0, 0.1),
     'L0_gnn_msg_b2': (0.0, 0.1),
     'L0_gnn_upd_b1': (0.0, 0.1),
     'L0_gnn_upd_b2': (0.0, 0.1),
     'L0_gnn_att_b1': (0.0, 2.0),
     'L0_gnn_glb_b': (0.0, 0.1)}
    factors = {'edge_weight': 64.0,
     'L0_gnn_att_W1': 2.754,
     'L1_gnn_b_ih': 3.411,
     'L1_gnn_b_hh': 7.666,
     'L2_gnn_b_ih': 4.756,
     'L2_gnn_b_hh': 4.957}
    for name, (base, spread) in spreads.items():
        noise = np.random.default_rng([zlib.crc32(name.encode()), seed]).standard_normal(out[name].shape)
        drawn = base * np.exp(spread * noise) if base else spread * noise
        out[name] = jnp.asarray(drawn.astype(out[name].dtype))
    for name, factor in factors.items():
        out[name] = (out[name] * factor).astype(out[name].dtype)
    return out
```

```python
import numpy as np
import concourse.bass as bass
from concourse import mybir
from concourse.alu_op_type import AluOpType as ALU
from contextlib import ExitStack

F32, I32, BF16 = mybir.dt.float32, mybir.dt.int32, mybir.dt.bfloat16
ACT = mybir.ActivationFunctionType
AX = mybir.AxisListType

P = 128
N = 3125
E = 100000
D = 128
NW = -(-N // P)
NP = NW * P
TAIL = N - (NW - 1) * P
EP = 125
EC = E // EP
QUAD = 4
NQ = 4
BODY = QUAD * NQ
NT = -(-((E + NW * (P - 1)) // P) // BODY) * BODY
NI = NT // BODY
NTP = NT + BODY
T4, T16 = 4, 16
BANK = 512
NB = -(-NP // BANK)
COL = NP
D_LOC, D_W, D_SRC, D_T4, D_T16, D_WORDS = 0, 1, 2, 3, 4, 8
S_LOC, S_W, S_DST, S_WORDS = 0, 1, 2, 4
SC = 16


class Count:

    def __init__(self, eng, sem, start=0):
        self.eng, self.sem, self.n = eng, sem, start

    def step(self, ins):
        self.n = self.n + 1
        ins.then_inc(self.sem, 1)
        self.eng.wait_ge(self.sem, self.n)


class Program:
    def __init__(self, nc, ctx):
        self.nc, self.ctx = nc, ctx
        self.sems, self.used = {}, {}

    def sb(self, name, shape, dt=F32, ctx=None):
        self.used[name] = self.used.get(name, 0) + 1
        unique = name if self.used[name] == 1 else f"{name}_{self.used[name]}"
        return (ctx or self.ctx).enter_context(self.nc.sbuf_tensor(unique, shape, dt))

    def sem(self, name):
        if name not in self.sems:
            self.sems[name] = self.ctx.enter_context(self.nc.semaphore(name))
        return self.sems[name]

    def end_phase(self):
        numbers = [s.num for s in self.sems.values()]
        every = range(min(numbers), max(numbers) + 1)
        self.nc.gpsimd.dma_reset(every)
        self.nc.all_engine_barrier()
        self.nc.sync.sem_clear(every)
        self.nc.all_engine_barrier()


def constants(k):
    nc = k.nc
    k.ident = k.sb("ident", [P, P])
    k.before = k.sb("before", [P, P])
    k.upto = k.sb("upto", [P, P])
    k.ones = k.sb("ones", [P, BANK])
    k.zeros = k.sb("zeros", [P, BANK])
    k.head = k.sb("head", [P, P])
    k.lane = k.sb("lane", [P, 1])
    k.tile_no = k.sb("tile_no", [P, NT])
    k.ps = k.ctx.enter_context(nc.psum_tensor("ps", [P, 8, BANK], F32))
    s_set, s_sel = k.sem("s_set"), k.sem("s_sel")
    with nc.Block() as block:
        @block.gpsimd
        def _(eng):
            eng.memset(k.ident[:, :], 0.0).then_inc(s_set, 1)
            eng.memset(k.before[:, :], 1.0).then_inc(s_set, 1)
            eng.memset(k.upto[:, :], 1.0).then_inc(s_set, 1)
            eng.memset(k.head[:, :], 1.0).then_inc(s_set, 1)
            eng.memset(k.ones[:, :], 1.0).then_inc(s_set, 1)
            eng.memset(k.zeros[:, :], 0.0).then_inc(s_set, 1)
            eng.iota(k.tile_no[:, :], [[1, NT]], 0, 0, allow_small_or_imprecise_dtypes=True).then_inc(s_set, 1)
            eng.iota(k.lane[:, :], [[0, 1]], 0, 1, allow_small_or_imprecise_dtypes=True).then_inc(s_set, 1)
            eng.wait_ge(s_set, 8)
            eng.affine_select(out=k.ident[:, :], in_=k.ident[:, :], compare_op=ALU.not_equal, fill=1.0,
                              base=0, pattern=[[-1, P]], channel_multiplier=1).then_inc(s_sel, 1)
            eng.affine_select(out=k.before[:, :], in_=k.before[:, :], compare_op=ALU.is_ge, fill=0.0,
                              base=-1, pattern=[[1, P]], channel_multiplier=-1).then_inc(s_sel, 1)
            eng.affine_select(out=k.upto[:, :], in_=k.upto[:, :], compare_op=ALU.is_ge, fill=0.0,
                              base=0, pattern=[[1, P]], channel_multiplier=-1).then_inc(s_sel, 1)
            eng.affine_select(out=k.head[:, :], in_=k.head[:, :], compare_op=ALU.is_ge, fill=0.0,
                              base=NW - 2, pattern=[[0, P]], channel_multiplier=-1).then_inc(s_sel, 1)
            eng.wait_ge(s_sel, 4)
    k.end_phase()


def route(k, a):
    nc = k.nc
    k.by_dst = k.sb("by_dst", [P, NTP, D_WORDS])
    k.by_src = k.sb("by_src", [P, NTP, S_WORDS])
    k.off = {s: k.sb(f"off_{s}", [1, NTP], I32) for s in ("dst", "src")}
    loc_rows = nc.dram_tensor("loc_rows", [NB * P, P], BF16, kind="Internal").ap()
    k.loc_rows = loc_rows
    dram_d = nc.dram_tensor("routed_by_dst", [P * NT, D_WORDS], F32, kind="Internal").ap()
    dram_s = nc.dram_tensor("routed_by_src", [P * NT, S_WORDS], F32, kind="Internal").ap()
    own = ExitStack()
    with own:
        sb = lambda name, shape, dt=F32: k.sb(name, shape, dt, own)
        raw = {s: sb(f"raw_{s}", [EP, EC], I32) for s in ("src", "dst", "rel")}
        weight = sb("weight", [EP, EC])
        attr = sb("attr", [EP, EC, T4])
        top = sb("top", [EP, EC])
        differs = sb("differs", [EP, 3, EC])
        pay_d = sb("pay_d", [EP, EC, D_WORDS])
        pay_s = sb("pay_s", [EP, EC, S_WORDS])
        win_i = {s: sb(f"win_i_{s}", [EP, EC], I32) for s in ("src", "dst")}
        win = {s: sb(f"win_{s}", [EP, EC]) for s in ("src", "dst")}
        f_src, f_dst, f_rel = sb("f_src", [EP, EC]), sb("f_dst", [EP, EC]), sb("f_rel", [EP, EC])
        eq, cum, part = sb("eq", [EP, EC]), sb("cum", [EP, EC]), sb("part", [EP, EC])
        unit = sb("unit", [EP, EC])
        place = {s: sb(f"place_{s}", [EP, EC]) for s in ("src", "dst")}
        dest = {s: sb(f"dest_{s}", [EP, EC], I32) for s in ("src", "dst")}
        total = {s: sb(f"total_{s}", [P, P]) for s in ("src", "dst")}
        tiles_i = sb("tiles_i", [P, NW], I32)
        tiles = sb("tiles", [P, NW])
        ends = sb("ends", [P, NW])
        base = {s: sb(f"base_{s}", [P, NW]) for s in ("src", "dst")}
        col_i, col = sb("col_i", [P, 1], I32), sb("col", [P, 1])
        past = sb("past", [P, NT])
        stage_i = {s: sb(f"stage_i_{s}", [EP, 2, SC], I32) for s in ("src", "dst")}
        stage_d = sb("stage_d", [EP, 2, SC, D_WORDS])
        stage_s = sb("stage_s", [EP, 2, SC, S_WORDS])
        loc_t = sb("loc_t", [P, NB, P], BF16)
        loc_c = sb("loc_c", [P, NB * P])
        ps = k.ps
        PREF, CNT, CNT_T, END, WIN = 0, 1, 2, 3, 4

        s_load, s_pad, s_dve = k.sem("s_load"), k.sem("s_pad"), k.sem("s_dve")
        s_tot, s_sums, s_col, s_end, s_past, s_win = (k.sem(x) for x in ("s_tot", "s_sums", "s_col", "s_end", "s_past", "s_win"))
        s_tbl, s_prefill = k.sem("s_tbl"), k.sem("s_prefill")
        with nc.Block() as block:
            @block.sync
            def _(eng):
                for dst, src in ((raw["src"], a["src"]), (raw["dst"], a["dst"]), (raw["rel"], a["edge_type_16"]),
                                 (weight, a["edge_weight"])):
                    eng.dma_start(dst[:, :], src.rearrange("(p c) -> p c", p=EP)).then_inc(s_load, 16)
                eng.dma_start(attr[:, :, :], a["edge_attr_4"].rearrange("(p c) t -> p c t", p=EP)).then_inc(s_load, 16)
                eng.wait_ge(s_pad, 6)
                eng.dma_start(dram_d.rearrange("(p t) c -> p t c", p=P), k.by_dst[:, 0:NT, :]).then_inc(s_prefill, 16)
                eng.dma_start(dram_s.rearrange("(p t) c -> p t c", p=P), k.by_src[:, 0:NT, :]).then_inc(s_prefill, 16)
                eng.wait_ge(s_prefill, 32)

            @block.gpsimd
            def _(eng):
                for t in (k.by_dst, k.by_src):
                    eng.memset(t[:, :, 0:1], -1.0).then_inc(s_pad, 1)
                    eng.memset(t[:, :, 1:t.shape[2]], 0.0).then_inc(s_pad, 1)
                for s in ("src", "dst"):
                    eng.memset(total[s][:, :], 0.0).then_inc(s_pad, 1)

            @block.vector
            def _(eng):
                c = Count(eng, s_dve)
                eng.wait_ge(s_load, 80)
                eng.wait_ge(s_pad, 6)
                c.step(eng.memset(unit[:, :], 1.0))
                c.step(eng.memset(pay_d[:, :, :], 0.0))
                c.step(eng.memset(pay_s[:, :, :], 0.0))
                for s, pay in (("src", pay_s), ("dst", pay_d)):
                    c.step(eng.tensor_scalar(win_i[s][:, :], raw[s][:, :], 7, None, ALU.arith_shift_right))
                    c.step(eng.tensor_copy(win[s][:, :], win_i[s][:, :]))
                    c.step(eng.tensor_scalar(win_i[s][:, :], raw[s][:, :], P - 1, None, ALU.bitwise_and))
                    c.step(eng.tensor_copy(pay[:, :, 0], win_i[s][:, :]))
                c.step(eng.tensor_copy(f_src[:, :], raw["src"][:, :]))
                c.step(eng.tensor_copy(f_rel[:, :], raw["rel"][:, :]))
                c.step(eng.tensor_copy(pay_d[:, :, D_W], weight[:, :]))
                c.step(eng.tensor_copy(pay_s[:, :, S_W], weight[:, :]))
                c.step(eng.tensor_copy(pay_d[:, :, D_SRC].bitcast(I32), raw["src"][:, :]))
                c.step(eng.tensor_copy(pay_s[:, :, S_DST].bitcast(I32), raw["dst"][:, :]))
                c.step(eng.scalar_tensor_tensor(pay_d[:, :, D_T16].bitcast(I32), f_rel[:, :], float(NP), f_src[:, :],
                                                ALU.mult, ALU.add))
                c.step(eng.tensor_reduce(top[:, :], attr[:, :, :], AX.X, ALU.max))
                for j in range(3):
                    c.step(eng.tensor_tensor(differs[:, j, :], attr[:, :, j], top[:, :], ALU.not_equal))
                for j in (1, 0):
                    c.step(eng.scalar_tensor_tensor(differs[:, j, :], differs[:, j + 1, :], 1.0, differs[:, j, :],
                                                    ALU.add, ALU.mult))
                c.step(eng.scalar_tensor_tensor(pay_d[:, :, D_T4].bitcast(I32), differs[:, 0, :], float(NP), f_src[:, :],
                                                ALU.mult, ALU.add))
                for s in ("dst", "src"):
                    c.step(eng.memset(place[s][:, :], -1.0))
                    start = c.n
                    with eng.Fori(0, NW) as w:
                        c.n = w * 5 + start
                        c.step(eng.tensor_scalar(eq[:, :], win[s][:, :], k.tile_no[0:EP, bass.ds(w, 1)], None, ALU.is_equal))
                        c.step(eng.tensor_tensor_scan(cum[:, :], unit[:, :], eq[:, :], 0.0, ALU.mult, ALU.add))
                        c.step(eng.tensor_copy(total[s][0:EP, bass.ds(w, 1)], cum[:, EC - 1:EC]))
                        c.step(eng.tensor_tensor(part[:, :], cum[:, :], eq[:, :], ALU.mult))
                        c.step(eng.tensor_tensor(place[s][:, :], place[s][:, :], part[:, :], ALU.add))
                    c.n = start + 5 * NW
                    eng.sem_inc(s_tot, 1)
                for n, s in enumerate(("dst", "src")):
                    eng.wait_ge(s_sums, n + 1)
                    c.step(eng.tensor_scalar(tiles_i[:, :], ps[:, CNT, 0:NW], float(P - 1), None, ALU.add))
                    c.step(eng.tensor_scalar(tiles_i[:, :], tiles_i[:, :], 7, None, ALU.arith_shift_right))
                    c.step(eng.tensor_copy(tiles[:, :], tiles_i[:, :]))
                    c.step(eng.tensor_tensor_scan(ends[:, :], k.ones[:, 0:NW], tiles[:, :], 0.0, ALU.mult, ALU.add))
                    c.step(eng.tensor_tensor(ends[:, :], ends[:, :], tiles[:, :], ALU.subtract))
                    c.step(eng.scalar_tensor_tensor(base[s][:, :], ends[:, :], float(P), ps[:, PREF, 0:NW], ALU.mult, ALU.add))
                    c.step(eng.tensor_scalar(col_i[:, :], ps[:, CNT_T, 0:1], float(P - 1), None, ALU.add))
                    c.step(eng.tensor_scalar(col_i[:, :], col_i[:, :], 7, None, ALU.arith_shift_right))
                    c.step(eng.tensor_copy(col[:, :], col_i[:, :]))
                    eng.sem_inc(s_col, 1)
                    eng.wait_ge(s_end, n + 1)
                    c.step(eng.tensor_copy(col[:, :], ps[:, END, 0:1]))
                    c.step(eng.tensor_scalar(past[:, :], k.tile_no[:, :], col[:, 0:1], None, ALU.is_ge))
                    eng.sem_inc(s_past, 1)
                    eng.wait_ge(s_win, n + 1)
                    c.step(eng.memset(k.off[s][0:1, :], 0))
                    for h in range(2):
                        c.step(eng.tensor_scalar(k.off[s][0:1, h * NT // 2:(h + 1) * NT // 2], ps[0:1, WIN + h, 0:NT // 2],
                                                 float(P), None, ALU.mult))
                    eng.sem_inc(s_tbl, 1)
                    start = c.n
                    with eng.Fori(0, NW) as w:
                        c.n = w * 2 + start
                        c.step(eng.tensor_scalar(eq[:, :], win[s][:, :], k.tile_no[0:EP, bass.ds(w, 1)],
                                                 base[s][0:EP, bass.ds(w, 1)], ALU.is_equal, ALU.mult))
                        c.step(eng.tensor_tensor(place[s][:, :], place[s][:, :], eq[:, :], ALU.add))
                    c.n = start + 2 * NW
                    c.step(eng.tensor_copy(dest[s][:, :], place[s][:, :]))
                    c.step(eng.tensor_scalar(win_i[s][:, :], dest[s][:, :], 7, None, ALU.arith_shift_right))
                    c.step(eng.tensor_scalar(dest[s][:, :], dest[s][:, :], P - 1, None, ALU.bitwise_and))
                    c.step(eng.tensor_copy(eq[:, :], win_i[s][:, :]))
                    c.step(eng.tensor_copy(cum[:, :], dest[s][:, :]))
                    c.step(eng.scalar_tensor_tensor(dest[s][:, :], cum[:, :], float(NT), eq[:, :], ALU.mult, ALU.add))

            @block.tensor
            def _(eng):
                for n, s in enumerate(("dst", "src")):
                    eng.wait_ge(s_tot, n + 1)
                    if n:
                        eng.wait_ge(s_tbl, n)
                    eng.matmul(ps[:, PREF, 0:NW], k.before[:, :], total[s][:, 0:NW], start=True, stop=True)
                    eng.matmul(ps[:, CNT, 0:NW], k.ones[:, 0:P], total[s][:, 0:NW], start=True, stop=True)
                    eng.matmul(ps[:, CNT_T, 0:1], total[s][:, :], k.ones[:, 0:1], start=True, stop=True).then_inc(s_sums, 1)
                    eng.wait_ge(s_col, n + 1)
                    eng.matmul(ps[:, END, 0:1], k.upto[:, :], col[:, 0:1], start=True, stop=True).then_inc(s_end, 1)
                    eng.wait_ge(s_past, n + 1)
                    for h in range(2):
                        last = eng.matmul(ps[:, WIN + h, 0:NT // 2], k.head[:, :], past[:, h * NT // 2:(h + 1) * NT // 2],
                                          start=True, stop=True)
                    last.then_inc(s_win, 1)
        k.end_phase()

        s_staged, s_go = k.sem("s_staged"), k.sem("s_go")
        s_sc = {(s, h): k.sem(f"s_sc_{s}_{h}") for s in ("dst", "src") for h in range(2)}
        NCH = EC // (2 * SC)
        with nc.Block() as block:
            @block.vector
            def _(eng):
                def stage(chunk, h):
                    at = chunk * SC
                    for s in ("dst", "src"):
                        eng.tensor_copy(stage_i[s][:, h, :], dest[s][:, bass.ds(at, SC)]).then_inc(s_staged, 1)
                    eng.tensor_copy(stage_d[:, h, :, :], pay_d[:, bass.ds(at, SC), :]).then_inc(s_staged, 1)
                    eng.tensor_copy(stage_s[:, h, :, :], pay_s[:, bass.ds(at, SC), :]).then_inc(s_staged, 1)
                for h in range(2):
                    stage(h, h)
                with eng.Fori(1, NCH) as i:
                    for h in range(2):
                        for s in ("dst", "src"):
                            eng.wait_ge(s_sc[s, h], i * (16 * SC))
                        stage(i * 2 + h, h)

            @block.gpsimd
            def _(eng):
                with eng.Fori(0, NCH) as i:
                    for h in range(2):
                        eng.wait_ge(s_staged, i * 8 + 4 * (h + 1))
                        eng.sem_inc(s_go, 1)
                        for j in range(SC):
                            eng.indirect_dma_start(dram_d, bass.IndirectOffsetOnAxis(stage_i["dst"][:, h, j:j + 1], 0),
                                                   stage_d[:, h, j, :], None).then_inc(s_sc["dst", h], 16)
                            eng.indirect_dma_start(dram_s, bass.IndirectOffsetOnAxis(stage_i["src"][:, h, j:j + 1], 0),
                                                   stage_s[:, h, j, :], None).then_inc(s_sc["src", h], 16)
                for s in ("dst", "src"):
                    for h in range(2):
                        eng.wait_ge(s_sc[s, h], NCH * 16 * SC)
        k.end_phase()

        s_list, s_cmp, s_tr, s_ev, s_row = (k.sem(x) for x in ("s_list", "s_cmp", "s_tr", "s_ev", "s_row"))
        with nc.Block() as block:
            @block.sync
            def _(eng):
                eng.dma_start(k.by_dst[:, 0:NT, :], dram_d.rearrange("(p t) c -> p t c", p=P)).then_inc(s_list, 16)
                eng.dma_start(k.by_src[:, 0:NT, :], dram_s.rearrange("(p t) c -> p t c", p=P)).then_inc(s_list, 16)
                eng.wait_ge(s_ev, NB)
                eng.dma_start(loc_rows.rearrange("(b p) e -> p b e", p=P), loc_t[:, :, :]).then_inc(s_row, 16)
                eng.wait_ge(s_row, 16)
                eng.wait_ge(s_list, 32)

            @block.vector
            def _(eng):
                c = Count(eng, s_dve)
                c.step(eng.memset(loc_c[:, :], -1.0))
                eng.wait_ge(s_list, 32)
                eng.tensor_copy(loc_c[:, 0:NT], k.by_dst[:, 0:NT, D_LOC]).then_inc(s_cmp, 1)
                for b in range(NB):
                    eng.wait_ge(s_tr, b + 1)
                    eng.tensor_copy(loc_t[:, b, :], ps[:, b, 0:P]).then_inc(s_ev, 1)

            @block.tensor
            def _(eng):
                eng.wait_ge(s_cmp, 1)
                for b in range(NB):
                    eng.transpose(ps[:, b, 0:P], loc_c[:, b * P:(b + 1) * P], k.ident[:, :]).then_inc(s_tr, 1)
        k.end_phase()


def banks():
    for b in range(NB):
        n = min(BANK, NP - b * BANK)
        yield b, b * BANK, n, b * BANK // P, n // P


def load_all(k, pairs, name):
    s = k.sem("s_load")
    with k.nc.Block() as block:
        @block.sync
        def _(eng):
            for dst, src in pairs:
                eng.dma_start(dst, src).then_inc(s, 16)
            eng.wait_ge(s, 16 * len(pairs))
    k.end_phase()


def load_x(k, x):
    k.x, k.h, k.hT = k.sb("x", [P, NW, D]), k.sb("h", [P, NW, D]), k.sb("hT", [P, NP])
    s_set, s_load = k.sem("s_set"), k.sem("s_load")
    with k.nc.Block() as block:
        @block.vector
        def _(eng):
            eng.memset(k.x[:, NW - 1, :], 0.0).then_inc(s_set, 1)

        @block.sync
        def _(eng):
            eng.dma_start(k.x[:, 0:NW - 1, :], x[0:(NW - 1) * P, :].rearrange("(w p) d -> p w d", p=P)).then_inc(s_load, 16)
            eng.wait_ge(s_set, 1)
            eng.dma_start(k.x[0:TAIL, NW - 1, :], x[(NW - 1) * P:N, :]).then_inc(s_load, 16)
            eng.wait_ge(s_load, 32)
    k.end_phase()


def normalise(k):
    nc = k.nc
    own = ExitStack()
    with own:
        sq = k.sb("sq", [P, NW, D], F32, own)
        stat = k.sb("stat", [P, NW], F32, own)
        s_dve, s_var, s_std, s_h, s_tr, s_ev = (k.sem(x) for x in ("s_dve", "s_var", "s_std", "s_h", "s_tr", "s_ev"))
        wide = lambda t: t[:, :].unsqueeze(2).to_broadcast([P, NW, D])
        with nc.Block() as block:
            @block.vector
            def _(eng):
                c = Count(eng, s_dve)
                c.step(eng.tensor_reduce(stat[:, :], k.x[:, :, :], AX.X, ALU.add))
                c.step(eng.tensor_scalar(stat[:, :], stat[:, :], 1.0 / D, None, ALU.mult))
                c.step(eng.tensor_tensor(k.h[:, :, :], k.x[:, :, :], wide(stat), ALU.subtract))
                c.step(eng.tensor_tensor(sq[:, :, :], k.h[:, :, :], k.h[:, :, :], ALU.mult))
                c.step(eng.tensor_reduce(stat[:, :], sq[:, :, :], AX.X, ALU.add))
                eng.tensor_scalar(stat[:, :], stat[:, :], 1.0 / D, 1e-5, ALU.mult, ALU.add).then_inc(s_var, 1)
                eng.wait_ge(s_std, 1)
                c.step(eng.reciprocal(stat[:, :], stat[:, :]))
                for b, _, _, w0, wn in banks():
                    part = k.h[:, w0:w0 + wn, :]
                    c.step(eng.tensor_tensor(part, part, stat[:, w0:w0 + wn].unsqueeze(2).to_broadcast([P, wn, D]), ALU.mult))
                    eng.tensor_scalar(part, part, 0.0, None, ALU.max).then_inc(s_h, 1)

            @block.scalar
            def _(eng):
                eng.wait_ge(s_var, 1)
                eng.activation(stat[:, :], stat[:, :], ACT.Sqrt).then_inc(s_std, 1)
                evacuate(k, eng, s_tr, s_ev, k.hT)

            @block.tensor
            def _(eng):
                turn(k, eng, k.h, s_h, s_tr)
        k.end_phase()


def turn(k, eng, rows, s_ready, s_done, s_free=None):
    for b, _, n, w0, wn in banks():
        eng.wait_ge(s_ready, b + 1)
        if s_free:
            eng.wait_ge(s_free, b + 1)
        for j in range(wn):
            last = eng.transpose(k.ps[:, b, j * P:(j + 1) * P], rows[:, w0 + j, :], k.ident[:, :])
        last.then_inc(s_done, 1)


def evacuate(k, eng, s_full, s_done, cols):
    for b, c0, n, _, _ in banks():
        eng.wait_ge(s_full, b + 1)
        eng.activation(cols[:, c0:c0 + n], k.ps[:, b, 0:n], ACT.Copy).then_inc(s_done, 1)


def table(k, own, weights, width, dram_rows, bias=None, keep=None, shared=None):
    nc = k.nc
    out_n = shared or width
    nb = -(-width // BANK)
    G = 5 if nb == 1 else 1
    st = k.sb("rows", [P, 2, G, out_n], F32, own)
    s_mm, s_row, s_keep = (k.sem(x) for x in ("s_mm", "s_row", "s_keep"))
    s_st = [k.sem(f"s_st{j}") for j in range(2)]
    half = 8 // nb
    cut = out_n if nb == 1 else BANK

    parts = len(dram_rows(0, G, st[:, 0, :, :]))

    with nc.Block() as block:
        @block.tensor
        def _(eng):
            for w in range(NW):
                if w >= half:
                    eng.wait_ge(s_row, (w - half + 1) * nb)
                    if keep is not None:
                        eng.wait_ge(s_keep, w - half + 1)
                for j in range(nb):
                    eng.matmul(k.ps[:, (w % half) * nb + j, :], k.hT[:, w * P:(w + 1) * P],
                               weights[:, j * BANK:(j + 1) * BANK], start=True, stop=True).then_inc(s_mm, 1)

        def rows(eng, w, j):
            g = w // G
            eng.wait_ge(s_mm, w * nb + j + 1)
            if g >= 2:
                eng.wait_ge(s_st[g % 2], 16 * parts * (g // 2))
            dst = st[:, g % 2, w % G, j * BANK:j * BANK + cut]
            src = k.ps[:, (w % half) * nb + j, 0:cut]
            return dst, src

        @block.scalar
        def _(eng):
            if bias is not None and keep is None:
                return
            for w in range(NW):
                for j in range(nb):
                    dst, src = rows(eng, w, j)
                    eng.activation(dst, src, ACT.Copy).then_inc(s_row, 1)

        @block.vector
        def _(eng):
            if keep is not None:
                for w in range(NW):
                    eng.wait_ge(s_row, w + 1)
                    eng.tensor_tensor(keep[:, w, :], k.ps[:, w % 8, shared:width], bias[:, :], ALU.add).then_inc(s_keep, 1)
            elif bias is not None:
                for w in range(NW):
                    for j in range(nb):
                        dst, src = rows(eng, w, j)
                        eng.tensor_tensor(dst, src, bias[:, j * BANK:(j + 1) * BANK], ALU.add).then_inc(s_row, 1)

        @block.sync
        def _(eng):
            for g in range(NW // G):
                eng.wait_ge(s_row, (g + 1) * G * nb)
                for dst, src in dram_rows(g * G, G, st[:, g % 2, :, :]):
                    eng.dma_start(dst, src).then_inc(s_st[g % 2], 16)
            for j in range(2):
                eng.wait_ge(s_st[j], 16 * parts * len(range(j, NW // G, 2)))
    k.end_phase()


def edge_pass(k, own, rows, words, loc, idx, off, weight=None, column=None, flipped=False):
    nc = k.nc
    ring = k.sb("ring", [P, NQ * QUAD, D], F32, own)
    mark = k.sb("mark", [P, NQ, QUAD, P], F32, own)
    stage = k.sb("stage", [P, NQ * QUAD], I32, own)
    s_full = [k.sem(f"s_full{q}") for q in range(NQ)]
    s_staged, s_mark, s_done, s_go = (k.sem(x) for x in ("s_staged", "s_mark", "s_done", "s_go"))
    index = lambda t0, n: words[:, bass.ds(t0, n), idx].bitcast(I32)

    with nc.Block() as block:
        @block.scalar
        def _(eng):
            for q in range(NQ):
                eng.activation(stage[:, q * QUAD:(q + 1) * QUAD], index(q * QUAD, QUAD), ACT.Copy).then_inc(s_staged, 1)
            with eng.Fori(0, NI) as i:
                for q in range(NQ):
                    eng.wait_ge(s_full[q], i * (16 * QUAD) + 16 * QUAD)
                    eng.activation(stage[:, q * QUAD:(q + 1) * QUAD], index(i * BODY + BODY + q * QUAD, QUAD),
                                   ACT.Copy).then_inc(s_staged, 1)

        @block.gpsimd
        def _(eng):
            with eng.Fori(0, NI) as i:
                for q in range(NQ):
                    eng.wait_ge(s_staged, i * NQ + q + 1)
                    eng.wait_ge(s_done, i * NQ + q + 1)
                    eng.sem_inc(s_go, 1)
                    for t in range(q * QUAD, (q + 1) * QUAD):
                        eng.indirect_dma_start(ring[:, t, :], None, rows,
                                               bass.IndirectOffsetOnAxis(stage[:, t:t + 1], 0)).then_inc(s_full[q], 16)
            for q in range(NQ):
                eng.wait_ge(s_full[q], NI * 16 * QUAD)

        @block.vector
        def _(eng):
            with eng.Fori(0, NI) as i:
                for q in range(NQ):
                    at = i * BODY + q * QUAD
                    eng.wait_ge(s_done, i * NQ + q + 1)
                    eng.tensor_tensor(mark[:, q, :, :], k.tile_no[:, 0:P].unsqueeze(1).to_broadcast([P, QUAD, P]),
                                      words[:, bass.ds(at, QUAD), loc].unsqueeze(2).to_broadcast([P, QUAD, P]),
                                      ALU.is_equal).then_inc(s_mark, 1)
                    if weight is not None:
                        eng.wait_ge(s_full[q], i * (16 * QUAD) + 16 * QUAD)
                        part = ring[:, q * QUAD:(q + 1) * QUAD, :]
                        eng.tensor_tensor(part, part, words[:, bass.ds(at, QUAD), weight].unsqueeze(2)
                                          .to_broadcast([P, QUAD, D]), ALU.mult).then_inc(s_mark, 1)

        @block.tensor
        def _(eng):
            per = 1 if weight is None else 2
            eng.sem_inc(s_done, NQ)
            open_banks(k, eng)
            with eng.Fori(0, NI) as i:
                for q in range(NQ):
                    at = i * BODY + q * QUAD
                    cols = [eng.value_load(off[0:1, bass.ds(at + j, 1)], min_val=0, max_val=(NW - 1) * P)
                            for j in range(QUAD)]
                    eng.wait_ge(s_mark, i * (NQ * per) + (q + 1) * per)
                    if weight is None:
                        eng.wait_ge(s_full[q], i * (16 * QUAD) + 16 * QUAD)
                    for j in range(QUAD):
                        row, marks = ring[:, q * QUAD + j, :], mark[:, q, j, :]
                        left, right = (row, marks) if flipped else (marks, row)
                        last = eng.matmul(k.psf[:, bass.ds(cols[j], P)], left, right, start=False, stop=False,
                                          skip_group_check=True)
                        if column == "weight":
                            last = eng.matmul(k.psf[:, bass.ds(cols[j] // P + COL, 1)], marks,
                                              words[:, bass.ds(at + j, 1), weight], start=False, stop=False,
                                              skip_group_check=True)
                        if column == "one":
                            last = eng.matmul(k.psf[:, bass.ds(cols[j] // P + COL, 1)], marks, k.ones[:, 0:1],
                                              start=False, stop=False, skip_group_check=True)
                    last.then_inc(s_done, 1)
            close_banks(k, eng)
    k.end_phase()


def open_banks(k, eng):
    for b in range(NB):
        eng.matmul(k.ps[:, b, :], k.zeros[:, 0:P], k.zeros[:, :], start=True, stop=False, skip_group_check=True)


def close_banks(k, eng):
    for b in range(NB):
        eng.matmul(k.ps[:, b, :], k.zeros[:, 0:P], k.zeros[:, :], start=False, stop=True, skip_group_check=True)


def attention_pass(k, own, rows, here, w_att, b_att):
    nc = k.nc
    W2 = 2 * D
    ring = k.sb("ring", [P, NQ * QUAD, W2], F32, own)
    mark = k.sb("mark", [P, NQ, QUAD, P], F32, own)
    spread = k.sb("spread", [P, NQ, QUAD * P], F32, own)
    locs = k.sb("locs", [P, NQ, QUAD * P], BF16, own)
    stage = k.sb("stage", [P, NQ * QUAD], I32, own)
    dot = k.sb("dot", [P, NQ * QUAD], F32, own)
    att = k.sb("att", [P, NQ * QUAD], F32, own)
    s_full = [k.sem(f"s_full{q}") for q in range(NQ)]
    s_locs = [k.sem(f"s_locs{q}") for q in range(NQ)]
    s_staged, s_mark, s_done, s_go = (k.sem(x) for x in ("s_staged", "s_mark", "s_done", "s_go"))
    s_spread, s_exp, s_add, s_dot, s_att, s_msg = (k.sem(x) for x in ("s_spread", "s_exp", "s_add", "s_dot", "s_att", "s_msg"))
    words = k.by_dst
    index = lambda t0, n: words[:, bass.ds(t0, n), D_SRC].bitcast(I32)
    hid = k.ps[:, 7, :].rearrange("p (s c) -> p s c", s=2)

    with nc.Block() as block:
        @block.sync
        def _(eng):
            def fetch(t0, q):
                eng.dma_start(locs[:, q, :], k.loc_rows[bass.ds(t0, QUAD), :].rearrange("t e -> (t e)").partition_broadcast(P)).then_inc(s_locs[q], 16)
            for q in range(NQ):
                fetch(q * QUAD, q)
            with eng.Fori(0, NI) as i:
                for q in range(NQ):
                    eng.wait_ge(s_spread, i * NQ + q + 1)
                    fetch(i * BODY + BODY + q * QUAD, q)
            for q in range(NQ):
                eng.wait_ge(s_locs[q], 16 * (NI + 1))

        @block.gpsimd
        def _(eng):
            with eng.Fori(0, NI) as i:
                for q in range(NQ):
                    eng.wait_ge(s_staged, i * NQ + q + 1)
                    eng.wait_ge(s_done, i * NQ + q + 1)
                    eng.sem_inc(s_go, 1)
                    for t in range(q * QUAD, (q + 1) * QUAD):
                        eng.indirect_dma_start(ring[:, t, :], None, rows,
                                               bass.IndirectOffsetOnAxis(stage[:, t:t + 1], 0)).then_inc(s_full[q], 16)
            for q in range(NQ):
                eng.wait_ge(s_full[q], NI * 16 * QUAD)

        @block.vector
        def _(eng):
            def spread_quad(i, q, g):
                eng.wait_ge(s_locs[q], i * 16 + 16)
                eng.wait_ge(s_exp, g * 2 + 2)
                eng.tensor_scalar(spread[:, q, :], locs[:, q, :], k.lane[:, 0:1], None, ALU.is_equal).then_inc(s_spread, 1)

            def body(i, last):
                for q in range(NQ):
                    g = i * NQ + q
                    at = i * BODY + q * QUAD
                    if q + 1 < NQ:
                        spread_quad(i, q + 1, g + 1)
                    elif not last:
                        spread_quad(i + 1, 0, g + 1)
                    eng.wait_ge(s_done, g + 1)
                    eng.tensor_tensor(mark[:, q, :, :], k.tile_no[:, 0:P].unsqueeze(1).to_broadcast([P, QUAD, P]),
                                      words[:, bass.ds(at, QUAD), D_LOC].unsqueeze(2).to_broadcast([P, QUAD, P]),
                                      ALU.is_equal).then_inc(s_mark, 1)
                    eng.wait_ge(s_full[q], i * (16 * QUAD) + 16 * QUAD)
                    for pair in range(2):
                        t = q * QUAD + pair * 2
                        eng.wait_ge(s_exp, g * 2 + (pair + 1 + NQ * 2))
                        eng.tensor_tensor(ring[:, t:t + 2, :], ring[:, t:t + 2, :], hid, ALU.add).then_inc(s_add, 1)
                        if pair == 0:
                            continue
                        for j in range(QUAD):
                            eng.wait_ge(s_add, g * 2 + (j // 2 + 2))
                            t = q * QUAD + j
                            eng.scalar_tensor_tensor(ring[:, t, D:W2], ring[:, t, D:W2], 0.0, w_att[:, :], ALU.max, ALU.mult,
                                                     accum_out=dot[:, t:t + 1]).then_inc(s_dot, 1)
            eng.sem_inc(s_add, 1)
            spread_quad(0, 0, 0)
            with eng.Fori(0, NI - 1) as i:
                body(i, False)
            body(NI - 1, True)

        @block.scalar
        def _(eng):
            for q in range(NQ):
                eng.activation(stage[:, q * QUAD:(q + 1) * QUAD], index(q * QUAD, QUAD), ACT.Copy).then_inc(s_staged, 1)
            with eng.Fori(0, NI) as i:
                for q in range(NQ):
                    g = i * NQ + q
                    eng.wait_ge(s_full[q], i * (16 * QUAD) + 16 * QUAD)
                    eng.activation(stage[:, q * QUAD:(q + 1) * QUAD], index(i * BODY + BODY + q * QUAD, QUAD),
                                   ACT.Copy).then_inc(s_staged, 1)
                    eng.wait_ge(s_dot, g * QUAD + QUAD)
                    eng.activation(att[:, q * QUAD:(q + 1) * QUAD], dot[:, q * QUAD:(q + 1) * QUAD], ACT.Sigmoid,
                                   bias=b_att[:, 0:1]).then_inc(s_att, 1)
                    eng.wait_ge(s_att, g + 1)
                    for j in range(QUAD):
                        t = q * QUAD + j
                        eng.activation(ring[:, t, 0:D], ring[:, t, 0:D], ACT.Relu, scale=att[:, t:t + 1]).then_inc(s_msg, 1)

        @block.tensor
        def _(eng):
            def offsets(at):
                return [eng.value_load(k.off["dst"][0:1, bass.ds(at + j, 1)], min_val=0, max_val=(NW - 1) * P)
                        for j in range(QUAD)]

            def expand(g, q, pair, cols):
                eng.wait_ge(s_add, g * 2 + (pair + 1))
                for j in range(2):
                    t = pair * 2 + j
                    last = eng.matmul(hid[:, j, :], spread[:, q, t * P:(t + 1) * P], here[:, bass.ds(cols[t] * 2, W2)],
                                      start=True, stop=True)
                last.then_inc(s_exp, 1)

            def body(i, last):
                col = offsets(i * BODY)
                for q in range(NQ):
                    g = i * NQ + q
                    more = q + 1 < NQ or not last
                    if more:
                        nxt = offsets(i * BODY + (q + 1) * QUAD)
                        eng.wait_ge(s_spread, g + 2)
                    eng.wait_ge(s_mark, g + 1)
                    for j in range(QUAD):
                        if more and j % 2 == 0:
                            expand(g + 1, (q + 1) % NQ, j // 2, nxt)
                        eng.wait_ge(s_msg, g * QUAD + (j + 1))
                        eng.matmul(k.psf[:, bass.ds(col[j], D)], mark[:, q, j, :], ring[:, q * QUAD + j, 0:D],
                                   start=False, stop=False, skip_group_check=True)
                        done = eng.matmul(k.psf[:, bass.ds(col[j] // P + COL, 1)], mark[:, q, j, :],
                                          att[:, q * QUAD + j:q * QUAD + j + 1], start=False, stop=False,
                                          skip_group_check=True)
                    done.then_inc(s_done, 1)
                    if more:
                        col = nxt

            eng.sem_inc(s_done, NQ)
            eng.sem_inc(s_exp, NQ * 2)
            open_banks(k, eng)
            first = offsets(0)
            eng.wait_ge(s_spread, 1)
            for pair in range(2):
                expand(0, 0, pair, first)
            with eng.Fori(0, NI - 1) as i:
                body(i, False)
            body(NI - 1, True)
            close_banks(k, eng)
    k.end_phase()


def accumulated(k, rows, column=None):
    s_a, s_v = k.sem("s_a"), k.sem("s_v")
    flat = rows.rearrange("p w d -> p (w d)") if len(rows.shape) == 3 else rows
    with k.nc.Block() as block:
        @block.scalar
        def _(eng):
            for b, c0, n, _, _ in banks():
                if b % 2:
                    eng.activation(flat[:, c0:c0 + n], k.ps[:, b, 0:n], ACT.Copy).then_inc(s_a, 1)

        @block.vector
        def _(eng):
            for b, c0, n, _, _ in banks():
                if not b % 2:
                    eng.tensor_copy(flat[:, c0:c0 + n], k.ps[:, b, 0:n]).then_inc(s_v, 1)
            if column is not None:
                eng.tensor_copy(column, k.psf[:, COL:COL + NW]).then_inc(s_v, 1)
    k.end_phase()


def layer0(k, a):
    nc = k.nc
    own = ExitStack()
    with own:
        sb = lambda name, shape, dt=F32: k.sb(name, shape, dt, own)
        w1 = sb("w1", [P, 4 * D])
        bias1 = sb("bias1", [P, 2 * D])
        w2, b2 = sb("w2", [P, D]), sb("b2", [P, D])
        u1, u2 = sb("u1", [P, 2, D]), sb("u2", [P, D])
        c1, c2 = sb("c1", [P, 1]), sb("c2", [P, D])
        wg, bg = sb("wg", [P, D]), sb("bg", [P, D])
        w_att, b_att = sb("w_att", [P, D]), sb("b_att", [P, 1])
        glob = sb("glob", [P, D])
        here = sb("here", [P, NW, 2 * D])
        mean_wide = sb("mean_wide", [P, P])
        att_sum = sb("att_sum", [P, NW])
        mean = sb("mean", [P, 1])
        rows = nc.dram_tensor("rows0", [NP, 2 * D], F32, kind="Internal").ap()
        L = "L0_gnn_"
        wide = lambda v: a[L + v].partition_broadcast(P)
        load_all(k, [(w1[:, 0:D], a[L + "msg_W1"][0:D, :]), (w1[:, D:2 * D], a[L + "att_W1"][0:D, :]),
                     (w1[:, 2 * D:3 * D], a[L + "msg_W1"][D:2 * D, :]), (w1[:, 3 * D:4 * D], a[L + "att_W1"][D:2 * D, :]),
                     (bias1[:, 0:D], wide("msg_b1")), (bias1[:, D:2 * D], wide("att_b1")),
                     (w2[:, :], a[L + "msg_W2"]), (b2[:, :], wide("msg_b2")),
                     (u1[:, :, :], a[L + "upd_W1"].rearrange("(s p) d -> p s d", p=P)), (u2[:, :], a[L + "upd_W2"]),
                     (c1[:, :], a[L + "upd_b1"]), (c2[:, :], wide("upd_b2")),
                     (wg[:, :], a[L + "glb_W"]), (bg[:, :], wide("glb_b")),
                     (w_att[:, :], a[L + "att_W2"].partition_broadcast(P)), (b_att[:, :], wide("att_b2"))], "w0")
        s_dve, s_mean, s_g = k.sem("s_dve"), k.sem("s_mean"), k.sem("s_g")
        with nc.Block() as block:
            @block.vector
            def _(eng):
                c = Count(eng, s_dve)
                c.step(eng.tensor_reduce(mean[:, :], k.hT[:, 0:N], AX.X, ALU.add))
                c.step(eng.tensor_scalar(mean[:, :], mean[:, :], 1.0 / N, None, ALU.mult))
                eng.tensor_scalar(mean_wide[:, :], k.ones[:, 0:P], mean[:, 0:1], None, ALU.mult).then_inc(s_mean, 1)
                eng.wait_ge(s_g, 1)
                c.step(eng.tensor_tensor(glob[:, :], k.ps[:, 0, 0:D], bg[:, :], ALU.add))
                c.step(eng.scalar_tensor_tensor(glob[:, :], glob[:, :], 0.0, c2[:, :], ALU.max, ALU.add))

            @block.tensor
            def _(eng):
                eng.wait_ge(s_mean, 1)
                eng.matmul(k.ps[:, 0, 0:D], mean_wide[:, :], wg[:, :], start=True, stop=True).then_inc(s_g, 1)
        k.end_phase()

        with nc.Fori(0, 2) as _step:
            with ExitStack() as inner:
                table(k, inner, w1, 4 * D, lambda w0, n, st: [(rows[w0 * P:(w0 + n) * P, :].rearrange("(w p) d -> p w d", p=P), st)],
                      bias=bias1, keep=here, shared=2 * D)
            with ExitStack() as inner:
                attention_pass(k, inner, rows, here.rearrange("p w d -> p (w d)"), w_att, b_att)
            with ExitStack() as inner:
                agg = k.sb("agg", [P, NW, D], F32, inner)
                aggT, zT = k.sb("aggT", [P, NP], F32, inner), k.sb("zT", [P, NP], F32, inner)
                accumulated(k, agg, att_sum[:, :])
                update0(k, agg, aggT, zT, att_sum, w2, b2, u1, c1, u2, glob)
        s_x = k.sem("s_x")
        with nc.Block() as block:
            @block.vector
            def _(eng):
                eng.tensor_tensor(k.x[:, :, :], k.x[:, :, :], k.h[:, :, :], ALU.add).then_inc(s_x, 1)
        k.end_phase()


def update0(k, agg, aggT, zT, att_sum, w2, b2, u1, c1, u2, glob):
    S = {n: (k.sem(f"s_pe_{n}"), k.sem(f"s_ev_{n}")) for n in "ABCDEF"}
    s_dve = k.sem("s_dve")
    with k.nc.Block() as block:
        @block.tensor
        def _(eng):
            def stage(name, before, product):
                for b, c0, n, w0, wn in banks():
                    if before:
                        eng.wait_ge(S[before][1], b + 1)
                    last = product(b, c0, n, w0, wn)
                    last.then_inc(S[name][0], 1)

            def turned(b, c0, n, w0, wn, rows):
                for j in range(wn):
                    last = eng.transpose(k.ps[:, b, j * P:(j + 1) * P], rows[:, w0 + j, :], k.ident[:, :])
                return last

            def times(b, c0, n, w0, wn, cols, w):
                for j in range(wn):
                    last = eng.matmul(k.ps[:, b, j * P:(j + 1) * P], cols[:, (w0 + j) * P:(w0 + j + 1) * P], w[:, :],
                                      start=True, stop=True)
                return last

            def hidden(b, c0, n, w0, wn):
                eng.matmul(k.ps[:, b, 0:n], u1[:, 0, :], k.hT[:, c0:c0 + n], start=True, stop=False)
                return eng.matmul(k.ps[:, b, 0:n], u1[:, 1, :], aggT[:, c0:c0 + n], start=False, stop=True)

            stage("A", None, lambda *s: turned(*s, agg))
            stage("B", "A", lambda *s: times(*s, aggT, w2))
            stage("C", "B", lambda *s: turned(*s, agg))
            stage("D", "C", hidden)
            stage("E", "D", lambda *s: times(*s, zT, u2))
            stage("F", "E", lambda *s: turned(*s, k.h))

        @block.scalar
        def _(eng):
            for name, out in (("A", aggT), ("C", aggT), ("D", zT), ("F", k.hT)):
                for b, c0, n, _, _ in banks():
                    eng.wait_ge(S[name][0], b + 1)
                    if name == "D":
                        eng.activation(out[:, c0:c0 + n], k.ps[:, b, 0:n], ACT.Relu, bias=c1[:, 0:1]).then_inc(S[name][1], 1)
                    else:
                        eng.activation(out[:, c0:c0 + n], k.ps[:, b, 0:n], ACT.Copy).then_inc(S[name][1], 1)

        @block.vector
        def _(eng):
            c = Count(eng, s_dve)
            for b, c0, n, w0, wn in banks():
                eng.wait_ge(S["B"][0], b + 1)
                for j in range(wn):
                    ins = eng.scalar_tensor_tensor(agg[:, w0 + j, :], b2[:, :], att_sum[:, w0 + j:w0 + j + 1],
                                                   k.ps[:, b, j * P:(j + 1) * P], ALU.mult, ALU.add)
                ins.then_inc(S["B"][1], 1)
            for b, c0, n, w0, wn in banks():
                eng.wait_ge(S["E"][0], b + 1)
                part = k.h[:, w0:w0 + wn, :]
                c.step(eng.tensor_tensor(part, part, glob[:, :].unsqueeze(1).to_broadcast([P, wn, D]), ALU.add))
                eng.tensor_tensor(part, part, k.ps[:, b, 0:n].rearrange("p (w d) -> p w d", d=D), ALU.add)\
                   .then_inc(S["E"][1], 1)
    k.end_phase()


def gru(k, inputs, w_h, b_r, b_z, b_i, b_n, buf):
    r, z, t, n_ = buf
    s_pe, s_rz, s_pre, s_n, s_dve, s_new = (k.sem(x) for x in ("s_pe", "s_rz", "s_pre", "s_n", "s_dve", "s_new"))
    R, Z, I, H = range(4)
    with k.nc.Block() as block:
        @block.tensor
        def _(eng):
            for b, c0, n, _, _ in banks():
                if b >= 2:
                    eng.wait_ge(s_pre, b - 1)
                bank = lambda g: k.ps[:, (b % 2) * 4 + g, 0:n]
                for g in (R, Z, I):
                    for m, (cols, w) in enumerate(inputs):
                        eng.matmul(bank(g), w[:, g * D:(g + 1) * D], cols[:, c0:c0 + n], start=m == 0,
                                   stop=g == I and m + 1 == len(inputs))
                    if g != I:
                        eng.matmul(bank(g), w_h[:, g * D:(g + 1) * D], k.hT[:, c0:c0 + n], start=False, stop=True)
                eng.matmul(bank(H), w_h[:, 2 * D:3 * D], k.hT[:, c0:c0 + n], start=True, stop=True).then_inc(s_pe, 1)

        @block.scalar
        def _(eng):
            def gates(b, n):
                eng.wait_ge(s_pe, b + 1)
                if b >= 2:
                    eng.wait_ge(s_new, b - 1)
                eng.activation(r[:, b % 2, 0:n], k.ps[:, (b % 2) * 4 + R, 0:n], ACT.Sigmoid, bias=b_r).then_inc(s_rz, 1)
                eng.activation(z[:, b % 2, 0:n], k.ps[:, (b % 2) * 4 + Z, 0:n], ACT.Sigmoid, bias=b_z).then_inc(s_rz, 1)
            every = list(banks())
            gates(0, every[0][2])
            for b, c0, n, _, _ in every:
                if b + 1 < NB:
                    gates(b + 1, every[b + 1][2])
                eng.wait_ge(s_pre, b + 1)
                eng.activation(n_[:, b % 2, 0:n], t[:, b % 2, 0:n], ACT.Tanh, bias=b_i).then_inc(s_n, 1)

        @block.vector
        def _(eng):
            c = Count(eng, s_dve)
            for b, c0, n, _, _ in banks():
                p = b % 2
                eng.wait_ge(s_rz, 2 * b + 2)
                c.step(eng.scalar_tensor_tensor(t[:, p, 0:n], k.ps[:, p * 4 + H, 0:n], b_n, r[:, p, 0:n], ALU.add, ALU.mult))
                eng.tensor_tensor(t[:, p, 0:n], t[:, p, 0:n], k.ps[:, p * 4 + I, 0:n], ALU.add).then_inc(s_pre, 1)
                eng.wait_ge(s_n, b + 1)
                h = k.hT[:, c0:c0 + n]
                c.step(eng.tensor_tensor(h, h, n_[:, p, 0:n], ALU.subtract))
                c.step(eng.tensor_tensor(h, h, z[:, p, 0:n], ALU.mult))
                eng.tensor_tensor(h, h, n_[:, p, 0:n], ALU.add).then_inc(s_new, 1)
    k.end_phase()


def gru_weights(k, own, a, name, wide_in):
    ih = k.sb("w_ih", [P, wide_in, 3 * D], F32, own)
    hh = k.sb("w_hh", [P, 3 * D], F32, own)
    bi, bh = k.sb("b_ih", [P, 3], F32, own), k.sb("b_hh", [P, 3], F32, own)
    both = k.sb("b_both", [P, 3], F32, own)
    load_all(k, [(ih[:, :, :], a[name + "ih"].rearrange("(s p) g -> p s g", p=P)), (hh[:, :], a[name + "hh"]),
                 (bi[:, :], a[name + "b_ih"]), (bh[:, :], a[name + "b_hh"])], "gru")
    s = k.sem("s_dve")
    with k.nc.Block() as block:
        @block.vector
        def _(eng):
            eng.tensor_tensor(both[:, :], bi[:, :], bh[:, :], ALU.add).then_inc(s, 1)
    k.end_phase()
    return ih, hh, both, bi, bh


def add_turned(k):
    s_tr, s_x = k.sem("s_tr"), k.sem("s_x")
    with k.nc.Block() as block:
        @block.tensor
        def _(eng):
            for b, c0, n, w0, wn in banks():
                for j in range(wn):
                    last = eng.transpose(k.ps[:, b, j * P:(j + 1) * P], k.hT[:, c0 + j * P:c0 + (j + 1) * P], k.ident[:, :])
                last.then_inc(s_tr, 1)

        @block.vector
        def _(eng):
            for b, c0, n, w0, wn in banks():
                eng.wait_ge(s_tr, b + 1)
                part = k.x[:, w0:w0 + wn, :]
                eng.tensor_tensor(part, part, k.ps[:, b, 0:n].rearrange("p (w d) -> p w d", d=D), ALU.add).then_inc(s_x, 1)
    k.end_phase()


def store_h(k, rows):
    s = k.sem("s_load")
    with k.nc.Block() as block:
        @block.sync
        def _(eng):
            eng.dma_start(rows.rearrange("(w p) d -> p w d", p=P), k.h[:, :, :]).then_inc(s, 16)
            eng.wait_ge(s, 16)
    k.end_phase()


def layer1(k, a):
    nc = k.nc
    own = ExitStack()
    with own:
        sb = lambda name, shape, dt=F32: k.sb(name, shape, dt, own)
        wn = [sb("wn1", [P, D]), sb("wn2", [P, D])]
        mean = sb("mean", [P, NW, D])
        meanT = sb("meanT", [P, NP])
        mixT = [sb("mix1", [P, NP]), sb("mix2", [P, NP])]
        total, some, safe = sb("total", [P, NW]), sb("some", [P, NW]), sb("safe", [P, NW])
        buf = [sb(f"gru{j}", [P, 2, BANK]) for j in range(4)]
        rows = nc.dram_tensor("rows1", [NP, D], F32, kind="Internal").ap()
        store_h(k, rows)
        load_all(k, [(wn[0][:, :], a["L1_W1T"]), (wn[1][:, :], a["L1_W2T"])], "w1")
        ih, hh, both, bi, bh = gru_weights(k, own, a, "L1_", 2)
        for m, (words, idx, off) in enumerate(((k.by_dst, D_SRC, k.off["dst"]), (k.by_src, S_DST, k.off["src"]))):
            inner = ExitStack()
            with inner:
                edge_pass(k, inner, rows, words, D_LOC, idx, off, weight=D_W, column="weight")
                accumulated(k, mean, total[:, :])
            s_dve, s_ready = k.sem("s_dve"), k.sem("s_ready")
            S = {n: (k.sem(f"s_pe_{n}"), k.sem(f"s_ev_{n}")) for n in "AB"}
            with nc.Block() as block:
                @block.vector
                def _(eng):
                    c = Count(eng, s_dve)
                    c.step(eng.tensor_scalar(some[:, :], total[:, :], 0.0, None, ALU.is_gt))
                    c.step(eng.tensor_scalar(safe[:, :], some[:, :], -1.0, 1.0, ALU.mult, ALU.add))
                    c.step(eng.tensor_tensor(total[:, :], total[:, :], some[:, :], ALU.mult))
                    c.step(eng.tensor_tensor(safe[:, :], safe[:, :], total[:, :], ALU.add))
                    c.step(eng.reciprocal(safe[:, :], safe[:, :]))
                    c.step(eng.tensor_tensor(safe[:, :], safe[:, :], some[:, :], ALU.mult))
                    for b, _, _, w0, n in banks():
                        part = mean[:, w0:w0 + n, :]
                        eng.tensor_tensor(part, part, safe[:, w0:w0 + n].unsqueeze(2).to_broadcast([P, n, D]), ALU.mult)\
                           .then_inc(s_ready, 1)

                @block.tensor
                def _(eng):
                    turn(k, eng, mean, s_ready, S["A"][0])
                    for b, c0, n, _, _ in banks():
                        eng.wait_ge(S["A"][1], b + 1)
                        eng.matmul(k.ps[:, b, 0:n], wn[m][:, :], meanT[:, c0:c0 + n], start=True, stop=True)\
                           .then_inc(S["B"][0], 1)

                @block.scalar
                def _(eng):
                    evacuate(k, eng, *S["A"], meanT)
                    evacuate(k, eng, *S["B"], mixT[m])
            k.end_phase()
        gru(k, [(mixT[0], ih[:, 0, :]), (mixT[1], ih[:, 1, :])], hh, both[:, 0:1], both[:, 1:2], bi[:, 2:3], bh[:, 2:3], buf)
        add_turned(k)


def layer2(k, a):
    nc = k.nc
    own = ExitStack()
    with own:
        sb = lambda name, shape, dt=F32: k.sb(name, shape, dt, own)
        we, be = sb("we", [P, T4 * D]), sb("be", [P, T4 * D])
        sumT = sb("sumT", [P, NP])
        buf = [sb(f"gru{j}", [P, 2, BANK]) for j in range(4)]
        rows = nc.dram_tensor("rows2", [T4, NP, D], F32, kind="Internal").ap()
        load_all(k, [(we[:, :], a["L2_We"]), (be[:, :], a["L2_be"].partition_broadcast(P))], "w2")
        ih, hh, both, bi, bh = gru_weights(k, own, a, "L2_", 1)
        with nc.Fori(0, 4) as _step:
            with ExitStack() as inner:
                table(k, inner, we, T4 * D,
                      lambda w0, n, st: [(rows[t, w0 * P:(w0 + n) * P, :].rearrange("(w p) d -> p w d", p=P), st[:, :, t * D:(t + 1) * D])
                                         for t in range(T4)],
                      bias=be)
            with ExitStack() as inner:
                edge_pass(k, inner, rows.rearrange("t n d -> (t n) d"), k.by_dst, D_LOC, D_T4, k.off["dst"], flipped=True)
            accumulated(k, sumT)
            gru(k, [(sumT, ih[:, 0, :])], hh, both[:, 0:1], both[:, 1:2], bi[:, 2:3], bh[:, 2:3], buf)
        add_turned(k)


def layer3(k, a, out):
    nc = k.nc
    own = ExitStack()
    with own:
        sb = lambda name, shape, dt=F32: k.sb(name, shape, dt, own)
        coef = sb("coef", [P, T16, 8])
        bases = sb("bases", [P, 8, D])
        loop = sb("loop", [P, D])
        agg = sb("agg", [P, NW, D])
        deg = sb("deg", [P, NW])
        rows = nc.dram_tensor("rows3", [T16, NP, D], F32, kind="Internal").ap()
        load_all(k, [(coef[:, :, :].rearrange("p r b -> p (r b)"), a["L3_gnn_coefficients"].partition_broadcast(P)),
                     (bases[:, :, :], a["L3_bases"]), (loop[:, :], a["L3_gnn_self_loop"])], "w3")
        s_dve = k.sem("s_dve")
        early = ExitStack()
        with early:
            rel = k.sb("rel", [P, T16, D], F32, early)
            part = k.sb("part3", [P, T16, D], F32, early)
            with nc.Block() as block:
                @block.vector
                def _(eng):
                    c = Count(eng, s_dve)
                    for b in range(8):
                        out_ = rel if b == 0 else part
                        c.step(eng.tensor_tensor(out_[:, :, :], bases[:, b, :].unsqueeze(1).to_broadcast([P, T16, D]),
                                                 coef[:, :, b].unsqueeze(2).to_broadcast([P, T16, D]), ALU.mult))
                        if b:
                            c.step(eng.tensor_tensor(rel[:, :, :], rel[:, :, :], part[:, :, :], ALU.add))
            k.end_phase()
            table(k, early, rel.rearrange("p r d -> p (r d)"), T16 * D,
                  lambda w0, n, st: [(rows[:, w0 * P:(w0 + 1) * P, :].rearrange("r p d -> p r d"),
                                      st[:, 0, :].rearrange("p (r d) -> p r d", d=D))])
        late = ExitStack()
        with late:
            edge_pass(k, late, rows.rearrange("r n d -> (r n) d"), k.by_dst, D_LOC, D_T16, k.off["dst"], column="one")
            accumulated(k, agg, deg[:, :])
        s_mm, s_out, s_x = k.sem("s_mm"), k.sem("s_out"), k.sem("s_x")
        with nc.Block() as block:
            @block.tensor
            def _(eng):
                for b, c0, n, w0, wn in banks():
                    for j in range(wn):
                        last = eng.matmul(k.ps[:, b, j * P:(j + 1) * P], k.hT[:, c0 + j * P:c0 + (j + 1) * P], loop[:, :],
                                          start=True, stop=True)
                    last.then_inc(s_mm, 1)

            @block.vector
            def _(eng):
                c = Count(eng, s_dve)
                c.step(eng.tensor_scalar(deg[:, :], deg[:, :], 1.0, None, ALU.max))
                c.step(eng.reciprocal(deg[:, :], deg[:, :]))
                for b, c0, n, w0, wn in banks():
                    part, x = agg[:, w0:w0 + wn, :], k.x[:, w0:w0 + wn, :]
                    c.step(eng.tensor_tensor(part, part, deg[:, w0:w0 + wn].unsqueeze(2).to_broadcast([P, wn, D]), ALU.mult))
                    eng.wait_ge(s_mm, b + 1)
                    c.step(eng.tensor_tensor(part, part, k.ps[:, b, 0:n].rearrange("p (w d) -> p w d", d=D), ALU.add))
                    eng.tensor_tensor(x, x, part, ALU.add).then_inc(s_x, 1)

            @block.sync
            def _(eng):
                eng.wait_ge(s_x, NB)
                eng.dma_start(out[0:(NW - 1) * P, :].rearrange("(w p) d -> p w d", p=P), k.x[:, 0:NW - 1, :]).then_inc(s_out, 16)
                eng.dma_start(out[(NW - 1) * P:N, :], k.x[0:TAIL, NW - 1, :]).then_inc(s_out, 16)
                eng.wait_ge(s_out, 32)


def build(nc, a, out):
    with ExitStack() as ctx:
        k = Program(nc, ctx)
        constants(k)
        k.psf = k.ps[:, :, :].rearrange("p b c -> p (b c)")
        route(k, a)
        load_x(k, a["x"])
        normalise(k)
        layer0(k, a)
        normalise(k)
        layer1(k, a)
        normalise(k)
        layer2(k, a)
        normalise(k)
        layer3(k, a, out)


def kernel(**inputs):
    import concourse.bacc as bacc
    from concourse.bass_utils import run_bass_kernel_spmd as run
    nc = bacc.Bacc("TRN2", target_bir_lowering=False, num_devices=1)
    v = {n: np.asarray(x) for n, x in inputs.items()}
    laid = {n: v[n] for n in ("x", "src", "dst", "edge_attr_4", "edge_type_16", "edge_weight", "L3_gnn_self_loop")}
    laid.update({n: v[n] for n in v if n.startswith("L0_")})
    laid["L0_gnn_upd_b1"] = v["L0_gnn_upd_b1"].reshape(D, 1)
    laid["L0_gnn_att_W2"] = v["L0_gnn_att_W2"].reshape(D)
    laid["L1_W1T"], laid["L1_W2T"] = v["L1_gnn_W1"].T, v["L1_gnn_W2"].T
    laid["L2_We"] = v["L2_gnn_W_edge"].transpose(2, 0, 1).reshape(D, T4 * D)
    laid["L2_be"] = v["L2_gnn_b_edge"].reshape(T4 * D)
    for l, ih, hh in (("L1_", "L1_gnn_w_ih", "L1_gnn_w_hh"), ("L2_", "L2_gnn_W_ih", "L2_gnn_W_hh")):
        laid[l + "ih"], laid[l + "hh"] = v[ih].T, v[hh].T
        for b in ("b_ih", "b_hh"):
            laid[l + b] = v[l + "gnn_" + b].reshape(3, D).T
    laid["L3_bases"] = v["L3_gnn_bases"].transpose(1, 0, 2)
    laid["L3_gnn_coefficients"] = v["L3_gnn_coefficients"].reshape(-1)
    arrays, aps = {}, {}
    for n, x in laid.items():
        x = np.ascontiguousarray(x)
        arrays[n + "_dram"] = x
        aps[n] = nc.dram_tensor(n + "_dram", x.shape, mybir.dt.from_np(x.dtype), kind="ExternalInput").ap()
    out = nc.dram_tensor("out_dram", (N, D), F32, kind="ExternalOutput").ap()
    build(nc, aps, out)
    r = run(nc, [arrays], core_ids=[0])
    return r.results[0]["out_dram"]
```

```python
import numpy as np
import concourse.bass as bass
from concourse import mybir
from concourse.alu_op_type import AluOpType as ALU
from contextlib import ExitStack

F32, I32, BF16 = mybir.dt.float32, mybir.dt.int32, mybir.dt.bfloat16
ACT = mybir.ActivationFunctionType
AX = mybir.AxisListType

P = 128
N = 3125
E = 100000
D = 128
NW = -(-N // P)
NP = NW * P
TAIL = N - (NW - 1) * P
EP = 125
EC = E // EP
QUAD = 4
NQ = 4
NQ0 = 6
ROUND = 48
NT = -(-((E + NW * (P - 1)) // P) // ROUND) * ROUND
NTP = NT + QUAD * NQ0
T4, T16 = 4, 16
BANK = 512
NB = -(-NP // BANK)
COL = NP
D_LOC, D_W, D_SRC, D_T4, D_T16, D_WORDS = 0, 1, 2, 3, 4, 8
S_LOC, S_W, S_DST, S_WORDS = 0, 1, 2, 4
SC = 16
STARTS = 8


class Count:

    def __init__(self, eng, sem, start=0):
        self.eng, self.sem, self.n = eng, sem, start

    def step(self, ins):
        self.n = self.n + 1
        ins.then_inc(self.sem, 1)
        self.eng.wait_ge(self.sem, self.n)


class Program:
    def __init__(self, nc, ctx):
        self.nc, self.ctx = nc, ctx
        self.sems, self.used = {}, {}

    def sb(self, name, shape, dt=F32, ctx=None):
        self.used[name] = self.used.get(name, 0) + 1
        unique = name if self.used[name] == 1 else f"{name}_{self.used[name]}"
        return (ctx or self.ctx).enter_context(self.nc.sbuf_tensor(unique, shape, dt))

    def sem(self, name):
        if name not in self.sems:
            self.sems[name] = self.ctx.enter_context(self.nc.semaphore(name))
        return self.sems[name]

    def flag(self, eng):
        return eng.value_load(self.in_order[0:1, 0:1], min_val=0, max_val=1)

    def uid(self):
        self.used["uid"] = self.used.get("uid", 0) + 1
        return self.used["uid"]

    def end_phase(self):
        numbers = [s.num for s in self.sems.values()]
        every = range(min(numbers), max(numbers) + 1)
        self.nc.gpsimd.dma_reset(every)
        self.nc.all_engine_barrier()
        self.nc.sync.sem_clear(every)
        self.nc.all_engine_barrier()


def constants(k):
    nc = k.nc
    k.ident = k.sb("ident", [P, P])
    k.before = k.sb("before", [P, P])
    k.upto = k.sb("upto", [P, P])
    k.ones = k.sb("ones", [P, BANK])
    k.zeros = k.sb("zeros", [P, BANK])
    k.head = k.sb("head", [P, P])
    k.lane = k.sb("lane", [P, 1])
    k.tile_no = k.sb("tile_no", [P, NT])
    k.ps = k.ctx.enter_context(nc.psum_tensor("ps", [P, 8, BANK], F32))
    s_set, s_sel = k.sem("s_set"), k.sem("s_sel")
    with nc.Block() as block:
        @block.gpsimd
        def _(eng):
            eng.memset(k.ident[:, :], 0.0).then_inc(s_set, 1)
            eng.memset(k.before[:, :], 1.0).then_inc(s_set, 1)
            eng.memset(k.upto[:, :], 1.0).then_inc(s_set, 1)
            eng.memset(k.head[:, :], 1.0).then_inc(s_set, 1)
            eng.memset(k.ones[:, :], 1.0).then_inc(s_set, 1)
            eng.memset(k.zeros[:, :], 0.0).then_inc(s_set, 1)
            eng.iota(k.tile_no[:, :], [[1, NT]], 0, 0, allow_small_or_imprecise_dtypes=True).then_inc(s_set, 1)
            eng.iota(k.lane[:, :], [[0, 1]], 0, 1, allow_small_or_imprecise_dtypes=True).then_inc(s_set, 1)
            eng.wait_ge(s_set, 8)
            eng.affine_select(out=k.ident[:, :], in_=k.ident[:, :], compare_op=ALU.not_equal, fill=1.0,
                              base=0, pattern=[[-1, P]], channel_multiplier=1).then_inc(s_sel, 1)
            eng.affine_select(out=k.before[:, :], in_=k.before[:, :], compare_op=ALU.is_ge, fill=0.0,
                              base=-1, pattern=[[1, P]], channel_multiplier=-1).then_inc(s_sel, 1)
            eng.affine_select(out=k.upto[:, :], in_=k.upto[:, :], compare_op=ALU.is_ge, fill=0.0,
                              base=0, pattern=[[1, P]], channel_multiplier=-1).then_inc(s_sel, 1)
            eng.affine_select(out=k.head[:, :], in_=k.head[:, :], compare_op=ALU.is_ge, fill=0.0,
                              base=NW - 2, pattern=[[0, P]], channel_multiplier=-1).then_inc(s_sel, 1)
            eng.wait_ge(s_sel, 4)
    k.end_phase()


def route(k, a):
    nc = k.nc
    k.by_dst = k.sb("by_dst", [P, NTP, D_WORDS])
    k.by_src = k.sb("by_src", [P, NTP, S_WORDS])
    k.where = {s: k.sb(f"where_{s}", [1, NTP // QUAD, 2 * QUAD], I32) for s in ("dst", "src")}
    k.loc_rows = nc.dram_tensor("loc_rows", [NB * P, P], BF16, kind="Internal").ap()
    k.first_node = k.sb("first_node", [P, NT])
    k.in_order = k.sb("in_order", [1, 1], I32)
    words = {"dst": D_WORDS, "src": S_WORDS}
    routed = {"dst": k.by_dst, "src": k.by_src}
    dram = {s: nc.dram_tensor(f"routed_by_{s}", [P * NT, words[s]], F32, kind="Internal").ap() for s in words}
    own = ExitStack()
    with own:
        sb = lambda name, shape, dt=F32: k.sb(name, shape, dt, own)
        raw = {s: sb(f"raw_{s}", [EP, EC], I32) for s in ("src", "dst", "rel")}
        weight = sb("weight", [EP, EC])
        attr = sb("attr", [EP, EC, T4])
        top = sb("top", [EP, EC])
        differs = sb("differs", [EP, 3, EC])
        pay = {s: sb(f"pay_{s}", [EP, EC, words[s]]) for s in words}
        win_i = {s: sb(f"win_i_{s}", [EP, EC], I32) for s in words}
        win = {s: sb(f"win_{s}", [EP, EC]) for s in words}
        f_rel = sb("f_rel", [EP, EC])
        eq, cum, part = sb("eq", [EP, EC]), sb("cum", [EP, EC]), sb("part", [EP, EC])
        unit = sb("unit", [EP, EC])
        place = sb("place", [EP, EC])
        dest = {s: sb(f"dest_{s}", [EP, EC], I32) for s in words}
        total = {s: sb(f"total_{s}", [P, P]) for s in words}
        tiles_i = sb("tiles_i", [P, NW], I32)
        tiles = sb("tiles", [P, NW])
        ends = sb("ends", [P, NW])
        base = {s: sb(f"base_{s}", [P, NW]) for s in words}
        col_i, col = sb("col_i", [P, 1], I32), sb("col", [P, 1])
        past = sb("past", [P, NT])
        stage_i = {s: sb(f"stage_i_{s}", [EP, 2, SC], I32) for s in words}
        after = sb("after", [EP, EC], I32)
        falls = sb("falls", [P, 1])
        pads = sb("pads", [P, 1])
        pad_head, shift = sb("pad_head", [P, P]), sb("shift", [1, NT])
        start_of = sb("start_of", [1, NT], I32)
        tail = sb("tail", [P, D_WORDS])
        listed = nc.dram_tensor("listed", [E + P, D_WORDS], F32, kind="Internal").ap()
        stage_w = {s: sb(f"stage_{s}", [EP, 2, SC, words[s]]) for s in words}
        ps = k.ps
        PREF, CNT, CNT_T, END, WIN = 0, 1, 2, 3, 4
        NCH = EC // (2 * SC)

        names = ("s_load", "s_pad", "s_dve", "s_tot", "s_sums", "s_col", "s_end", "s_past", "s_win", "s_pay", "s_store")
        s_load, s_pad, s_dve, s_tot, s_sums, s_col, s_end, s_past, s_win, s_pay, s_store = (k.sem(x) for x in names)
        SHIFT = 6
        s_general = k.sem("s_general")
        s_dest, s_staged, s_go = ({s: k.sem(f"{x}_{s}") for s in words} for x in ("s_dest", "s_staged", "s_go"))
        s_sc = {(s, h): k.sem(f"s_sc_{s}_{h}") for s in words for h in range(2)}
        s_copied = k.sem("s_copied")

        def window_totals(eng, c, s):
            c.step(eng.tensor_scalar(win_i[s][:, :], raw[s][:, :], 7, None, ALU.arith_shift_right))
            c.step(eng.tensor_copy(win[s][:, :], win_i[s][:, :]))
            start = c.n
            with eng.Fori(0, NW) as w:
                c.n = w + start
                c.step(eng.tensor_scalar(eq[:, :], win[s][:, :], k.tile_no[0:EP, bass.ds(w, 1)], 0.0, ALU.is_equal,
                                         ALU.add, accum_out=total[s][0:EP, bass.ds(w, 1)]))
            c.n = start + NW

        def window_starts(eng, c, s):
            eng.sem_inc(s_tot, 1)
            eng.wait_ge(s_sums, 1)
            c.step(eng.tensor_scalar(tiles_i[:, :], ps[:, CNT, 0:NW], float(P - 1), None, ALU.add))
            c.step(eng.tensor_scalar(tiles_i[:, :], tiles_i[:, :], 7, None, ALU.arith_shift_right))
            c.step(eng.tensor_copy(tiles[:, :], tiles_i[:, :]))
            c.step(eng.tensor_tensor_scan(ends[:, :], k.ones[:, 0:NW], tiles[:, :], 0.0, ALU.mult, ALU.add))
            c.step(eng.tensor_tensor(ends[:, :], ends[:, :], tiles[:, :], ALU.subtract))
            c.step(eng.scalar_tensor_tensor(base[s][:, :], ends[:, :], float(P), ps[:, PREF, 0:NW], ALU.mult, ALU.add))
            c.step(eng.tensor_scalar(col_i[:, :], ps[:, CNT_T, 0:1], float(P - 1), None, ALU.add))
            c.step(eng.tensor_scalar(col_i[:, :], col_i[:, :], 7, None, ALU.arith_shift_right))
            c.step(eng.tensor_copy(col[:, :], col_i[:, :]))
            if s == "dst":
                c.step(eng.scalar_tensor_tensor(pads[:, :], col[:, :], float(P), ps[:, CNT_T, 0:1], ALU.mult, ALU.subtract))
                c.step(eng.tensor_scalar(pad_head[:, :], k.head[:, :], pads[:, 0:1], None, ALU.mult))
            eng.sem_inc(s_col, 1)
            eng.wait_ge(s_end, 1)
            c.step(eng.tensor_copy(col[:, :], ps[:, END, 0:1]))
            c.step(eng.tensor_scalar(past[:, :], k.tile_no[:, :], col[:, 0:1], None, ALU.is_ge))
            eng.sem_inc(s_past, 1)
            c.step(eng.memset(k.where[s][0:1, :, :], 0))
            eng.wait_ge(s_win, 1)
            for h in range(2):
                w = ps[0:1, WIN + h, 0:NT // 2].rearrange("p (g j) -> p g j", j=QUAD)
                to = k.where[s][0:1, h * NT // 2 // QUAD:(h + 1) * NT // 2 // QUAD, :]
                c.step(eng.tensor_scalar(to[:, :, 0:QUAD], w, float(P), None, ALU.mult))
                c.step(eng.tensor_scalar(to[:, :, QUAD:2 * QUAD], w, float(COL), None, ALU.add))
                if s == "dst":
                    c.step(eng.tensor_scalar(k.first_node[:, h * NT // 2:(h + 1) * NT // 2], ps[:, WIN + h, 0:NT // 2],
                                             float(P), None, ALU.mult))

        def count_on_pe(eng, s):
            eng.wait_ge(s_tot, 1)
            eng.matmul(ps[:, PREF, 0:NW], k.before[:, :], total[s][:, 0:NW], start=True, stop=True)
            if s == "dst":
                eng.matmul(ps[:, CNT, NW:NW + 1], k.ones[:, 0:P], falls[:, 0:1], start=True, stop=True)
            eng.matmul(ps[:, CNT, 0:NW], k.ones[:, 0:P], total[s][:, 0:NW], start=True, stop=True)
            eng.matmul(ps[:, CNT_T, 0:1], total[s][:, :], k.ones[:, 0:1], start=True, stop=True).then_inc(s_sums, 1)
            eng.wait_ge(s_col, 1)
            eng.matmul(ps[:, END, 0:1], k.upto[:, :], col[:, 0:1], start=True, stop=True).then_inc(s_end, 1)
            eng.wait_ge(s_past, 1)
            for to, of in ((WIN, k.head),) + (((SHIFT, pad_head),) if s == "dst" else ()):
                for h in range(2):
                    last = eng.matmul(ps[:, to + h, 0:NT // 2], of[:, :], past[:, h * NT // 2:(h + 1) * NT // 2],
                                      start=True, stop=True)
            last.then_inc(s_win, 1)

        def places(eng, c, s):
            c.step(eng.memset(place[:, :], -1.0))
            start = c.n
            with eng.Fori(0, NW) as w:
                c.n = w * 4 + start
                c.step(eng.tensor_scalar(eq[:, :], win[s][:, :], k.tile_no[0:EP, bass.ds(w, 1)], None, ALU.is_equal))
                c.step(eng.tensor_tensor_scan(cum[:, :], unit[:, :], eq[:, :], base[s][0:EP, bass.ds(w, 1)],
                                              ALU.mult, ALU.add))
                c.step(eng.tensor_tensor(part[:, :], cum[:, :], eq[:, :], ALU.mult))
                c.step(eng.tensor_tensor(place[:, :], place[:, :], part[:, :], ALU.add))
            c.n = start + 4 * NW
            c.step(eng.tensor_copy(dest[s][:, :], place[:, :]))
            c.step(eng.tensor_scalar(win_i[s][:, :], dest[s][:, :], 7, None, ALU.arith_shift_right))
            c.step(eng.tensor_scalar(dest[s][:, :], dest[s][:, :], P - 1, None, ALU.bitwise_and))
            c.step(eng.tensor_copy(eq[:, :], win_i[s][:, :]))
            c.step(eng.tensor_copy(cum[:, :], dest[s][:, :]))
            c.step(eng.scalar_tensor_tensor(dest[s][:, :], cum[:, :], float(NT), eq[:, :], ALU.mult, ALU.add))

        with nc.Block() as block:
            @block.sync
            def _(eng):
                eng.wait_ge(s_pad, 1)
                for dst, src in ((raw["dst"], a["dst"]), (raw["src"], a["src"]), (raw["rel"], a["edge_type_16"]),
                                 (weight, a["edge_weight"])):
                    eng.dma_start(dst[:, :], src.rearrange("(p c) -> p c", p=EP)).then_inc(s_load, 16)
                eng.dma_start(after[0:EP - 1, :], a["dst"][1:1 + (EP - 1) * EC].rearrange("(p c) -> p c", c=EC)).then_inc(s_load, 16)
                eng.dma_start(after[EP - 1:EP, 0:EC - 1], a["dst"][E - EC + 1:E].rearrange("(p c) -> p c", p=1)).then_inc(s_load, 16)
                eng.dma_start(attr[:, :, :], a["edge_attr_4"].rearrange("(p c) t -> p c t", p=EP)).then_inc(s_load, 16)
                eng.wait_ge(s_pad, 9)
                for s in words:
                    eng.dma_start(dram[s].rearrange("(p t) c -> p t c", p=P), routed[s][:, 0:NT, :]).then_inc(s_store, 16)
                eng.dma_start(listed[E:E + P, :], tail[:, :]).then_inc(s_store, 16)
                eng.wait_ge(s_pay, 1)
                eng.dma_start(listed[0:E, :].rearrange("(p c) w -> p c w", p=EP), pay["dst"][:, :, :]).then_inc(s_store, 16)
                eng.wait_ge(s_store, 64)

            @block.gpsimd
            def _(eng):
                eng.memset(after[:, :], N).then_inc(s_pad, 1)
                for t in (k.by_dst, k.by_src):
                    eng.memset(t[:, :, 0:1], -1.0).then_inc(s_pad, 1)
                    eng.memset(t[:, :, 1:t.shape[2]], 0.0).then_inc(s_pad, 1)
                for s in words:
                    eng.memset(total[s][:, :], 0.0).then_inc(s_pad, 1)
                eng.memset(tail[:, 0:1], -1.0).then_inc(s_pad, 1)
                eng.memset(tail[:, 1:D_WORDS], 0.0).then_inc(s_pad, 1)

            @block.vector
            def _(eng):
                c = Count(eng, s_dve)
                eng.wait_ge(s_load, 112)
                eng.wait_ge(s_pad, 9)
                window_totals(eng, c, "dst")
                c.step(eng.memset(falls[:, :], 0.0))
                c.step(eng.tensor_scalar(after[:, :], after[:, :], 7, None, ALU.arith_shift_right))
                c.step(eng.tensor_tensor(eq[:, :], after[:, :], win["dst"][:, :], ALU.is_lt))
                c.step(eng.tensor_reduce(falls[0:EP, :], eq[:, :], AX.X, ALU.add))
                c.step(eng.memset(unit[:, :], 1.0))
                c.step(eng.memset(pay["dst"][:, :, :], 0.0))
                c.step(eng.tensor_copy(pay["dst"][:, :, D_SRC], raw["src"][:, :]))
                c.step(eng.tensor_copy(pay["dst"][:, :, D_LOC], raw["dst"][:, :]))
                c.step(eng.tensor_copy(f_rel[:, :], raw["rel"][:, :]))
                c.step(eng.tensor_copy(pay["dst"][:, :, D_W], weight[:, :]))
                f_src = pay["dst"][:, :, D_SRC]
                c.step(eng.scalar_tensor_tensor(pay["dst"][:, :, D_T16], f_rel[:, :], float(NP), f_src, ALU.mult, ALU.add))
                c.step(eng.tensor_reduce(top[:, :], attr[:, :, :], AX.X, ALU.max))
                for j in range(3):
                    c.step(eng.tensor_tensor(differs[:, j, :], attr[:, :, j], top[:, :], ALU.not_equal))
                for j in (1, 0):
                    c.step(eng.scalar_tensor_tensor(differs[:, j, :], differs[:, j + 1, :], 1.0, differs[:, j, :],
                                                    ALU.add, ALU.mult))
                c.step(eng.scalar_tensor_tensor(pay["dst"][:, :, D_T4], differs[:, 0, :], float(NP), f_src, ALU.mult, ALU.add))
                eng.sem_inc(s_pay, 1)
                window_starts(eng, c, "dst")
                for h in range(2):
                    half = slice(h * NT // 2, (h + 1) * NT // 2)
                    c.step(eng.scalar_tensor_tensor(shift[0:1, half], k.tile_no[0:1, half], float(P),
                                                    ps[0:1, SHIFT + h, 0:NT // 2], ALU.mult, ALU.subtract))
                    c.step(eng.tensor_scalar(start_of[0:1, half], shift[0:1, half], float(E), None, ALU.min))
                c.step(eng.tensor_scalar(k.in_order[0:1, 0:1], ps[0:1, CNT, NW:NW + 1], 0.0, None, ALU.is_equal))

            @block.tensor
            def _(eng):
                count_on_pe(eng, "dst")
        k.end_phase()

        with nc.Block() as block:
            @block.sync
            def _(eng):
                ordered = k.flag(eng)
                with eng.If(ordered > 0):
                    regs = [eng.alloc_register(f"start_{j}") for j in range(STARTS)]
                    with eng.Fori(0, NT // STARTS) as i:
                        eng.load(regs, start_of[0:1, bass.ds(i * STARTS, STARTS)])
                        for j, r in enumerate(regs):
                            at = eng.snap(r, min_val=0, max_val=E)
                            eng.dma_start(k.by_dst[:, bass.ds(i * STARTS + j, 1), :].rearrange("p t c -> p (t c)"),
                                          listed[bass.ds(at, P), :]).then_inc(s_copied, 16)
                    eng.wait_ge(s_copied, 16 * NT)

            def scatter(eng, s):
                with eng.Fori(0, NCH) as i:
                    for h in range(2):
                        eng.wait_ge(s_staged[s], i * 4 + 2 * (h + 1))
                        eng.sem_inc(s_go[s], 1)
                        for j in range(SC):
                            eng.indirect_dma_start(dram[s], bass.IndirectOffsetOnAxis(stage_i[s][:, h, j:j + 1], 0),
                                                   stage_w[s][:, h, j, :], None).then_inc(s_sc[s, h], 16)
                for h in range(2):
                    eng.wait_ge(s_sc[s, h], NCH * 16 * SC)

            @block.gpsimd
            def _(eng):
                ordered = k.flag(eng)
                with eng.If(ordered < 1):
                    scatter(eng, "dst")
                scatter(eng, "src")

            def stage_all(eng, s):
                def stage(chunk, h):
                    at = chunk * SC
                    eng.activation(stage_i[s][:, h, :], dest[s][:, bass.ds(at, SC)], ACT.Copy).then_inc(s_staged[s], 1)
                    eng.activation(stage_w[s][:, h, :, :], pay[s][:, bass.ds(at, SC), :], ACT.Copy).then_inc(s_staged[s], 1)
                eng.wait_ge(s_dest[s], 1)
                for h in range(2):
                    stage(h, h)
                with eng.Fori(1, NCH) as i:
                    for h in range(2):
                        eng.wait_ge(s_sc[s, h], i * (16 * SC))
                        stage(i * 2 + h, h)

            @block.scalar
            def _(eng):
                ordered = k.flag(eng)
                with eng.If(ordered < 1):
                    stage_all(eng, "dst")
                stage_all(eng, "src")

            @block.vector
            def _(eng):
                ordered = k.flag(eng)
                with eng.If(ordered < 1):
                    places(eng, Count(eng, s_general), "dst")
                    eng.sem_inc(s_dest["dst"], 1)
                c = Count(eng, s_dve)
                c.step(eng.memset(pay["src"][:, :, :], 0.0))
                c.step(eng.tensor_copy(pay["src"][:, :, S_DST], raw["dst"][:, :]))
                c.step(eng.tensor_copy(pay["src"][:, :, S_W], weight[:, :]))
                window_totals(eng, c, "src")
                c.step(eng.tensor_scalar(win_i["src"][:, :], raw["src"][:, :], P - 1, None, ALU.bitwise_and))
                c.step(eng.tensor_copy(pay["src"][:, :, S_LOC], win_i["src"][:, :]))
                window_starts(eng, c, "src")
                places(eng, c, "src")
                eng.sem_inc(s_dest["src"], 1)

            @block.tensor
            def _(eng):
                count_on_pe(eng, "src")
        k.end_phase()

    own = ExitStack()
    with own:
        loc_t = k.sb("loc_t", [P, NB, P], BF16, own)
        loc_c = k.sb("loc_c", [P, NB * P], F32, own)
        names = ("s_list", "s_src", "s_here", "s_cmp", "s_tr", "s_ev", "s_row", "s_dve")
        s_list, s_src, s_here, s_cmp, s_tr, s_ev, s_row, s_dve = (k.sem(x) for x in names)
        with nc.Block() as block:
            @block.sync
            def _(eng):
                ordered = k.flag(eng)
                with eng.If(ordered < 1):
                    eng.dma_start(k.by_dst[:, 0:NT, :], dram["dst"].rearrange("(p t) c -> p t c", p=P)).then_inc(s_list, 16)
                    eng.wait_ge(s_list, 16)
                eng.sem_inc(s_here, 1)
                eng.dma_start(k.by_src[:, 0:NT, :], dram["src"].rearrange("(p t) c -> p t c", p=P)).then_inc(s_src, 16)
                eng.wait_ge(s_ev, NB)
                eng.dma_start(k.loc_rows.rearrange("(b p) e -> p b e", p=P), loc_t[:, :, :]).then_inc(s_row, 16)
                eng.wait_ge(s_row, 16)
                eng.wait_ge(s_src, 16)

            @block.vector
            def _(eng):
                c = Count(eng, s_dve)
                c.step(eng.memset(loc_c[:, :], -1.0))
                eng.wait_ge(s_here, 1)
                loc = k.by_dst[:, 0:NT, D_LOC]
                c.step(eng.tensor_tensor(loc, loc, k.first_node[:, :], ALU.subtract))
                eng.tensor_copy(loc_c[:, 0:NT], k.by_dst[:, 0:NT, D_LOC]).then_inc(s_cmp, 1)
                for b in range(NB):
                    eng.wait_ge(s_tr, b + 1)
                    eng.tensor_copy(loc_t[:, b, :], k.ps[:, b, 0:P]).then_inc(s_ev, 1)

            @block.tensor
            def _(eng):
                eng.wait_ge(s_cmp, 1)
                for b in range(NB):
                    eng.transpose(k.ps[:, b, 0:P], loc_c[:, b * P:(b + 1) * P], k.ident[:, :]).then_inc(s_tr, 1)
        k.end_phase()


class Where:

    def __init__(self, k, eng, table):
        self.k, self.eng, self.table = k, eng, table
        self.regs = [eng.alloc_register(f"where_{k.uid()}") for _ in range(2 * QUAD)]

    def load(self, quad):
        self.eng.load(self.regs, self.table[0:1, bass.ds(quad, 1), :].rearrange("p g j -> p (g j)"))
        col = [self.eng.snap(r, min_val=0, max_val=(NW - 1) * P) for r in self.regs[:QUAD]]
        scalar = [self.eng.snap(r, min_val=COL, max_val=COL + NW - 1) for r in self.regs[QUAD:]]
        return col, scalar


def banks():
    for b in range(NB):
        n = min(BANK, NP - b * BANK)
        yield b, b * BANK, n, b * BANK // P, n // P


def load_all(k, pairs, name):
    s = k.sem("s_load")
    with k.nc.Block() as block:
        @block.sync
        def _(eng):
            for dst, src in pairs:
                eng.dma_start(dst, src).then_inc(s, 16)
            eng.wait_ge(s, 16 * len(pairs))
    k.end_phase()


def load_x(k, x):
    k.x, k.h, k.hT = k.sb("x", [P, NW, D]), k.sb("h", [P, NW, D]), k.sb("hT", [P, NP])
    s_set, s_load = k.sem("s_set"), k.sem("s_load")
    with k.nc.Block() as block:
        @block.vector
        def _(eng):
            eng.memset(k.x[:, NW - 1, :], 0.0).then_inc(s_set, 1)

        @block.sync
        def _(eng):
            eng.dma_start(k.x[:, 0:NW - 1, :], x[0:(NW - 1) * P, :].rearrange("(w p) d -> p w d", p=P)).then_inc(s_load, 16)
            eng.wait_ge(s_set, 1)
            eng.dma_start(k.x[0:TAIL, NW - 1, :], x[(NW - 1) * P:N, :]).then_inc(s_load, 16)
            eng.wait_ge(s_load, 32)
    k.end_phase()


def normalise(k):
    nc = k.nc
    own = ExitStack()
    with own:
        sq = k.sb("sq", [P, NW, D], F32, own)
        stat = k.sb("stat", [P, NW], F32, own)
        s_dve, s_var, s_std, s_h, s_tr, s_ev = (k.sem(x) for x in ("s_dve", "s_var", "s_std", "s_h", "s_tr", "s_ev"))
        wide = lambda t: t[:, :].unsqueeze(2).to_broadcast([P, NW, D])
        with nc.Block() as block:
            @block.vector
            def _(eng):
                c = Count(eng, s_dve)
                c.step(eng.tensor_reduce(stat[:, :], k.x[:, :, :], AX.X, ALU.add))
                c.step(eng.tensor_scalar(stat[:, :], stat[:, :], 1.0 / D, None, ALU.mult))
                c.step(eng.tensor_tensor(k.h[:, :, :], k.x[:, :, :], wide(stat), ALU.subtract))
                c.step(eng.tensor_tensor(sq[:, :, :], k.h[:, :, :], k.h[:, :, :], ALU.mult))
                c.step(eng.tensor_reduce(stat[:, :], sq[:, :, :], AX.X, ALU.add))
                eng.tensor_scalar(stat[:, :], stat[:, :], 1.0 / D, 1e-5, ALU.mult, ALU.add).then_inc(s_var, 1)
                eng.wait_ge(s_std, 1)
                c.step(eng.reciprocal(stat[:, :], stat[:, :]))
                for b, _, _, w0, wn in banks():
                    part = k.h[:, w0:w0 + wn, :]
                    c.step(eng.tensor_tensor(part, part, stat[:, w0:w0 + wn].unsqueeze(2).to_broadcast([P, wn, D]), ALU.mult))
                    eng.tensor_scalar(part, part, 0.0, None, ALU.max).then_inc(s_h, 1)

            @block.scalar
            def _(eng):
                eng.wait_ge(s_var, 1)
                eng.activation(stat[:, :], stat[:, :], ACT.Sqrt).then_inc(s_std, 1)
                evacuate(k, eng, s_tr, s_ev, k.hT)

            @block.tensor
            def _(eng):
                turn(k, eng, k.h, s_h, s_tr)
        k.end_phase()


def turn(k, eng, rows, s_ready, s_done, s_free=None):
    for b, _, n, w0, wn in banks():
        eng.wait_ge(s_ready, b + 1)
        if s_free:
            eng.wait_ge(s_free, b + 1)
        for j in range(wn):
            last = eng.transpose(k.ps[:, b, j * P:(j + 1) * P], rows[:, w0 + j, :], k.ident[:, :])
        last.then_inc(s_done, 1)


def evacuate(k, eng, s_full, s_done, cols):
    for b, c0, n, _, _ in banks():
        eng.wait_ge(s_full, b + 1)
        eng.activation(cols[:, c0:c0 + n], k.ps[:, b, 0:n], ACT.Copy).then_inc(s_done, 1)


def table(k, own, weights, width, dram_rows, bias=None, keep=None, shared=None):
    nc = k.nc
    out_n = shared or width
    nb = -(-width // BANK)
    G = 5 if nb == 1 else 1
    st = k.sb("rows", [P, 2, G, out_n], F32, own)
    s_mm, s_row, s_keep = (k.sem(x) for x in ("s_mm", "s_row", "s_keep"))
    s_st = [k.sem(f"s_st{j}") for j in range(2)]
    half = 8 // nb
    cut = out_n if nb == 1 else BANK

    parts = len(dram_rows(0, G, st[:, 0, :, :]))

    with nc.Block() as block:
        @block.tensor
        def _(eng):
            for w in range(NW):
                if w >= half:
                    eng.wait_ge(s_row, (w - half + 1) * nb)
                    if keep is not None:
                        eng.wait_ge(s_keep, w - half + 1)
                for j in range(nb):
                    eng.matmul(k.ps[:, (w % half) * nb + j, :], k.hT[:, w * P:(w + 1) * P],
                               weights[:, j * BANK:(j + 1) * BANK], start=True, stop=True).then_inc(s_mm, 1)

        def rows(eng, w, j):
            g = w // G
            eng.wait_ge(s_mm, w * nb + j + 1)
            if g >= 2:
                eng.wait_ge(s_st[g % 2], 16 * parts * (g // 2))
            dst = st[:, g % 2, w % G, j * BANK:j * BANK + cut]
            src = k.ps[:, (w % half) * nb + j, 0:cut]
            return dst, src

        @block.scalar
        def _(eng):
            if bias is not None and keep is None:
                return
            for w in range(NW):
                for j in range(nb):
                    dst, src = rows(eng, w, j)
                    eng.activation(dst, src, ACT.Copy).then_inc(s_row, 1)

        @block.vector
        def _(eng):
            if keep is not None:
                for w in range(NW):
                    eng.wait_ge(s_row, w + 1)
                    eng.tensor_tensor(keep[:, w, :], k.ps[:, w % 8, shared:width], bias[:, :], ALU.add).then_inc(s_keep, 1)
            elif bias is not None:
                for w in range(NW):
                    for j in range(nb):
                        dst, src = rows(eng, w, j)
                        eng.tensor_tensor(dst, src, bias[:, j * BANK:(j + 1) * BANK], ALU.add).then_inc(s_row, 1)

        @block.sync
        def _(eng):
            for g in range(NW // G):
                eng.wait_ge(s_row, (g + 1) * G * nb)
                for dst, src in dram_rows(g * G, G, st[:, g % 2, :, :]):
                    eng.dma_start(dst, src).then_inc(s_st[g % 2], 16)
            for j in range(2):
                eng.wait_ge(s_st[j], 16 * parts * len(range(j, NW // G, 2)))
    k.end_phase()


def edge_pass(k, own, rows, words, loc, idx, where, weight=None, column=None, flipped=False):
    nc = k.nc
    body, bodies = QUAD * NQ, NT // (QUAD * NQ)
    ring = k.sb("ring", [P, NQ * QUAD, D], F32, own)
    mark = k.sb("mark", [P, NQ, QUAD, P], F32, own)
    stage = k.sb("stage", [P, NQ * QUAD], I32, own)
    s_full = [k.sem(f"s_full{q}") for q in range(NQ)]
    s_staged, s_mark, s_done, s_go = (k.sem(x) for x in ("s_staged", "s_mark", "s_done", "s_go"))
    index = lambda t0, n: words[:, bass.ds(t0, n), idx]

    with nc.Block() as block:
        @block.scalar
        def _(eng):
            for q in range(NQ):
                eng.activation(stage[:, q * QUAD:(q + 1) * QUAD], index(q * QUAD, QUAD), ACT.Copy).then_inc(s_staged, 1)
            with eng.Fori(0, bodies) as i:
                for q in range(NQ):
                    eng.wait_ge(s_full[q], i * (16 * QUAD) + 16 * QUAD)
                    eng.activation(stage[:, q * QUAD:(q + 1) * QUAD], index(i * body + body + q * QUAD, QUAD),
                                   ACT.Copy).then_inc(s_staged, 1)

        @block.gpsimd
        def _(eng):
            with eng.Fori(0, bodies) as i:
                for q in range(NQ):
                    eng.wait_ge(s_staged, i * NQ + q + 1)
                    eng.wait_ge(s_done, i * NQ + q + 1)
                    eng.sem_inc(s_go, 1)
                    for t in range(q * QUAD, (q + 1) * QUAD):
                        eng.indirect_dma_start(ring[:, t, :], None, rows,
                                               bass.IndirectOffsetOnAxis(stage[:, t:t + 1], 0)).then_inc(s_full[q], 16)
            for q in range(NQ):
                eng.wait_ge(s_full[q], bodies * 16 * QUAD)

        @block.vector
        def _(eng):
            with eng.Fori(0, bodies) as i:
                for q in range(NQ):
                    at = i * body + q * QUAD
                    eng.wait_ge(s_done, i * NQ + q + 1)
                    eng.tensor_tensor(mark[:, q, :, :], k.tile_no[:, 0:P].unsqueeze(1).to_broadcast([P, QUAD, P]),
                                      words[:, bass.ds(at, QUAD), loc].unsqueeze(2).to_broadcast([P, QUAD, P]),
                                      ALU.is_equal).then_inc(s_mark, 1)
                    if weight is not None:
                        eng.wait_ge(s_full[q], i * (16 * QUAD) + 16 * QUAD)
                        part = ring[:, q * QUAD:(q + 1) * QUAD, :]
                        eng.tensor_tensor(part, part, words[:, bass.ds(at, QUAD), weight].unsqueeze(2)
                                          .to_broadcast([P, QUAD, D]), ALU.mult).then_inc(s_mark, 1)

        @block.tensor
        def _(eng):
            per = 1 if weight is None else 2
            eng.sem_inc(s_done, NQ)
            open_banks(k, eng)
            tiles = Where(k, eng, where)
            with eng.Fori(0, bodies) as i:
                for q in range(NQ):
                    at = i * body + q * QUAD
                    cols, scalars = tiles.load(i * NQ + q)
                    eng.wait_ge(s_mark, i * (NQ * per) + (q + 1) * per)
                    if weight is None:
                        eng.wait_ge(s_full[q], i * (16 * QUAD) + 16 * QUAD)
                    for j in range(QUAD):
                        row, marks = ring[:, q * QUAD + j, :], mark[:, q, j, :]
                        left, right = (row, marks) if flipped else (marks, row)
                        last = eng.matmul(k.psf[:, bass.ds(cols[j], P)], left, right, start=False, stop=False,
                                          skip_group_check=True)
                        if column == "weight":
                            last = eng.matmul(k.psf[:, bass.ds(scalars[j], 1)], marks,
                                              words[:, bass.ds(at + j, 1), weight], start=False, stop=False,
                                              skip_group_check=True)
                        if column == "one":
                            last = eng.matmul(k.psf[:, bass.ds(scalars[j], 1)], marks, k.ones[:, 0:1],
                                              start=False, stop=False, skip_group_check=True)
                    last.then_inc(s_done, 1)
            close_banks(k, eng)
    k.end_phase()


def open_banks(k, eng):
    for b in range(NB):
        eng.matmul(k.ps[:, b, :], k.zeros[:, 0:P], k.zeros[:, :], start=True, stop=False, skip_group_check=True)


def close_banks(k, eng):
    for b in range(NB):
        eng.matmul(k.ps[:, b, :], k.zeros[:, 0:P], k.zeros[:, :], start=False, stop=True, skip_group_check=True)


def attention_pass(k, own, rows, here, w_att, b_att):
    nc = k.nc
    NQ = NQ0
    LAG = 2
    in_body, bodies = QUAD * NQ, NT // (QUAD * NQ)
    W2 = 2 * D
    ring = k.sb("ring", [P, NQ * QUAD, W2], F32, own)
    mark = k.sb("mark", [P, NQ, QUAD, P], F32, own)
    spread = k.sb("spread", [P, NQ, QUAD * P], F32, own)
    locs = k.sb("locs", [P, NQ, QUAD * P], BF16, own)
    stage = k.sb("stage", [P, NQ * QUAD], I32, own)
    dot = k.sb("dot", [P, NQ * QUAD], F32, own)
    att = k.sb("att", [P, NQ * QUAD], F32, own)
    s_full = [k.sem(f"s_full{q}") for q in range(NQ)]
    s_locs = [k.sem(f"s_locs{q}") for q in range(NQ)]
    s_staged, s_mark, s_done, s_go = (k.sem(x) for x in ("s_staged", "s_mark", "s_done", "s_go"))
    s_spread, s_exp, s_add, s_dot, s_att, s_msg = (k.sem(x) for x in ("s_spread", "s_exp", "s_add", "s_dot", "s_att", "s_msg"))
    words = k.by_dst
    index = lambda t0, n: words[:, bass.ds(t0, n), D_SRC]
    hid = k.ps[:, 7, :].rearrange("p (s c) -> p s c", s=2)

    with nc.Block() as block:
        @block.sync
        def _(eng):
            def fetch(t0, q):
                eng.dma_start(locs[:, q, :], k.loc_rows[bass.ds(t0, QUAD), :].rearrange("t e -> (t e)").partition_broadcast(P)).then_inc(s_locs[q], 16)
            for q in range(NQ):
                fetch(q * QUAD, q)
            with eng.Fori(0, bodies) as i:
                for q in range(NQ):
                    eng.wait_ge(s_spread, i * NQ + q + 1)
                    fetch(i * in_body + in_body + q * QUAD, q)
            for q in range(NQ):
                eng.wait_ge(s_locs[q], 16 * (bodies + 1))

        @block.gpsimd
        def _(eng):
            with eng.Fori(0, bodies) as i:
                for q in range(NQ):
                    eng.wait_ge(s_staged, i * NQ + q + 1)
                    eng.wait_ge(s_done, i * NQ + q + 1)
                    eng.sem_inc(s_go, 1)
                    for t in range(q * QUAD, (q + 1) * QUAD):
                        eng.indirect_dma_start(ring[:, t, :], None, rows,
                                               bass.IndirectOffsetOnAxis(stage[:, t:t + 1], 0)).then_inc(s_full[q], 16)
            for q in range(NQ):
                eng.wait_ge(s_full[q], bodies * 16 * QUAD)

        @block.vector
        def _(eng):
            def spread_quad(i, q, g):
                eng.wait_ge(s_locs[q], i * 16 + 16)
                eng.wait_ge(s_exp, g * 2 + 2)
                eng.tensor_scalar(spread[:, q, :], locs[:, q, :], k.lane[:, 0:1], None, ALU.is_equal).then_inc(s_spread, 1)

            def body(i, last):
                for q in range(NQ):
                    g = i * NQ + q
                    at = i * in_body + q * QUAD
                    if q + 1 < NQ:
                        spread_quad(i, q + 1, g + 1)
                    elif not last:
                        spread_quad(i + 1, 0, g + 1)
                    eng.wait_ge(s_done, g + 1)
                    eng.tensor_tensor(mark[:, q, :, :], k.tile_no[:, 0:P].unsqueeze(1).to_broadcast([P, QUAD, P]),
                                      words[:, bass.ds(at, QUAD), D_LOC].unsqueeze(2).to_broadcast([P, QUAD, P]),
                                      ALU.is_equal).then_inc(s_mark, 1)
                    eng.wait_ge(s_full[q], i * (16 * QUAD) + 16 * QUAD)
                    for pair in range(2):
                        t = q * QUAD + pair * 2
                        eng.wait_ge(s_exp, g * 2 + (pair + 1 + NQ * 2))
                        eng.tensor_tensor(ring[:, t:t + 2, :], ring[:, t:t + 2, :], hid, ALU.add).then_inc(s_add, 1)
                        for j in (pair * 2, pair * 2 + 1):
                            eng.wait_ge(s_add, g * 2 + (j // 2 + 2))
                            t = q * QUAD + j
                            eng.scalar_tensor_tensor(ring[:, t, D:W2], ring[:, t, D:W2], 0.0, w_att[:, :], ALU.max, ALU.mult,
                                                     accum_out=dot[:, t:t + 1]).then_inc(s_dot, 1)
            eng.sem_inc(s_add, 1)
            spread_quad(0, 0, 0)
            with eng.Fori(0, bodies - 1) as i:
                body(i, False)
            body(bodies - 1, True)

        @block.scalar
        def _(eng):
            for q in range(NQ):
                eng.activation(stage[:, q * QUAD:(q + 1) * QUAD], index(q * QUAD, QUAD), ACT.Copy).then_inc(s_staged, 1)
            with eng.Fori(0, bodies) as i:
                for q in range(NQ):
                    g = i * NQ + q
                    eng.wait_ge(s_full[q], i * (16 * QUAD) + 16 * QUAD)
                    eng.activation(stage[:, q * QUAD:(q + 1) * QUAD], index(i * in_body + in_body + q * QUAD, QUAD),
                                   ACT.Copy).then_inc(s_staged, 1)
                    eng.wait_ge(s_dot, g * QUAD + QUAD)
                    eng.activation(att[:, q * QUAD:(q + 1) * QUAD], dot[:, q * QUAD:(q + 1) * QUAD], ACT.Sigmoid,
                                   bias=b_att[:, 0:1]).then_inc(s_att, 1)
                    eng.wait_ge(s_att, g + 1)
                    for j in range(QUAD):
                        t = q * QUAD + j
                        eng.activation(ring[:, t, 0:D], ring[:, t, 0:D], ACT.Relu, scale=att[:, t:t + 1]).then_inc(s_msg, 1)

        @block.tensor
        def _(eng):
            tiles = Where(k, eng, k.where["dst"])

            def expand(g, q, pair, cols):
                eng.wait_ge(s_add, g * 2 + (pair + 1))
                for j in range(2):
                    t = pair * 2 + j
                    last = eng.matmul(hid[:, j, :], spread[:, q, t * P:(t + 1) * P], here[:, bass.ds(cols[t] * 2, W2)],
                                      start=True, stop=True)
                last.then_inc(s_exp, 1)

            def body(i, last):
                for q in range(NQ):
                    g = i * NQ + q
                    more = q + LAG < NQ or not last
                    if more:
                        ahead, _ = tiles.load(g + LAG)
                    now, scalar = tiles.load(g)
                    if more:
                        eng.wait_ge(s_spread, g + (LAG + 1))
                    eng.wait_ge(s_mark, g + 1)
                    for j in range(QUAD):
                        if more and j % 2 == 0:
                            expand(g + LAG, (q + LAG) % NQ, j // 2, ahead)
                        eng.wait_ge(s_msg, g * QUAD + (j + 1))
                        eng.matmul(k.psf[:, bass.ds(now[j], D)], mark[:, q, j, :], ring[:, q * QUAD + j, 0:D],
                                   start=False, stop=False, skip_group_check=True)
                        done = eng.matmul(k.psf[:, bass.ds(scalar[j], 1)], mark[:, q, j, :],
                                          att[:, q * QUAD + j:q * QUAD + j + 1], start=False, stop=False,
                                          skip_group_check=True)
                    done.then_inc(s_done, 1)

            eng.sem_inc(s_done, NQ)
            eng.sem_inc(s_exp, NQ * 2)
            open_banks(k, eng)
            for g in range(LAG):
                first, _ = tiles.load(g)
                eng.wait_ge(s_spread, g + 1)
                for pair in range(2):
                    expand(g, g, pair, first)
            with eng.Fori(0, bodies - 1) as i:
                body(i, False)
            body(bodies - 1, True)
            close_banks(k, eng)
    k.end_phase()


def accumulated(k, rows, column=None):
    s_a, s_v = k.sem("s_a"), k.sem("s_v")
    flat = rows.rearrange("p w d -> p (w d)") if len(rows.shape) == 3 else rows
    with k.nc.Block() as block:
        @block.scalar
        def _(eng):
            for b, c0, n, _, _ in banks():
                if b % 2:
                    eng.activation(flat[:, c0:c0 + n], k.ps[:, b, 0:n], ACT.Copy).then_inc(s_a, 1)

        @block.vector
        def _(eng):
            for b, c0, n, _, _ in banks():
                if not b % 2:
                    eng.tensor_copy(flat[:, c0:c0 + n], k.ps[:, b, 0:n]).then_inc(s_v, 1)
            if column is not None:
                eng.tensor_copy(column, k.psf[:, COL:COL + NW]).then_inc(s_v, 1)
    k.end_phase()


def layer0(k, a):
    nc = k.nc
    own = ExitStack()
    with own:
        sb = lambda name, shape, dt=F32: k.sb(name, shape, dt, own)
        w1 = sb("w1", [P, 4 * D])
        bias1 = sb("bias1", [P, 2 * D])
        w2, b2 = sb("w2", [P, D]), sb("b2", [P, D])
        u1, u2 = sb("u1", [P, 2, D]), sb("u2", [P, D])
        c1, c2 = sb("c1", [P, 1]), sb("c2", [P, D])
        wg, bg = sb("wg", [P, D]), sb("bg", [P, D])
        w_att, b_att = sb("w_att", [P, D]), sb("b_att", [P, 1])
        glob = sb("glob", [P, D])
        here = sb("here", [P, NW, 2 * D])
        mean_wide = sb("mean_wide", [P, P])
        att_sum = sb("att_sum", [P, NW])
        mean = sb("mean", [P, 1])
        rows = nc.dram_tensor("rows0", [NP, 2 * D], F32, kind="Internal").ap()
        L = "L0_gnn_"
        wide = lambda v: a[L + v].partition_broadcast(P)
        load_all(k, [(w1[:, 0:D], a[L + "msg_W1"][0:D, :]), (w1[:, D:2 * D], a[L + "att_W1"][0:D, :]),
                     (w1[:, 2 * D:3 * D], a[L + "msg_W1"][D:2 * D, :]), (w1[:, 3 * D:4 * D], a[L + "att_W1"][D:2 * D, :]),
                     (bias1[:, 0:D], wide("msg_b1")), (bias1[:, D:2 * D], wide("att_b1")),
                     (w2[:, :], a[L + "msg_W2"]), (b2[:, :], wide("msg_b2")),
                     (u1[:, :, :], a[L + "upd_W1"].rearrange("(s p) d -> p s d", p=P)), (u2[:, :], a[L + "upd_W2"]),
                     (c1[:, :], a[L + "upd_b1"]), (c2[:, :], wide("upd_b2")),
                     (wg[:, :], a[L + "glb_W"]), (bg[:, :], wide("glb_b")),
                     (w_att[:, :], a[L + "att_W2"].partition_broadcast(P)), (b_att[:, :], wide("att_b2"))], "w0")
        s_dve, s_mean, s_g = k.sem("s_dve"), k.sem("s_mean"), k.sem("s_g")
        with nc.Block() as block:
            @block.vector
            def _(eng):
                c = Count(eng, s_dve)
                c.step(eng.tensor_reduce(mean[:, :], k.hT[:, 0:N], AX.X, ALU.add))
                c.step(eng.tensor_scalar(mean[:, :], mean[:, :], 1.0 / N, None, ALU.mult))
                eng.tensor_scalar(mean_wide[:, :], k.ones[:, 0:P], mean[:, 0:1], None, ALU.mult).then_inc(s_mean, 1)
                eng.wait_ge(s_g, 1)
                c.step(eng.tensor_tensor(glob[:, :], k.ps[:, 0, 0:D], bg[:, :], ALU.add))
                c.step(eng.scalar_tensor_tensor(glob[:, :], glob[:, :], 0.0, c2[:, :], ALU.max, ALU.add))

            @block.tensor
            def _(eng):
                eng.wait_ge(s_mean, 1)
                eng.matmul(k.ps[:, 0, 0:D], mean_wide[:, :], wg[:, :], start=True, stop=True).then_inc(s_g, 1)
        k.end_phase()

        with nc.Fori(0, 2) as _step:
            with ExitStack() as inner:
                table(k, inner, w1, 4 * D, lambda w0, n, st: [(rows[w0 * P:(w0 + n) * P, :].rearrange("(w p) d -> p w d", p=P), st)],
                      bias=bias1, keep=here, shared=2 * D)
            with ExitStack() as inner:
                attention_pass(k, inner, rows, here.rearrange("p w d -> p (w d)"), w_att, b_att)
            with ExitStack() as inner:
                agg = k.sb("agg", [P, NW, D], F32, inner)
                aggT, zT = k.sb("aggT", [P, NP], F32, inner), k.sb("zT", [P, NP], F32, inner)
                accumulated(k, agg, att_sum[:, :])
                update0(k, agg, aggT, zT, att_sum, w2, b2, u1, c1, u2, glob)
        s_x = k.sem("s_x")
        with nc.Block() as block:
            @block.vector
            def _(eng):
                eng.tensor_tensor(k.x[:, :, :], k.x[:, :, :], k.h[:, :, :], ALU.add).then_inc(s_x, 1)
        k.end_phase()


def update0(k, agg, aggT, zT, att_sum, w2, b2, u1, c1, u2, glob):
    S = {n: (k.sem(f"s_pe_{n}"), k.sem(f"s_ev_{n}")) for n in "ABCDEF"}
    s_dve = k.sem("s_dve")
    with k.nc.Block() as block:
        @block.tensor
        def _(eng):
            def stage(name, before, product):
                for b, c0, n, w0, wn in banks():
                    if before:
                        eng.wait_ge(S[before][1], b + 1)
                    last = product(b, c0, n, w0, wn)
                    last.then_inc(S[name][0], 1)

            def turned(b, c0, n, w0, wn, rows):
                for j in range(wn):
                    last = eng.transpose(k.ps[:, b, j * P:(j + 1) * P], rows[:, w0 + j, :], k.ident[:, :])
                return last

            def times(b, c0, n, w0, wn, cols, w):
                for j in range(wn):
                    last = eng.matmul(k.ps[:, b, j * P:(j + 1) * P], cols[:, (w0 + j) * P:(w0 + j + 1) * P], w[:, :],
                                      start=True, stop=True)
                return last

            def hidden(b, c0, n, w0, wn):
                eng.matmul(k.ps[:, b, 0:n], u1[:, 0, :], k.hT[:, c0:c0 + n], start=True, stop=False)
                return eng.matmul(k.ps[:, b, 0:n], u1[:, 1, :], aggT[:, c0:c0 + n], start=False, stop=True)

            stage("A", None, lambda *s: turned(*s, agg))
            stage("B", "A", lambda *s: times(*s, aggT, w2))
            stage("C", "B", lambda *s: turned(*s, agg))
            stage("D", "C", hidden)
            stage("E", "D", lambda *s: times(*s, zT, u2))
            stage("F", "E", lambda *s: turned(*s, k.h))

        @block.scalar
        def _(eng):
            for name, out in (("A", aggT), ("C", aggT), ("D", zT), ("F", k.hT)):
                for b, c0, n, _, _ in banks():
                    eng.wait_ge(S[name][0], b + 1)
                    if name == "D":
                        eng.activation(out[:, c0:c0 + n], k.ps[:, b, 0:n], ACT.Relu, bias=c1[:, 0:1]).then_inc(S[name][1], 1)
                    else:
                        eng.activation(out[:, c0:c0 + n], k.ps[:, b, 0:n], ACT.Copy).then_inc(S[name][1], 1)

        @block.vector
        def _(eng):
            c = Count(eng, s_dve)
            for b, c0, n, w0, wn in banks():
                eng.wait_ge(S["B"][0], b + 1)
                for j in range(wn):
                    ins = eng.scalar_tensor_tensor(agg[:, w0 + j, :], b2[:, :], att_sum[:, w0 + j:w0 + j + 1],
                                                   k.ps[:, b, j * P:(j + 1) * P], ALU.mult, ALU.add)
                ins.then_inc(S["B"][1], 1)
            for b, c0, n, w0, wn in banks():
                eng.wait_ge(S["E"][0], b + 1)
                part = k.h[:, w0:w0 + wn, :]
                c.step(eng.tensor_tensor(part, part, glob[:, :].unsqueeze(1).to_broadcast([P, wn, D]), ALU.add))
                eng.tensor_tensor(part, part, k.ps[:, b, 0:n].rearrange("p (w d) -> p w d", d=D), ALU.add)\
                   .then_inc(S["E"][1], 1)
    k.end_phase()


def gru(k, inputs, w_h, b_r, b_z, b_i, b_n, buf):
    r, z, t, n_ = buf
    s_pe, s_rz, s_pre, s_n, s_dve, s_new = (k.sem(x) for x in ("s_pe", "s_rz", "s_pre", "s_n", "s_dve", "s_new"))
    R, Z, I, H = range(4)
    with k.nc.Block() as block:
        @block.tensor
        def _(eng):
            for b, c0, n, _, _ in banks():
                if b >= 2:
                    eng.wait_ge(s_pre, b - 1)
                bank = lambda g: k.ps[:, (b % 2) * 4 + g, 0:n]
                for g in (R, Z, I):
                    for m, (cols, w) in enumerate(inputs):
                        eng.matmul(bank(g), w[:, g * D:(g + 1) * D], cols[:, c0:c0 + n], start=m == 0,
                                   stop=g == I and m + 1 == len(inputs))
                    if g != I:
                        eng.matmul(bank(g), w_h[:, g * D:(g + 1) * D], k.hT[:, c0:c0 + n], start=False, stop=True)
                eng.matmul(bank(H), w_h[:, 2 * D:3 * D], k.hT[:, c0:c0 + n], start=True, stop=True).then_inc(s_pe, 1)

        @block.scalar
        def _(eng):
            def gates(b, n):
                eng.wait_ge(s_pe, b + 1)
                if b >= 2:
                    eng.wait_ge(s_new, b - 1)
                eng.activation(r[:, b % 2, 0:n], k.ps[:, (b % 2) * 4 + R, 0:n], ACT.Sigmoid, bias=b_r).then_inc(s_rz, 1)
                eng.activation(z[:, b % 2, 0:n], k.ps[:, (b % 2) * 4 + Z, 0:n], ACT.Sigmoid, bias=b_z).then_inc(s_rz, 1)
            every = list(banks())
            gates(0, every[0][2])
            for b, c0, n, _, _ in every:
                if b + 1 < NB:
                    gates(b + 1, every[b + 1][2])
                eng.wait_ge(s_pre, b + 1)
                eng.activation(n_[:, b % 2, 0:n], t[:, b % 2, 0:n], ACT.Tanh, bias=b_i).then_inc(s_n, 1)

        @block.vector
        def _(eng):
            c = Count(eng, s_dve)
            for b, c0, n, _, _ in banks():
                p = b % 2
                eng.wait_ge(s_rz, 2 * b + 2)
                c.step(eng.scalar_tensor_tensor(t[:, p, 0:n], k.ps[:, p * 4 + H, 0:n], b_n, r[:, p, 0:n], ALU.add, ALU.mult))
                eng.tensor_tensor(t[:, p, 0:n], t[:, p, 0:n], k.ps[:, p * 4 + I, 0:n], ALU.add).then_inc(s_pre, 1)
                eng.wait_ge(s_n, b + 1)
                h = k.hT[:, c0:c0 + n]
                c.step(eng.tensor_tensor(h, h, n_[:, p, 0:n], ALU.subtract))
                c.step(eng.tensor_tensor(h, h, z[:, p, 0:n], ALU.mult))
                eng.tensor_tensor(h, h, n_[:, p, 0:n], ALU.add).then_inc(s_new, 1)
    k.end_phase()


def gru_weights(k, own, a, name, wide_in):
    ih = k.sb("w_ih", [P, wide_in, 3 * D], F32, own)
    hh = k.sb("w_hh", [P, 3 * D], F32, own)
    bi, bh = k.sb("b_ih", [P, 3], F32, own), k.sb("b_hh", [P, 3], F32, own)
    both = k.sb("b_both", [P, 3], F32, own)
    load_all(k, [(ih[:, :, :], a[name + "ih"].rearrange("(s p) g -> p s g", p=P)), (hh[:, :], a[name + "hh"]),
                 (bi[:, :], a[name + "b_ih"]), (bh[:, :], a[name + "b_hh"])], "gru")
    s = k.sem("s_dve")
    with k.nc.Block() as block:
        @block.vector
        def _(eng):
            eng.tensor_tensor(both[:, :], bi[:, :], bh[:, :], ALU.add).then_inc(s, 1)
    k.end_phase()
    return ih, hh, both, bi, bh


def add_turned(k):
    s_tr, s_x = k.sem("s_tr"), k.sem("s_x")
    with k.nc.Block() as block:
        @block.tensor
        def _(eng):
            for b, c0, n, w0, wn in banks():
                for j in range(wn):
                    last = eng.transpose(k.ps[:, b, j * P:(j + 1) * P], k.hT[:, c0 + j * P:c0 + (j + 1) * P], k.ident[:, :])
                last.then_inc(s_tr, 1)

        @block.vector
        def _(eng):
            for b, c0, n, w0, wn in banks():
                eng.wait_ge(s_tr, b + 1)
                part = k.x[:, w0:w0 + wn, :]
                eng.tensor_tensor(part, part, k.ps[:, b, 0:n].rearrange("p (w d) -> p w d", d=D), ALU.add).then_inc(s_x, 1)
    k.end_phase()


def store_h(k, rows):
    s = k.sem("s_load")
    with k.nc.Block() as block:
        @block.sync
        def _(eng):
            eng.dma_start(rows.rearrange("(w p) d -> p w d", p=P), k.h[:, :, :]).then_inc(s, 16)
            eng.wait_ge(s, 16)
    k.end_phase()


def layer1(k, a):
    nc = k.nc
    own = ExitStack()
    with own:
        sb = lambda name, shape, dt=F32: k.sb(name, shape, dt, own)
        wn = [sb("wn1", [P, D]), sb("wn2", [P, D])]
        mean = sb("mean", [P, NW, D])
        meanT = sb("meanT", [P, NP])
        mixT = [sb("mix1", [P, NP]), sb("mix2", [P, NP])]
        total, some, safe = sb("total", [P, NW]), sb("some", [P, NW]), sb("safe", [P, NW])
        buf = [sb(f"gru{j}", [P, 2, BANK]) for j in range(4)]
        rows = nc.dram_tensor("rows1", [NP, D], F32, kind="Internal").ap()
        store_h(k, rows)
        load_all(k, [(wn[0][:, :], a["L1_W1T"]), (wn[1][:, :], a["L1_W2T"])], "w1")
        ih, hh, both, bi, bh = gru_weights(k, own, a, "L1_", 2)
        for m, (words, idx, where) in enumerate(((k.by_dst, D_SRC, k.where["dst"]), (k.by_src, S_DST, k.where["src"]))):
            inner = ExitStack()
            with inner:
                edge_pass(k, inner, rows, words, D_LOC, idx, where, weight=D_W, column="weight")
                accumulated(k, mean, total[:, :])
            s_dve, s_ready = k.sem("s_dve"), k.sem("s_ready")
            S = {n: (k.sem(f"s_pe_{n}"), k.sem(f"s_ev_{n}")) for n in "AB"}
            with nc.Block() as block:
                @block.vector
                def _(eng):
                    c = Count(eng, s_dve)
                    c.step(eng.tensor_scalar(some[:, :], total[:, :], 0.0, None, ALU.is_gt))
                    c.step(eng.tensor_scalar(safe[:, :], some[:, :], -1.0, 1.0, ALU.mult, ALU.add))
                    c.step(eng.tensor_tensor(total[:, :], total[:, :], some[:, :], ALU.mult))
                    c.step(eng.tensor_tensor(safe[:, :], safe[:, :], total[:, :], ALU.add))
                    c.step(eng.reciprocal(safe[:, :], safe[:, :]))
                    c.step(eng.tensor_tensor(safe[:, :], safe[:, :], some[:, :], ALU.mult))
                    for b, _, _, w0, n in banks():
                        part = mean[:, w0:w0 + n, :]
                        eng.tensor_tensor(part, part, safe[:, w0:w0 + n].unsqueeze(2).to_broadcast([P, n, D]), ALU.mult)\
                           .then_inc(s_ready, 1)

                @block.tensor
                def _(eng):
                    turn(k, eng, mean, s_ready, S["A"][0])
                    for b, c0, n, _, _ in banks():
                        eng.wait_ge(S["A"][1], b + 1)
                        eng.matmul(k.ps[:, b, 0:n], wn[m][:, :], meanT[:, c0:c0 + n], start=True, stop=True)\
                           .then_inc(S["B"][0], 1)

                @block.scalar
                def _(eng):
                    evacuate(k, eng, *S["A"], meanT)
                    evacuate(k, eng, *S["B"], mixT[m])
            k.end_phase()
        gru(k, [(mixT[0], ih[:, 0, :]), (mixT[1], ih[:, 1, :])], hh, both[:, 0:1], both[:, 1:2], bi[:, 2:3], bh[:, 2:3], buf)
        add_turned(k)


def layer2(k, a):
    nc = k.nc
    own = ExitStack()
    with own:
        sb = lambda name, shape, dt=F32: k.sb(name, shape, dt, own)
        we, be = sb("we", [P, T4 * D]), sb("be", [P, T4 * D])
        sumT = sb("sumT", [P, NP])
        buf = [sb(f"gru{j}", [P, 2, BANK]) for j in range(4)]
        rows = nc.dram_tensor("rows2", [T4, NP, D], F32, kind="Internal").ap()
        load_all(k, [(we[:, :], a["L2_We"]), (be[:, :], a["L2_be"].partition_broadcast(P))], "w2")
        ih, hh, both, bi, bh = gru_weights(k, own, a, "L2_", 1)
        with nc.Fori(0, 4) as _step:
            with ExitStack() as inner:
                table(k, inner, we, T4 * D,
                      lambda w0, n, st: [(rows[t, w0 * P:(w0 + n) * P, :].rearrange("(w p) d -> p w d", p=P), st[:, :, t * D:(t + 1) * D])
                                         for t in range(T4)],
                      bias=be)
            with ExitStack() as inner:
                edge_pass(k, inner, rows.rearrange("t n d -> (t n) d"), k.by_dst, D_LOC, D_T4, k.where["dst"], flipped=True)
            accumulated(k, sumT)
            gru(k, [(sumT, ih[:, 0, :])], hh, both[:, 0:1], both[:, 1:2], bi[:, 2:3], bh[:, 2:3], buf)
        add_turned(k)


def layer3(k, a, out):
    nc = k.nc
    own = ExitStack()
    with own:
        sb = lambda name, shape, dt=F32: k.sb(name, shape, dt, own)
        coef = sb("coef", [P, T16, 8])
        bases = sb("bases", [P, 8, D])
        loop = sb("loop", [P, D])
        agg = sb("agg", [P, NW, D])
        deg = sb("deg", [P, NW])
        rows = nc.dram_tensor("rows3", [T16, NP, D], F32, kind="Internal").ap()
        load_all(k, [(coef[:, :, :].rearrange("p r b -> p (r b)"), a["L3_gnn_coefficients"].partition_broadcast(P)),
                     (bases[:, :, :], a["L3_bases"]), (loop[:, :], a["L3_gnn_self_loop"])], "w3")
        s_dve = k.sem("s_dve")
        early = ExitStack()
        with early:
            rel = k.sb("rel", [P, T16, D], F32, early)
            part = k.sb("part3", [P, T16, D], F32, early)
            with nc.Block() as block:
                @block.vector
                def _(eng):
                    c = Count(eng, s_dve)
                    for b in range(8):
                        out_ = rel if b == 0 else part
                        c.step(eng.tensor_tensor(out_[:, :, :], bases[:, b, :].unsqueeze(1).to_broadcast([P, T16, D]),
                                                 coef[:, :, b].unsqueeze(2).to_broadcast([P, T16, D]), ALU.mult))
                        if b:
                            c.step(eng.tensor_tensor(rel[:, :, :], rel[:, :, :], part[:, :, :], ALU.add))
            k.end_phase()
            table(k, early, rel.rearrange("p r d -> p (r d)"), T16 * D,
                  lambda w0, n, st: [(rows[:, w0 * P:(w0 + 1) * P, :].rearrange("r p d -> p r d"),
                                      st[:, 0, :].rearrange("p (r d) -> p r d", d=D))])
        late = ExitStack()
        with late:
            edge_pass(k, late, rows.rearrange("r n d -> (r n) d"), k.by_dst, D_LOC, D_T16, k.where["dst"], column="one")
            accumulated(k, agg, deg[:, :])
        s_mm, s_out, s_x = k.sem("s_mm"), k.sem("s_out"), k.sem("s_x")
        with nc.Block() as block:
            @block.tensor
            def _(eng):
                for b, c0, n, w0, wn in banks():
                    for j in range(wn):
                        last = eng.matmul(k.ps[:, b, j * P:(j + 1) * P], k.hT[:, c0 + j * P:c0 + (j + 1) * P], loop[:, :],
                                          start=True, stop=True)
                    last.then_inc(s_mm, 1)

            @block.vector
            def _(eng):
                c = Count(eng, s_dve)
                c.step(eng.tensor_scalar(deg[:, :], deg[:, :], 1.0, None, ALU.max))
                c.step(eng.reciprocal(deg[:, :], deg[:, :]))
                for b, c0, n, w0, wn in banks():
                    part, x = agg[:, w0:w0 + wn, :], k.x[:, w0:w0 + wn, :]
                    c.step(eng.tensor_tensor(part, part, deg[:, w0:w0 + wn].unsqueeze(2).to_broadcast([P, wn, D]), ALU.mult))
                    eng.wait_ge(s_mm, b + 1)
                    c.step(eng.tensor_tensor(part, part, k.ps[:, b, 0:n].rearrange("p (w d) -> p w d", d=D), ALU.add))
                    eng.tensor_tensor(x, x, part, ALU.add).then_inc(s_x, 1)

            @block.sync
            def _(eng):
                eng.wait_ge(s_x, NB)
                eng.dma_start(out[0:(NW - 1) * P, :].rearrange("(w p) d -> p w d", p=P), k.x[:, 0:NW - 1, :]).then_inc(s_out, 16)
                eng.dma_start(out[(NW - 1) * P:N, :], k.x[0:TAIL, NW - 1, :]).then_inc(s_out, 16)
                eng.wait_ge(s_out, 32)


def build(nc, a, out):
    with ExitStack() as ctx:
        k = Program(nc, ctx)
        constants(k)
        k.psf = k.ps[:, :, :].rearrange("p b c -> p (b c)")
        route(k, a)
        load_x(k, a["x"])
        normalise(k)
        layer0(k, a)
        normalise(k)
        layer1(k, a)
        normalise(k)
        layer2(k, a)
        normalise(k)
        layer3(k, a, out)


def kernel(**inputs):
    import concourse.bacc as bacc
    from concourse.bass_utils import run_bass_kernel_spmd as run
    nc = bacc.Bacc("TRN2", target_bir_lowering=False, num_devices=1)
    v = {n: np.asarray(x) for n, x in inputs.items()}
    laid = {n: v[n] for n in ("x", "src", "dst", "edge_attr_4", "edge_type_16", "edge_weight", "L3_gnn_self_loop")}
    laid.update({n: v[n] for n in v if n.startswith("L0_")})
    laid["L0_gnn_upd_b1"] = v["L0_gnn_upd_b1"].reshape(D, 1)
    laid["L0_gnn_att_W2"] = v["L0_gnn_att_W2"].reshape(D)
    laid["L1_W1T"], laid["L1_W2T"] = v["L1_gnn_W1"].T, v["L1_gnn_W2"].T
    laid["L2_We"] = v["L2_gnn_W_edge"].transpose(2, 0, 1).reshape(D, T4 * D)
    laid["L2_be"] = v["L2_gnn_b_edge"].reshape(T4 * D)
    for l, ih, hh in (("L1_", "L1_gnn_w_ih", "L1_gnn_w_hh"), ("L2_", "L2_gnn_W_ih", "L2_gnn_W_hh")):
        laid[l + "ih"], laid[l + "hh"] = v[ih].T, v[hh].T
        for b in ("b_ih", "b_hh"):
            laid[l + b] = v[l + "gnn_" + b].reshape(3, D).T
    laid["L3_bases"] = v["L3_gnn_bases"].transpose(1, 0, 2)
    laid["L3_gnn_coefficients"] = v["L3_gnn_coefficients"].reshape(-1)
    arrays, aps = {}, {}
    for n, x in laid.items():
        x = np.ascontiguousarray(x)
        arrays[n + "_dram"] = x
        aps[n] = nc.dram_tensor(n + "_dram", x.shape, mybir.dt.from_np(x.dtype), kind="ExternalInput").ap()
    out = nc.dram_tensor("out_dram", (N, D), F32, kind="ExternalOutput").ap()
    build(nc, aps, out)
    r = run(nc, [arrays], core_ids=[0])
    return r.results[0]["out_dram"]
```

```python
import numpy as np
import concourse.bass as bass
from concourse import mybir
from concourse.alu_op_type import AluOpType as ALU
from contextlib import ExitStack

F32, I32, BF16 = mybir.dt.float32, mybir.dt.int32, mybir.dt.bfloat16
ACT = mybir.ActivationFunctionType
AX = mybir.AxisListType

P = 128
N = 3125
E = 100000
D = 128
NW = -(-N // P)
NP = NW * P
TAIL = N - (NW - 1) * P
EP = 125
EC = E // EP
QUAD = 4
NQ = 4
NQ0 = 6
ROUND = 48
NT = -(-((E + NW * (P - 1)) // P) // ROUND) * ROUND
NQUADS = -(-((E + NW * (P - 1)) // P) // QUAD)
NTP = NT + QUAD * NQ0
T4, T16 = 4, 16
BANK = 512
NB = -(-NP // BANK)
COL = NP
D_LOC, D_W, D_SRC, D_T4, D_T16, D_WORDS = 0, 1, 2, 3, 4, 8
SUMS = 2 * QUAD
SUM_C = D + 1
SUM_ROWS = NP + P
SC = 16
LT = -(-E // P)
COPIES = 16
DVE_TILES, ACT_TILES = (NT * share // 100 // COPIES * COPIES for share in (31, 40))


class Count:

    def __init__(self, eng, sem, start=0):
        self.eng, self.sem, self.n = eng, sem, start

    def step(self, ins):
        self.n = self.n + 1
        ins.then_inc(self.sem, 1)
        self.eng.wait_ge(self.sem, self.n)


class Program:
    def __init__(self, nc, ctx):
        self.nc, self.ctx = nc, ctx
        self.sems, self.used = {}, {}

    def sb(self, name, shape, dt=F32, ctx=None):
        self.used[name] = self.used.get(name, 0) + 1
        unique = name if self.used[name] == 1 else f"{name}_{self.used[name]}"
        return (ctx or self.ctx).enter_context(self.nc.sbuf_tensor(unique, shape, dt))

    def sem(self, name):
        if name not in self.sems:
            self.sems[name] = self.ctx.enter_context(self.nc.semaphore(name))
        return self.sems[name]

    def flag(self, eng):
        return eng.value_load(self.in_order[0:1, 0:1], min_val=0, max_val=1)

    def uid(self):
        self.used["uid"] = self.used.get("uid", 0) + 1
        return self.used["uid"]

    def end_phase(self):
        numbers = [s.num for s in self.sems.values()]
        every = range(min(numbers), max(numbers) + 1)
        self.nc.gpsimd.dma_reset(every)
        self.nc.all_engine_barrier()
        self.nc.sync.sem_clear(every)
        self.nc.all_engine_barrier()


def constants(k):
    nc = k.nc
    k.ident = k.sb("ident", [P, P])
    k.before = k.sb("before", [P, P])
    k.upto = k.sb("upto", [P, P])
    k.ones = k.sb("ones", [P, BANK])
    k.zeros = k.sb("zeros", [P, BANK])
    k.head = k.sb("head", [P, P])
    k.lane = k.sb("lane", [P, 1])
    k.tile_no = k.sb("tile_no", [P, NT])
    k.ps = k.ctx.enter_context(nc.psum_tensor("ps", [P, 8, BANK], F32))
    s_set, s_sel = k.sem("s_set"), k.sem("s_sel")
    with nc.Block() as block:
        @block.gpsimd
        def _(eng):
            eng.memset(k.ident[:, :], 0.0).then_inc(s_set, 1)
            eng.memset(k.before[:, :], 1.0).then_inc(s_set, 1)
            eng.memset(k.upto[:, :], 1.0).then_inc(s_set, 1)
            eng.memset(k.head[:, :], 1.0).then_inc(s_set, 1)
            eng.memset(k.ones[:, :], 1.0).then_inc(s_set, 1)
            eng.memset(k.zeros[:, :], 0.0).then_inc(s_set, 1)
            eng.iota(k.tile_no[:, :], [[1, NT]], 0, 0, allow_small_or_imprecise_dtypes=True).then_inc(s_set, 1)
            eng.iota(k.lane[:, :], [[0, 1]], 0, 1, allow_small_or_imprecise_dtypes=True).then_inc(s_set, 1)
            eng.wait_ge(s_set, 8)
            eng.affine_select(out=k.ident[:, :], in_=k.ident[:, :], compare_op=ALU.not_equal, fill=1.0,
                              base=0, pattern=[[-1, P]], channel_multiplier=1).then_inc(s_sel, 1)
            eng.affine_select(out=k.before[:, :], in_=k.before[:, :], compare_op=ALU.is_ge, fill=0.0,
                              base=-1, pattern=[[1, P]], channel_multiplier=-1).then_inc(s_sel, 1)
            eng.affine_select(out=k.upto[:, :], in_=k.upto[:, :], compare_op=ALU.is_ge, fill=0.0,
                              base=0, pattern=[[1, P]], channel_multiplier=-1).then_inc(s_sel, 1)
            eng.affine_select(out=k.head[:, :], in_=k.head[:, :], compare_op=ALU.is_ge, fill=0.0,
                              base=NW - 2, pattern=[[0, P]], channel_multiplier=-1).then_inc(s_sel, 1)
            eng.wait_ge(s_sel, 4)
    k.end_phase()


def route(k, a):
    nc = k.nc
    k.x, k.h, k.hT = k.sb("x", [P, NW, D]), k.sb("h", [P, NW, D]), k.sb("hT", [P, NP])
    k.by_dst = k.sb("by_dst", [P, NTP, D_WORDS])
    k.where = k.sb("where", [1, NTP // QUAD, 2 * QUAD], I32)
    k.loc_rows = nc.dram_tensor("loc_rows", [NB * P, P], BF16, kind="Internal").ap()
    k.first_node = k.sb("first_node", [P, NT])
    k.in_order = k.sb("in_order", [1, 1], I32)
    k.src_rows = nc.dram_tensor("src_rows", [NB * P, P], F32, kind="Internal").ap()
    k.sums = [nc.dram_tensor(f"sums_{c}", [SUM_ROWS, SUM_C], F32, kind="Internal").ap() for c in range(SUMS)]
    routed = nc.dram_tensor("routed", [P * NT, D_WORDS], F32, kind="Internal").ap()
    own = ExitStack()
    with own:
        sb = lambda name, shape, dt=F32: k.sb(name, shape, dt, own)
        pay = sb("pay", [EP, EC, D_WORDS])
        win_i = sb("win_i", [EP, EC], I32)
        win = sb("win", [EP, EC])
        eq, cum, part = sb("eq", [EP, EC]), sb("cum", [EP, EC]), sb("part", [EP, EC])
        unit = sb("unit", [EP, EC])
        place = sb("place", [EP, EC])
        dest = sb("dest", [EP, EC], I32)
        total = sb("total", [P, P])
        tiles_i = sb("tiles_i", [P, NW], I32)
        tiles = sb("tiles", [P, NW])
        ends = sb("ends", [P, NW])
        base = sb("base", [P, NW])
        col = sb("col", [P, 1])
        past = sb("past", [P, NT])
        stage_i = sb("stage_i", [EP, 2, SC], I32)
        falls = sb("falls", [P, 1])
        flag = sb("flag", [P, 1])
        last_i, first_i = sb("last_i", [P, NW], I32), sb("first_i", [P, NW], I32)
        spans, steps, twice = sb("spans", [P, NW]), sb("steps", [P, NW]), sb("twice", [P, NW])
        shared = sb("shared", [P, 1])
        shared_head, shift = sb("shared_head", [P, P]), sb("shift", [1, NT])
        tile_of = sb("tile_of", [1, NT], I32)
        tail = sb("tail", [(LT * P + P - E) // 2, 2, D_WORDS])
        listed = nc.dram_tensor("listed", [(LT + 1) * P, D_WORDS], F32, kind="Internal").ap()
        stage_w = sb("stage_w", [EP, 2, SC, D_WORDS])
        nothing = sb("nothing", [P, SUM_ROWS // P * SUM_C])
        early = own.enter_context(ExitStack())
        raw = {s: k.sb(f"raw_{s}", [EP, EC], I32, early) for s in ("src", "dst", "rel")}
        weight = k.sb("weight", [EP, EC], F32, early)
        after = k.sb("after", [EP, EC], I32, early)
        attr = k.sb("attr", [EP, EC, T4], F32, early)
        top = k.sb("top", [EP, EC], F32, early)
        differs = k.sb("differs", [EP, 3, EC], F32, early)
        f_rel = k.sb("f_rel", [EP, EC], F32, early)
        ps = k.ps
        PREF, CNT, END, WIN = 0, 1, 3, 4
        NCH = EC // (2 * SC)

        names = ("s_load", "s_pad", "s_dve", "s_tot", "s_sums", "s_col", "s_end", "s_past", "s_win", "s_pay", "s_store")
        s_load, s_pad, s_dve, s_tot, s_sums, s_col, s_end, s_past, s_win, s_pay, s_store = (k.sem(x) for x in names)
        SHIFT = 6
        s_dest, s_staged, s_go, s_zero = (k.sem(x) for x in ("s_dest", "s_staged", "s_go", "s_zero"))
        s_sc = [k.sem(f"s_sc_{h}") for h in range(2)]

        def window_totals(eng, c):
            c.step(eng.tensor_scalar(win_i[:, :], raw["dst"][:, :], 7, None, ALU.arith_shift_right))
            c.step(eng.tensor_copy(win[:, :], win_i[:, :]))
            start = c.n
            with eng.Fori(0, NW) as w:
                c.n = w + start
                c.step(eng.tensor_scalar(eq[:, :], win[:, :], k.tile_no[0:EP, bass.ds(w, 1)], 0.0, ALU.is_equal,
                                         ALU.add, accum_out=total[0:EP, bass.ds(w, 1)]))
            c.n = start + NW

        def window_starts(eng, c):
            eng.sem_inc(s_tot, 1)
            eng.wait_ge(s_sums, 1)
            c.step(eng.tensor_scalar(flag[:, :], ps[:, CNT, NW:NW + 1], 0.0, None, ALU.is_equal))
            c.step(eng.tensor_scalar(tiles_i[:, :], ps[:, CNT, 0:NW], float(P - 1), None, ALU.add))
            c.step(eng.tensor_scalar(tiles_i[:, :], tiles_i[:, :], 7, None, ALU.arith_shift_right))
            c.step(eng.tensor_copy(tiles[:, :], tiles_i[:, :]))
            c.step(eng.tensor_tensor_scan(ends[:, :], k.ones[:, 0:NW], ps[:, CNT, 0:NW], 0.0, ALU.mult, ALU.add))
            c.step(eng.tensor_scalar(last_i[:, :], ends[:, :], float(P - 1), None, ALU.add))
            c.step(eng.tensor_scalar(last_i[:, :], last_i[:, :], 7, None, ALU.arith_shift_right))
            c.step(eng.tensor_copy(spans[:, :], last_i[:, :]))
            c.step(eng.tensor_copy(last_i[:, :], ends[:, :]))
            c.step(eng.tensor_scalar(last_i[:, :], last_i[:, :], 7, None, ALU.arith_shift_right))
            c.step(eng.tensor_copy(steps[:, :], last_i[:, :]))
            c.step(eng.tensor_tensor(first_i[:, :], ends[:, :], ps[:, CNT, 0:NW], ALU.subtract))
            c.step(eng.tensor_scalar(first_i[:, :], first_i[:, :], 7, None, ALU.arith_shift_right))
            c.step(eng.tensor_copy(twice[:, :], first_i[:, :]))
            c.step(eng.tensor_tensor(spans[:, :], spans[:, :], twice[:, :], ALU.subtract))
            c.step(eng.tensor_tensor(steps[:, :], steps[:, :], twice[:, :], ALU.subtract))
            c.step(eng.tensor_scalar(twice[:, :], ps[:, CNT, 0:NW], 0.0, None, ALU.is_gt))
            c.step(eng.tensor_tensor(spans[:, :], spans[:, :], twice[:, :], ALU.mult))
            c.step(eng.tensor_tensor(twice[:, :], spans[:, :], steps[:, :], ALU.subtract))
            c.step(eng.tensor_tensor(spans[:, :], spans[:, :], tiles[:, :], ALU.subtract))
            c.step(eng.scalar_tensor_tensor(tiles[:, :], spans[:, :], flag[:, 0:1], tiles[:, :], ALU.mult, ALU.add))
            c.step(eng.tensor_tensor_scan(ends[:, :], k.ones[:, 0:NW], tiles[:, :], 0.0, ALU.mult, ALU.add))
            c.step(eng.tensor_tensor(ends[:, :], ends[:, :], tiles[:, :], ALU.subtract))
            c.step(eng.scalar_tensor_tensor(base[:, :], ends[:, :], float(P), ps[:, PREF, 0:NW], ALU.mult, ALU.add))
            c.step(eng.tensor_tensor(tiles[:, :], tiles[:, :], k.ident[:, 0:NW], ALU.mult))
            c.step(eng.tensor_reduce(col[:, :], tiles[:, :], AX.X, ALU.add))
            c.step(eng.tensor_tensor(twice[:, :], twice[:, :], k.ident[:, 0:NW], ALU.mult))
            c.step(eng.tensor_reduce(shared[:, :], twice[:, :], AX.X, ALU.add))
            c.step(eng.tensor_scalar(shared_head[:, :], k.head[:, :], shared[:, 0:1], None, ALU.mult))
            eng.sem_inc(s_col, 1)
            eng.wait_ge(s_end, 1)
            c.step(eng.tensor_copy(col[:, :], ps[:, END, 0:1]))
            c.step(eng.tensor_scalar(past[:, :], k.tile_no[:, :], col[:, 0:1], None, ALU.is_ge))
            eng.sem_inc(s_past, 1)
            c.step(eng.memset(k.where[0:1, :, :], 0))
            eng.wait_ge(s_win, 1)
            for h in range(2):
                w = ps[0:1, WIN + h, 0:NT // 2].rearrange("p (g j) -> p g j", j=QUAD)
                to = k.where[0:1, h * NT // 2 // QUAD:(h + 1) * NT // 2 // QUAD, :]
                c.step(eng.tensor_scalar(to[:, :, 0:QUAD], w, float(P), None, ALU.mult))
                c.step(eng.tensor_scalar(to[:, :, QUAD:2 * QUAD], w, float(COL), None, ALU.add))
                c.step(eng.tensor_scalar(k.first_node[:, h * NT // 2:(h + 1) * NT // 2], ps[:, WIN + h, 0:NT // 2],
                                         float(P), None, ALU.mult))

        def count_on_pe(eng):
            eng.wait_ge(s_tot, 1)
            eng.matmul(ps[:, PREF, 0:NW], k.before[:, :], total[:, 0:NW], start=True, stop=True)
            eng.matmul(ps[:, CNT, NW:NW + 1], k.ones[:, 0:P], falls[:, 0:1], start=True, stop=True)
            eng.matmul(ps[:, CNT, 0:NW], k.ones[:, 0:P], total[:, 0:NW], start=True, stop=True).then_inc(s_sums, 1)
            eng.wait_ge(s_col, 1)
            eng.matmul(ps[:, END, 0:1], k.upto[:, :], col[:, 0:1], start=True, stop=True).then_inc(s_end, 1)
            eng.wait_ge(s_past, 1)
            for to, of in ((WIN, k.head), (SHIFT, shared_head)):
                for h in range(2):
                    last = eng.matmul(ps[:, to + h, 0:NT // 2], of[:, :], past[:, h * NT // 2:(h + 1) * NT // 2],
                                      start=True, stop=True)
            last.then_inc(s_win, 1)

        def places(eng, c):
            c.step(eng.memset(place[:, :], -1.0))
            start = c.n
            with eng.Fori(0, NW) as w:
                c.n = w * 4 + start
                c.step(eng.tensor_scalar(eq[:, :], win[:, :], k.tile_no[0:EP, bass.ds(w, 1)], None, ALU.is_equal))
                c.step(eng.tensor_tensor_scan(cum[:, :], unit[:, :], eq[:, :], base[0:EP, bass.ds(w, 1)],
                                              ALU.mult, ALU.add))
                c.step(eng.tensor_tensor(part[:, :], cum[:, :], eq[:, :], ALU.mult))
                c.step(eng.tensor_tensor(place[:, :], place[:, :], part[:, :], ALU.add))
            c.n = start + 4 * NW
            c.step(eng.tensor_copy(dest[:, :], place[:, :]))
            c.step(eng.tensor_scalar(win_i[:, :], dest[:, :], 7, None, ALU.arith_shift_right))
            c.step(eng.tensor_scalar(dest[:, :], dest[:, :], P - 1, None, ALU.bitwise_and))
            c.step(eng.tensor_copy(eq[:, :], win_i[:, :]))
            c.step(eng.tensor_copy(cum[:, :], dest[:, :]))
            c.step(eng.scalar_tensor_tensor(dest[:, :], cum[:, :], float(NT), eq[:, :], ALU.mult, ALU.add))

        with nc.Block() as block:
            @block.sync
            def _(eng):
                eng.wait_ge(s_pad, 1)
                for dst, src in ((raw["dst"], a["dst"]), (raw["src"], a["src"]), (raw["rel"], a["edge_type_16"]),
                                 (weight, a["edge_weight"])):
                    eng.dma_start(dst[:, :], src.rearrange("(p c) -> p c", p=EP)).then_inc(s_load, 16)
                eng.dma_start(after[0:EP - 1, :], a["dst"][1:1 + (EP - 1) * EC].rearrange("(p c) -> p c", c=EC)).then_inc(s_load, 16)
                eng.dma_start(after[EP - 1:EP, 0:EC - 1], a["dst"][E - EC + 1:E].rearrange("(p c) -> p c", p=1)).then_inc(s_load, 16)
                eng.dma_start(attr[:, :, :], a["edge_attr_4"].rearrange("(p c) t -> p c t", p=EP)).then_inc(s_load, 16)
                x = a["x"]
                eng.dma_start(k.x[:, 0:NW - 1, :], x[0:(NW - 1) * P, :].rearrange("(w p) d -> p w d", p=P)).then_inc(s_store, 16)
                eng.wait_ge(s_pad, 7)
                eng.dma_start(k.x[0:TAIL, NW - 1, :], x[(NW - 1) * P:N, :]).then_inc(s_store, 16)
                eng.dma_start(routed.rearrange("(p t) c -> p t c", p=P), k.by_dst[:, 0:NT, :]).then_inc(s_store, 16)
                eng.dma_start(listed[E:(LT + 1) * P, :].rearrange("(p r) c -> p r c", r=2), tail[:, :, :]).then_inc(s_store, 16)
                eng.wait_ge(s_pay, 1)
                eng.dma_start(listed[0:E, :].rearrange("(p c) w -> p c w", p=EP), pay[:, :, :]).then_inc(s_store, 16)
                eng.wait_ge(s_store, 80)

            @block.gpsimd
            def _(eng):
                eng.memset(after[:, :], N).then_inc(s_pad, 1)
                eng.memset(k.by_dst[:, :, 0:1], -1.0).then_inc(s_pad, 1)
                eng.memset(k.by_dst[:, :, 1:D_WORDS], 0.0).then_inc(s_pad, 1)
                eng.memset(total[:, :], 0.0).then_inc(s_pad, 1)
                eng.memset(tail[:, :, 0:1], -1.0).then_inc(s_pad, 1)
                eng.memset(tail[:, :, 1:D_WORDS], 0.0).then_inc(s_pad, 1)
                eng.memset(k.x[:, NW - 1, :], 0.0).then_inc(s_pad, 1)
                eng.memset(nothing[:, :], 0.0)

            @block.vector
            def _(eng):
                c = Count(eng, s_dve)
                eng.wait_ge(s_load, 112)
                eng.wait_ge(s_pad, 6)
                c.step(eng.memset(unit[:, :], 1.0))
                c.step(eng.memset(pay[:, :, :], 0.0))
                c.step(eng.tensor_copy(pay[:, :, D_SRC], raw["src"][:, :]))
                c.step(eng.tensor_copy(pay[:, :, D_LOC], raw["dst"][:, :]))
                c.step(eng.tensor_copy(f_rel[:, :], raw["rel"][:, :]))
                c.step(eng.tensor_copy(pay[:, :, D_W], weight[:, :]))
                f_src = pay[:, :, D_SRC]
                c.step(eng.scalar_tensor_tensor(pay[:, :, D_T16], f_rel[:, :], float(NP), f_src, ALU.mult, ALU.add))
                c.step(eng.tensor_reduce(top[:, :], attr[:, :, :], AX.X, ALU.max))
                for j in range(3):
                    c.step(eng.tensor_tensor(differs[:, j, :], attr[:, :, j], top[:, :], ALU.not_equal))
                for j in (1, 0):
                    c.step(eng.scalar_tensor_tensor(differs[:, j, :], differs[:, j + 1, :], 1.0, differs[:, j, :],
                                                    ALU.add, ALU.mult))
                c.step(eng.scalar_tensor_tensor(pay[:, :, D_T4], differs[:, 0, :], float(NP), f_src, ALU.mult, ALU.add))
                eng.sem_inc(s_pay, 1)
                window_totals(eng, c)
                c.step(eng.memset(falls[:, :], 0.0))
                c.step(eng.tensor_scalar(after[:, :], after[:, :], 7, None, ALU.arith_shift_right))
                c.step(eng.tensor_tensor(eq[:, :], after[:, :], win[:, :], ALU.is_lt))
                c.step(eng.tensor_reduce(falls[0:EP, :], eq[:, :], AX.X, ALU.add))
                window_starts(eng, c)
                for h in range(2):
                    half = slice(h * NT // 2, (h + 1) * NT // 2)
                    c.step(eng.tensor_tensor(shift[0:1, half], k.tile_no[0:1, half], ps[0:1, SHIFT + h, 0:NT // 2], ALU.subtract))
                    c.step(eng.tensor_scalar(tile_of[0:1, half], shift[0:1, half], float(LT), None, ALU.min))
                c.step(eng.tensor_scalar(k.in_order[0:1, 0:1], ps[0:1, CNT, NW:NW + 1], 0.0, None, ALU.is_equal))

            @block.tensor
            def _(eng):
                count_on_pe(eng)
        k.end_phase()

        early.close()

        norm_vector, norm_scalar, norm_tensor = normalise(k, own)
        by_tile = sb("by_tile", [P, LT + 1, D_WORDS])
        s_place, s_raw = k.sem("s_place"), k.sem("s_raw")
        with nc.Block() as block:
            def copy_tiles(eng, first, last):
                eng.wait_ge(s_raw, 16)
                regs = [eng.alloc_register(f"tile_{k.uid()}") for _ in range(COPIES)]
                with eng.Fori(first // COPIES, last // COPIES) as i:
                    eng.load(regs, tile_of[0:1, bass.ds(i * COPIES, COPIES)])
                    for j, r in enumerate(regs):
                        tile = eng.snap(r, min_val=0, max_val=LT)
                        to, of = k.by_dst[:, bass.ds(i * COPIES + j, 1), :], by_tile[:, bass.ds(tile, 1), :]
                        if eng is nc.scalar:
                            eng.activation(to, of, ACT.Copy)
                        else:
                            eng.tensor_copy(to, of)

            @block.sync
            def _(eng):
                ordered = k.flag(eng)
                with eng.If(ordered > 0):
                    eng.dma_start(by_tile[:, :, :], listed.rearrange("(t p) c -> p t c", p=P)).then_inc(s_raw, 16)
                    eng.wait_ge(s_raw, 16)

            @block.gpsimd
            def _(eng):
                ordered = k.flag(eng)
                with eng.If(ordered < 1):
                    with eng.Fori(0, NCH) as i:
                        for h in range(2):
                            eng.wait_ge(s_staged, i * 4 + 2 * (h + 1))
                            eng.sem_inc(s_go, 1)
                            for j in range(SC):
                                eng.indirect_dma_start(routed, bass.IndirectOffsetOnAxis(stage_i[:, h, j:j + 1], 0),
                                                       stage_w[:, h, j, :], None).then_inc(s_sc[h], 16)
                    for h in range(2):
                        eng.wait_ge(s_sc[h], NCH * 16 * SC)
                with eng.If(ordered > 0):
                    copy_tiles(eng, DVE_TILES + ACT_TILES, NT)

            @block.scalar
            def _(eng):
                ordered = k.flag(eng)
                for sums in k.sums:
                    eng.dma_start(sums.rearrange("(p r) c -> p (r c)", p=P), nothing[:, :]).then_inc(s_zero, 16)

                def stage(chunk, h):
                    at = chunk * SC
                    eng.activation(stage_i[:, h, :], dest[:, bass.ds(at, SC)], ACT.Copy).then_inc(s_staged, 1)
                    eng.activation(stage_w[:, h, :, :], pay[:, bass.ds(at, SC), :], ACT.Copy).then_inc(s_staged, 1)
                with eng.If(ordered < 1):
                    eng.wait_ge(s_dest, 1)
                    for h in range(2):
                        stage(h, h)
                    with eng.Fori(1, NCH) as i:
                        for h in range(2):
                            eng.wait_ge(s_sc[h], i * (16 * SC))
                            stage(i * 2 + h, h)
                norm_scalar(eng)
                with eng.If(ordered > 0):
                    copy_tiles(eng, DVE_TILES, DVE_TILES + ACT_TILES)
                eng.wait_ge(s_zero, 16 * SUMS)

            @block.vector
            def _(eng):
                ordered = k.flag(eng)
                with eng.If(ordered < 1):
                    places(eng, Count(eng, s_place))
                    eng.sem_inc(s_dest, 1)
                norm_vector(eng)
                with eng.If(ordered > 0):
                    copy_tiles(eng, 0, DVE_TILES)

            @block.tensor
            def _(eng):
                norm_tensor(eng)
        k.end_phase()

    own = ExitStack()
    with own:
        loc_t, src_t = k.sb("loc_t", [P, NB, P], BF16, own), k.sb("src_t", [P, NB, P], F32, own)
        loc_c, src_c = k.sb("loc_c", [P, NB * P], F32, own), k.sb("src_c", [P, NB * P], F32, own)
        inside, below = k.sb("inside", [P, NT], F32, own), k.sb("below", [P, NT], F32, own)
        names = ("s_list", "s_here", "s_cmp", "s_tr", "s_ev", "s_row", "s_dve")
        s_list, s_here, s_cmp, s_tr, s_ev, s_row, s_dve = (k.sem(x) for x in names)
        with nc.Block() as block:
            @block.sync
            def _(eng):
                ordered = k.flag(eng)
                with eng.If(ordered < 1):
                    eng.dma_start(k.by_dst[:, 0:NT, :], routed.rearrange("(p t) c -> p t c", p=P)).then_inc(s_list, 16)
                    eng.wait_ge(s_list, 16)
                eng.sem_inc(s_here, 1)
                eng.wait_ge(s_ev, 2 * NB)
                eng.dma_start(k.loc_rows.rearrange("(b p) e -> p b e", p=P), loc_t[:, :, :]).then_inc(s_row, 16)
                eng.dma_start(k.src_rows.rearrange("(b p) e -> p b e", p=P), src_t[:, :, :]).then_inc(s_row, 16)
                eng.wait_ge(s_row, 32)

            @block.vector
            def _(eng):
                c = Count(eng, s_dve)
                c.step(eng.memset(loc_c[:, :], -1.0))
                c.step(eng.memset(src_c[:, :], 0.0))
                eng.wait_ge(s_here, 1)
                loc = k.by_dst[:, 0:NT, D_LOC]
                c.step(eng.tensor_tensor(loc, loc, k.first_node[:, :], ALU.subtract))
                eng.tensor_copy(loc_c[:, 0:NT], loc).then_inc(s_cmp, 1)
                eng.tensor_copy(src_c[:, 0:NT], k.by_dst[:, 0:NT, D_SRC]).then_inc(s_cmp, 1)
                c.step(eng.tensor_scalar(inside[:, :], loc, 0.0, None, ALU.is_ge))
                c.step(eng.tensor_scalar(below[:, :], loc, float(P), None, ALU.is_lt))
                c.step(eng.tensor_tensor(inside[:, :], inside[:, :], below[:, :], ALU.mult))
                w = k.by_dst[:, 0:NT, D_W]
                c.step(eng.tensor_tensor(w, w, inside[:, :], ALU.mult))
                for b in range(NB):
                    eng.wait_ge(s_tr, b + 1)
                    eng.tensor_copy(loc_t[:, b, :], k.ps[:, b, 0:P]).then_inc(s_ev, 1)
                    eng.tensor_copy(src_t[:, b, :], k.ps[:, b, P:2 * P]).then_inc(s_ev, 1)

            @block.tensor
            def _(eng):
                eng.wait_ge(s_cmp, 2)
                for b in range(NB):
                    eng.transpose(k.ps[:, b, 0:P], loc_c[:, b * P:(b + 1) * P], k.ident[:, :])
                    eng.transpose(k.ps[:, b, P:2 * P], src_c[:, b * P:(b + 1) * P], k.ident[:, :]).then_inc(s_tr, 1)
        k.end_phase()


class Where:

    def __init__(self, k, eng, table):
        self.k, self.eng, self.table = k, eng, table
        self.regs = [eng.alloc_register(f"where_{k.uid()}") for _ in range(2 * QUAD)]

    def load(self, quad):
        self.eng.load(self.regs, self.table[0:1, bass.ds(quad, 1), :].rearrange("p g j -> p (g j)"))
        col = [self.eng.snap(r, min_val=0, max_val=(NW - 1) * P) for r in self.regs[:QUAD]]
        scalar = [self.eng.snap(r, min_val=COL, max_val=COL + NW - 1) for r in self.regs[QUAD:]]
        return col, scalar


def banks():
    for b in range(NB):
        n = min(BANK, NP - b * BANK)
        yield b, b * BANK, n, b * BANK // P, n // P


def load_all(k, pairs, name):
    s = k.sem("s_load")
    with k.nc.Block() as block:
        @block.sync
        def _(eng):
            for dst, src in pairs:
                eng.dma_start(dst, src).then_inc(s, 16)
            eng.wait_ge(s, 16 * len(pairs))
    k.end_phase()


def normalise(k, parts=None):
    nc = k.nc
    own = ExitStack()
    with own:
        sq = k.sb("sq", [P, NW, D], F32, parts or own)
        stat = k.sb("stat", [P, NW], F32, parts or own)
        s_norm, s_var, s_std, s_h, s_tr, s_ev = (k.sem(x) for x in ("s_norm", "s_var", "s_std", "s_h", "s_tr", "s_ev"))
        wide = lambda t: t[:, :].unsqueeze(2).to_broadcast([P, NW, D])

        def vector(eng):
            c = Count(eng, s_norm)
            c.step(eng.tensor_reduce(stat[:, :], k.x[:, :, :], AX.X, ALU.add))
            c.step(eng.tensor_scalar(stat[:, :], stat[:, :], 1.0 / D, None, ALU.mult))
            c.step(eng.tensor_tensor(k.h[:, :, :], k.x[:, :, :], wide(stat), ALU.subtract))
            c.step(eng.tensor_tensor(sq[:, :, :], k.h[:, :, :], k.h[:, :, :], ALU.mult))
            c.step(eng.tensor_reduce(stat[:, :], sq[:, :, :], AX.X, ALU.add))
            eng.tensor_scalar(stat[:, :], stat[:, :], 1.0 / D, 1e-5, ALU.mult, ALU.add).then_inc(s_var, 1)
            eng.wait_ge(s_std, 1)
            c.step(eng.reciprocal(stat[:, :], stat[:, :]))
            for b, _, _, w0, wn in banks():
                part = k.h[:, w0:w0 + wn, :]
                c.step(eng.tensor_tensor(part, part, stat[:, w0:w0 + wn].unsqueeze(2).to_broadcast([P, wn, D]), ALU.mult))
                eng.tensor_scalar(part, part, 0.0, None, ALU.max).then_inc(s_h, 1)

        def scalar(eng):
            eng.wait_ge(s_var, 1)
            eng.activation(stat[:, :], stat[:, :], ACT.Sqrt).then_inc(s_std, 1)
            evacuate(k, eng, s_tr, s_ev, k.hT)

        def tensor(eng):
            turn(k, eng, k.h, s_h, s_tr)

        if parts:
            return vector, scalar, tensor
        with nc.Block() as block:
            block.vector(vector)
            block.scalar(scalar)
            block.tensor(tensor)
        k.end_phase()


def turn(k, eng, rows, s_ready, s_done, s_free=None):
    for b, _, n, w0, wn in banks():
        eng.wait_ge(s_ready, b + 1)
        if s_free:
            eng.wait_ge(s_free, b + 1)
        for j in range(wn):
            last = eng.transpose(k.ps[:, b, j * P:(j + 1) * P], rows[:, w0 + j, :], k.ident[:, :])
        last.then_inc(s_done, 1)


def evacuate(k, eng, s_full, s_done, cols):
    for b, c0, n, _, _ in banks():
        eng.wait_ge(s_full, b + 1)
        eng.activation(cols[:, c0:c0 + n], k.ps[:, b, 0:n], ACT.Copy).then_inc(s_done, 1)


def table(k, own, weights, width, dram_rows, bias=None, keep=None, shared=None):
    nc = k.nc
    out_n = shared or width
    nb = -(-width // BANK)
    G = 5 if nb == 1 else 1
    st = k.sb("rows", [P, 2, G, out_n], F32, own)
    s_mm, s_row, s_keep = (k.sem(x) for x in ("s_mm", "s_row", "s_keep"))
    s_st = [k.sem(f"s_st{j}") for j in range(2)]
    half = 8 // nb
    cut = out_n if nb == 1 else BANK

    parts = len(dram_rows(0, G, st[:, 0, :, :]))

    with nc.Block() as block:
        @block.tensor
        def _(eng):
            for w in range(NW):
                if w >= half:
                    eng.wait_ge(s_row, (w - half + 1) * nb)
                    if keep is not None:
                        eng.wait_ge(s_keep, w - half + 1)
                for j in range(nb):
                    eng.matmul(k.ps[:, (w % half) * nb + j, :], k.hT[:, w * P:(w + 1) * P],
                               weights[:, j * BANK:(j + 1) * BANK], start=True, stop=True).then_inc(s_mm, 1)

        def rows(eng, w, j):
            g = w // G
            eng.wait_ge(s_mm, w * nb + j + 1)
            if g >= 2:
                eng.wait_ge(s_st[g % 2], 16 * parts * (g // 2))
            dst = st[:, g % 2, w % G, j * BANK:j * BANK + cut]
            src = k.ps[:, (w % half) * nb + j, 0:cut]
            return dst, src

        @block.scalar
        def _(eng):
            if bias is not None and keep is None:
                return
            for w in range(NW):
                for j in range(nb):
                    dst, src = rows(eng, w, j)
                    eng.activation(dst, src, ACT.Copy).then_inc(s_row, 1)

        @block.vector
        def _(eng):
            if keep is not None:
                for w in range(NW):
                    eng.wait_ge(s_row, w + 1)
                    eng.tensor_tensor(keep[:, w, :], k.ps[:, w % 8, shared:width], bias[:, :], ALU.add).then_inc(s_keep, 1)
            elif bias is not None:
                for w in range(NW):
                    for j in range(nb):
                        dst, src = rows(eng, w, j)
                        eng.tensor_tensor(dst, src, bias[:, j * BANK:(j + 1) * BANK], ALU.add).then_inc(s_row, 1)

        @block.sync
        def _(eng):
            for g in range(NW // G):
                eng.wait_ge(s_row, (g + 1) * G * nb)
                for dst, src in dram_rows(g * G, G, st[:, g % 2, :, :]):
                    eng.dma_start(dst, src).then_inc(s_st[g % 2], 16)
            for j in range(2):
                eng.wait_ge(s_st[j], 16 * parts * len(range(j, NW // G, 2)))
    k.end_phase()


def edge_pass(k, own, rows, words, loc, idx, where, weight=None, column=None, flipped=False):
    nc = k.nc
    body = QUAD * NQ
    bodies, rest = divmod(NQUADS, NQ)
    ring = k.sb("ring", [P, NQ * QUAD, D], F32, own)
    mark = k.sb("mark", [P, NQ, QUAD, P], F32, own)
    stage = k.sb("stage", [P, NQ * QUAD], I32, own)
    s_full = [k.sem(f"s_full{q}") for q in range(NQ)]
    s_staged, s_mark, s_done, s_go = (k.sem(x) for x in ("s_staged", "s_mark", "s_done", "s_go"))
    index = lambda t0, n: words[:, bass.ds(t0, n), idx]

    def every(eng, quad):
        with eng.Fori(0, bodies) as i:
            for q in range(NQ):
                quad(i, q)
        for q in range(rest):
            quad(bodies, q)

    with nc.Block() as block:
        @block.scalar
        def _(eng):
            for q in range(NQ):
                eng.activation(stage[:, q * QUAD:(q + 1) * QUAD], index(q * QUAD, QUAD), ACT.Copy).then_inc(s_staged, 1)
            with eng.Fori(0, bodies) as i:
                for q in range(NQ):
                    eng.wait_ge(s_full[q], i * (16 * QUAD) + 16 * QUAD)
                    eng.activation(stage[:, q * QUAD:(q + 1) * QUAD], index(i * body + body + q * QUAD, QUAD),
                                   ACT.Copy).then_inc(s_staged, 1)

        @block.gpsimd
        def _(eng):
            def quad(i, q):
                eng.wait_ge(s_staged, i * NQ + q + 1)
                eng.wait_ge(s_done, i * NQ + q + 1)
                eng.sem_inc(s_go, 1)
                for t in range(q * QUAD, (q + 1) * QUAD):
                    eng.indirect_dma_start(ring[:, t, :], None, rows,
                                           bass.IndirectOffsetOnAxis(stage[:, t:t + 1], 0)).then_inc(s_full[q], 16)
            every(eng, quad)
            for q in range(NQ):
                eng.wait_ge(s_full[q], (bodies + (q < rest)) * 16 * QUAD)

        @block.vector
        def _(eng):
            def quad(i, q):
                at = i * body + q * QUAD
                eng.wait_ge(s_done, i * NQ + q + 1)
                eng.tensor_tensor(mark[:, q, :, :], k.tile_no[:, 0:P].unsqueeze(1).to_broadcast([P, QUAD, P]),
                                  words[:, bass.ds(at, QUAD), loc].unsqueeze(2).to_broadcast([P, QUAD, P]),
                                  ALU.is_equal).then_inc(s_mark, 1)
                if weight is not None:
                    eng.wait_ge(s_full[q], i * (16 * QUAD) + 16 * QUAD)
                    part = ring[:, q * QUAD:(q + 1) * QUAD, :]
                    eng.tensor_tensor(part, part, words[:, bass.ds(at, QUAD), weight].unsqueeze(2)
                                      .to_broadcast([P, QUAD, D]), ALU.mult).then_inc(s_mark, 1)
            every(eng, quad)

        @block.tensor
        def _(eng):
            per = 1 if weight is None else 2
            eng.sem_inc(s_done, NQ)
            open_banks(k, eng)
            tiles = Where(k, eng, where)

            def quad(i, q):
                at = i * body + q * QUAD
                cols, scalars = tiles.load(i * NQ + q)
                eng.wait_ge(s_mark, i * (NQ * per) + (q + 1) * per)
                if weight is None:
                    eng.wait_ge(s_full[q], i * (16 * QUAD) + 16 * QUAD)
                for j in range(QUAD):
                    row, marks = ring[:, q * QUAD + j, :], mark[:, q, j, :]
                    left, right = (row, marks) if flipped else (marks, row)
                    last = eng.matmul(k.psf[:, bass.ds(cols[j], P)], left, right, start=False, stop=False,
                                      skip_group_check=True)
                    if column == "weight":
                        last = eng.matmul(k.psf[:, bass.ds(scalars[j], 1)], marks,
                                          words[:, bass.ds(at + j, 1), weight], start=False, stop=False,
                                          skip_group_check=True)
                    if column == "one":
                        last = eng.matmul(k.psf[:, bass.ds(scalars[j], 1)], marks, k.ones[:, 0:1],
                                          start=False, stop=False, skip_group_check=True)
                last.then_inc(s_done, 1)
            every(eng, quad)
            close_banks(k, eng)
    k.end_phase()


def open_banks(k, eng):
    for b in range(NB):
        eng.matmul(k.ps[:, b, :], k.zeros[:, 0:P], k.zeros[:, :], start=True, stop=False, skip_group_check=True)


def close_banks(k, eng):
    for b in range(NB):
        eng.matmul(k.ps[:, b, :], k.zeros[:, 0:P], k.zeros[:, :], start=False, stop=True, skip_group_check=True)


def attention_pass(k, own, rows, here, w_att, b_att):
    nc = k.nc
    NQ = NQ0
    LAG = 2
    in_body, bodies = QUAD * NQ, NT // (QUAD * NQ)
    W2 = 2 * D
    ring = k.sb("ring", [P, NQ * QUAD, W2], F32, own)
    mark = k.sb("mark", [P, NQ, QUAD, P], F32, own)
    spread = k.sb("spread", [P, NQ, QUAD * P], F32, own)
    locs = k.sb("locs", [P, NQ, QUAD * P], BF16, own)
    stage = k.sb("stage", [P, NQ * QUAD], I32, own)
    dot = k.sb("dot", [P, NQ * QUAD], F32, own)
    att = k.sb("att", [P, NQ * QUAD], F32, own)
    s_full = [k.sem(f"s_full{q}") for q in range(NQ)]
    s_locs = [k.sem(f"s_locs{q}") for q in range(NQ)]
    s_staged, s_mark, s_done, s_go = (k.sem(x) for x in ("s_staged", "s_mark", "s_done", "s_go"))
    s_spread, s_exp, s_add, s_dot, s_att, s_msg = (k.sem(x) for x in ("s_spread", "s_exp", "s_add", "s_dot", "s_att", "s_msg"))
    words = k.by_dst
    index = lambda t0, n: words[:, bass.ds(t0, n), D_SRC]
    hid = k.ps[:, 7, :].rearrange("p (s c) -> p s c", s=2)

    with nc.Block() as block:
        @block.sync
        def _(eng):
            def fetch(t0, q):
                eng.dma_start(locs[:, q, :], k.loc_rows[bass.ds(t0, QUAD), :].rearrange("t e -> (t e)").partition_broadcast(P)).then_inc(s_locs[q], 16)
            for q in range(NQ):
                fetch(q * QUAD, q)
            with eng.Fori(0, bodies) as i:
                for q in range(NQ):
                    eng.wait_ge(s_spread, i * NQ + q + 1)
                    fetch(i * in_body + in_body + q * QUAD, q)
            for q in range(NQ):
                eng.wait_ge(s_locs[q], 16 * (bodies + 1))

        @block.gpsimd
        def _(eng):
            with eng.Fori(0, bodies) as i:
                for q in range(NQ):
                    eng.wait_ge(s_staged, i * NQ + q + 1)
                    eng.wait_ge(s_done, i * NQ + q + 1)
                    eng.sem_inc(s_go, 1)
                    for t in range(q * QUAD, (q + 1) * QUAD):
                        eng.indirect_dma_start(ring[:, t, :], None, rows,
                                               bass.IndirectOffsetOnAxis(stage[:, t:t + 1], 0)).then_inc(s_full[q], 16)
            for q in range(NQ):
                eng.wait_ge(s_full[q], bodies * 16 * QUAD)

        @block.vector
        def _(eng):
            def spread_quad(i, q, g):
                eng.wait_ge(s_locs[q], i * 16 + 16)
                eng.wait_ge(s_exp, g * 2 + 2)
                eng.tensor_scalar(spread[:, q, :], locs[:, q, :], k.lane[:, 0:1], None, ALU.is_equal).then_inc(s_spread, 1)

            def body(i, last):
                for q in range(NQ):
                    g = i * NQ + q
                    at = i * in_body + q * QUAD
                    if q + 1 < NQ:
                        spread_quad(i, q + 1, g + 1)
                    elif not last:
                        spread_quad(i + 1, 0, g + 1)
                    eng.wait_ge(s_done, g + 1)
                    eng.tensor_tensor(mark[:, q, :, :], k.tile_no[:, 0:P].unsqueeze(1).to_broadcast([P, QUAD, P]),
                                      words[:, bass.ds(at, QUAD), D_LOC].unsqueeze(2).to_broadcast([P, QUAD, P]),
                                      ALU.is_equal).then_inc(s_mark, 1)
                    eng.wait_ge(s_full[q], i * (16 * QUAD) + 16 * QUAD)
                    for pair in range(2):
                        t = q * QUAD + pair * 2
                        eng.wait_ge(s_exp, g * 2 + (pair + 1 + NQ * 2))
                        eng.tensor_tensor(ring[:, t:t + 2, :], ring[:, t:t + 2, :], hid, ALU.add).then_inc(s_add, 1)
                        for j in (pair * 2, pair * 2 + 1):
                            eng.wait_ge(s_add, g * 2 + (j // 2 + 2))
                            t = q * QUAD + j
                            eng.scalar_tensor_tensor(ring[:, t, D:W2], ring[:, t, D:W2], 0.0, w_att[:, :], ALU.max, ALU.mult,
                                                     accum_out=dot[:, t:t + 1]).then_inc(s_dot, 1)
            eng.sem_inc(s_add, 1)
            spread_quad(0, 0, 0)
            with eng.Fori(0, bodies - 1) as i:
                body(i, False)
            body(bodies - 1, True)

        @block.scalar
        def _(eng):
            for q in range(NQ):
                eng.activation(stage[:, q * QUAD:(q + 1) * QUAD], index(q * QUAD, QUAD), ACT.Copy).then_inc(s_staged, 1)
            with eng.Fori(0, bodies) as i:
                for q in range(NQ):
                    g = i * NQ + q
                    eng.wait_ge(s_full[q], i * (16 * QUAD) + 16 * QUAD)
                    eng.activation(stage[:, q * QUAD:(q + 1) * QUAD], index(i * in_body + in_body + q * QUAD, QUAD),
                                   ACT.Copy).then_inc(s_staged, 1)
                    eng.wait_ge(s_dot, g * QUAD + QUAD)
                    eng.activation(att[:, q * QUAD:(q + 1) * QUAD], dot[:, q * QUAD:(q + 1) * QUAD], ACT.Sigmoid,
                                   bias=b_att[:, 0:1]).then_inc(s_att, 1)
                    eng.wait_ge(s_att, g + 1)
                    for j in range(QUAD):
                        t = q * QUAD + j
                        eng.activation(ring[:, t, 0:D], ring[:, t, 0:D], ACT.Relu, scale=att[:, t:t + 1]).then_inc(s_msg, 1)

        @block.tensor
        def _(eng):
            tiles = Where(k, eng, k.where)

            def expand(g, q, pair, cols):
                eng.wait_ge(s_add, g * 2 + (pair + 1))
                for j in range(2):
                    t = pair * 2 + j
                    last = eng.matmul(hid[:, j, :], spread[:, q, t * P:(t + 1) * P], here[:, bass.ds(cols[t] * 2, W2)],
                                      start=True, stop=True)
                last.then_inc(s_exp, 1)

            def body(i, last):
                for q in range(NQ):
                    g = i * NQ + q
                    more = q + LAG < NQ or not last
                    if more:
                        ahead, _ = tiles.load(g + LAG)
                    now, scalar = tiles.load(g)
                    if more:
                        eng.wait_ge(s_spread, g + (LAG + 1))
                    eng.wait_ge(s_mark, g + 1)
                    for j in range(QUAD):
                        if more and j % 2 == 0:
                            expand(g + LAG, (q + LAG) % NQ, j // 2, ahead)
                        eng.wait_ge(s_msg, g * QUAD + (j + 1))
                        eng.matmul(k.psf[:, bass.ds(now[j], D)], mark[:, q, j, :], ring[:, q * QUAD + j, 0:D],
                                   start=False, stop=False, skip_group_check=True)
                        done = eng.matmul(k.psf[:, bass.ds(scalar[j], 1)], mark[:, q, j, :],
                                          att[:, q * QUAD + j:q * QUAD + j + 1], start=False, stop=False,
                                          skip_group_check=True)
                    done.then_inc(s_done, 1)

            eng.sem_inc(s_done, NQ)
            eng.sem_inc(s_exp, NQ * 2)
            open_banks(k, eng)
            for g in range(LAG):
                first, _ = tiles.load(g)
                eng.wait_ge(s_spread, g + 1)
                for pair in range(2):
                    expand(g, g, pair, first)
            with eng.Fori(0, bodies - 1) as i:
                body(i, False)
            body(bodies - 1, True)
            close_banks(k, eng)
    k.end_phase()


def reverse_pass(k, own):
    nc = k.nc
    body_t, bodies = QUAD * NQ, NT // (QUAD * NQ)
    quad = [P, NQ, QUAD * P]
    locs, srcs = k.sb("locs", quad, BF16, own), k.sb("srcs", quad, F32, own)
    spread = k.sb("spread", quad, F32, own)
    pairs = k.sb("pairs", quad, F32, own)
    later = k.sb("later", [P, QUAD, P], F32, own)
    twins = k.sb("twins", [P, NQ * QUAD], F32, own)
    index = k.sb("index", [P, NQ * QUAD], F32, own)
    stage = k.sb("stage", [P, NQ * QUAD], I32, own)
    spare = k.sb("spare", [P, 1], F32, own)
    edge = k.sb("edge_rows", [P, NQ * QUAD, SUM_C], F32, own)
    out = k.sb("sum_rows", [P, NQ * QUAD, SUM_C], F32, own)
    s_in = [k.sem(f"s_in{q}") for q in range(NQ)]
    s_sc = [k.sem(f"s_sum{q}") for q in range(NQ)]
    names = ("s_set", "s_spread", "s_pairs", "s_twins", "s_index", "s_exp", "s_row", "s_sum", "s_out", "s_go", "s_dve")
    s_set, s_spread, s_pairs, s_twins, s_index, s_exp, s_row, s_sum, s_out, s_go, s_dve = (k.sem(x) for x in names)
    words = k.by_dst
    h = k.h[:, :, :].rearrange("p w d -> p (w d)")
    landed = lambda i: i * (16 * QUAD)
    EXP0, ROW0, SUM0, OUT0 = NQ, 2, 2 * NQ, 4

    with nc.Block() as block:
        @block.sync
        def _(eng):
            def fetch(t0, q):
                for to, rows in ((locs, k.loc_rows), (srcs, k.src_rows)):
                    eng.dma_start(to[:, q, :], rows[bass.ds(t0, QUAD), :].rearrange("t e -> (t e)").partition_broadcast(P))\
                       .then_inc(s_in[q], 16)
            for q in range(NQ):
                fetch(q * QUAD, q)
            with eng.Fori(0, bodies - 1) as i:
                for q in range(NQ):
                    eng.wait_ge(s_index, i * NQ + q + 1)
                    fetch(i * body_t + body_t + q * QUAD, q)

        @block.vector
        def _(eng):
            c = Count(eng, s_dve)
            eng.memset(edge[:, :, D:SUM_C], 1.0).then_inc(s_set, 1)
            c.step(eng.tensor_scalar(spare[:, :], k.lane[:, :], float(NP), None, ALU.add))

            def body(i, first):
                for q in range(NQ):
                    g = i * NQ + q
                    at = i * body_t + q * QUAD
                    col = lambda j, word: words[:, bass.ds(at + j, 1), word]
                    eng.wait_ge(s_in[q], i * 32 + 32)
                    eng.wait_ge(s_exp, g + 1)
                    eng.tensor_scalar(spread[:, q, :], locs[:, q, :], k.lane[:, 0:1], None, ALU.is_equal).then_inc(s_spread, 1)
                    eng.wait_ge(s_sum, g * 2 + 2)
                    for j in range(QUAD):
                        other = srcs[:, q, j * P:(j + 1) * P]
                        eng.tensor_scalar(pairs[:, q, j * P:(j + 1) * P], other, col(j, D_SRC), col(j, D_W),
                                          ALU.is_equal, ALU.mult).then_inc(s_pairs, 1)
                        eng.scalar_tensor_tensor(later[:, j, :], other, col(j, D_SRC), k.before[:, :], ALU.is_equal, ALU.mult,
                                                 accum_out=twins[:, q * QUAD + j:q * QUAD + j + 1]).then_inc(s_twins, 1)
                    now = slice(q * QUAD, (q + 1) * QUAD)
                    src = words[:, bass.ds(at, QUAD), D_SRC]
                    c.n = g * 2 + 1
                    c.step(eng.tensor_scalar(index[:, now], src, -1.0, spare[:, 0:1], ALU.mult, ALU.add))
                    eng.wait_ge(s_twins, g * QUAD + QUAD)
                    c.step(eng.scalar_tensor_tensor(index[:, now], twins[:, now], 0.0, index[:, now], ALU.is_gt, ALU.mult))
                    if not first:
                        eng.wait_ge(s_sc[q], landed(i))
                    eng.tensor_tensor(stage[:, now], index[:, now], src, ALU.add).then_inc(s_index, 1)
            body(0, True)
            with eng.Fori(1, bodies) as i:
                body(i, False)

        @block.tensor
        def _(eng):
            eng.sem_inc(s_exp, EXP0)
            eng.sem_inc(s_row, ROW0)
            eng.sem_inc(s_sum, SUM0)
            eng.sem_inc(s_out, OUT0)
            tiles = Where(k, eng, k.where)

            def expand(g, q):
                cols, _ = tiles.load(g)
                eng.wait_ge(s_spread, g + 1)
                eng.wait_ge(s_row, g + 1)
                for j in range(QUAD):
                    last = eng.matmul(k.ps[:, q % 2, j * P:(j + 1) * P], spread[:, q, j * P:(j + 1) * P],
                                      h[:, bass.ds(cols[j], D)], start=True, stop=True)
                last.then_inc(s_exp, 1)

            def combine(g, q):
                eng.wait_ge(s_pairs, g * QUAD + QUAD)
                eng.wait_ge(s_row, g + (1 + ROW0))
                for half in range(2):
                    eng.wait_ge(s_out, g * 2 + (half + 1))
                    bank = k.ps[:, 2 + 2 * (q % 2) + half, :]
                    for m in range(2):
                        j = half * 2 + m
                        last = eng.matmul(bank[:, m * SUM_C:(m + 1) * SUM_C], pairs[:, q, j * P:(j + 1) * P],
                                          edge[:, q * QUAD + j, :], start=True, stop=True)
                    last.then_inc(s_sum, 1)

            eng.wait_ge(s_set, 1)
            expand(0, 0)
            for q in range(1, NQ):
                expand(q, q)
                combine(q - 1, q - 1)
            with eng.Fori(1, bodies) as i:
                for q in range(NQ):
                    expand(i * NQ + q, q)
                    combine(i * NQ + q - 1, (q - 1) % NQ)
            combine(bodies * NQ - 1, NQ - 1)

        @block.scalar
        def _(eng):
            def row(g, q):
                eng.wait_ge(s_exp, g + (1 + EXP0))
                eng.activation(edge[:, q * QUAD:(q + 1) * QUAD, 0:D], k.ps[:, q % 2, :].rearrange("p (t d) -> p t d", d=D),
                               ACT.Copy).then_inc(s_row, 1)

            def sums(g, q, before=None):
                if before is not None:
                    eng.wait_ge(s_sc[q], landed(before))
                for half in range(2):
                    eng.wait_ge(s_sum, g * 2 + (half + 1 + SUM0))
                    t = q * QUAD + half * 2
                    eng.activation(out[:, t:t + 2, :], k.ps[:, 2 + 2 * (q % 2) + half, 0:2 * SUM_C]
                                   .rearrange("p (t c) -> p t c", c=SUM_C), ACT.Copy).then_inc(s_out, 1)
            row(0, 0)
            for q in range(1, NQ):
                row(q, q)
                sums(q - 1, q - 1)
            row(NQ, 0)
            sums(NQ - 1, NQ - 1)
            for q in range(1, NQ):
                row(NQ + q, q)
                sums(NQ + q - 1, q - 1, 1)
            with eng.Fori(2, bodies) as i:
                for q in range(NQ):
                    row(i * NQ + q, q)
                    if q:
                        sums(i * NQ + q - 1, q - 1, i)
                    else:
                        sums(i * NQ - 1, NQ - 1, i - 1)
            sums(bodies * NQ - 1, NQ - 1, bodies - 1)

        @block.gpsimd
        def _(eng):
            def body(i, first):
                for q in range(NQ):
                    g = i * NQ + q
                    eng.wait_ge(s_index, g + 1)
                    eng.wait_ge(s_out, g * 2 + (2 + OUT0))
                    if q >= 2:
                        eng.wait_ge(s_sc[q - 2], landed(i + 1))
                    elif not first:
                        eng.wait_ge(s_sc[q + 2], landed(i))
                    eng.sem_inc(s_go, 1)
                    for j in range(QUAD):
                        t = q * QUAD + j
                        eng.indirect_dma_start(k.sums[q % 2 * QUAD + j], bass.IndirectOffsetOnAxis(stage[:, t:t + 1], 0),
                                               out[:, t, :], None, compute_op=ALU.add).then_inc(s_sc[q], 16)
            body(0, True)
            with eng.Fori(1, bodies) as i:
                body(i, False)
            for q in range(NQ):
                eng.wait_ge(s_sc[q], landed(bodies))
    k.end_phase()


def sum_copies(k, own, rows, column):
    got = k.sb("got", [P, 2, NW, SUM_C], F32, own)
    s_got, s_dve = [k.sem(f"s_got{j}") for j in range(2)], k.sem("s_dve")
    with k.nc.Block() as block:
        @block.sync
        def _(eng):
            for c in range(SUMS):
                if c >= 2:
                    eng.wait_ge(s_dve, 2 * (c - 1))
                eng.dma_start(got[:, c % 2, :, :], k.sums[c][0:NP, :].rearrange("(w p) c -> p w c", p=P))\
                   .then_inc(s_got[c % 2], 16)

        @block.vector
        def _(eng):
            count = Count(eng, s_dve)
            for c in range(SUMS):
                eng.wait_ge(s_got[c % 2], 16 * (c // 2 + 1))
                new, scalar = got[:, c % 2, :, 0:D], got[:, c % 2, :, D]
                if c:
                    count.step(eng.tensor_tensor(rows[:, :, :], rows[:, :, :], new, ALU.add))
                    count.step(eng.tensor_tensor(column, column, scalar, ALU.add))
                else:
                    count.step(eng.tensor_copy(rows[:, :, :], new))
                    count.step(eng.tensor_copy(column, scalar))
    k.end_phase()


def accumulated(k, rows, column=None):
    s_a, s_v = k.sem("s_a"), k.sem("s_v")
    flat = rows.rearrange("p w d -> p (w d)") if len(rows.shape) == 3 else rows
    with k.nc.Block() as block:
        @block.scalar
        def _(eng):
            for b, c0, n, _, _ in banks():
                if b % 2:
                    eng.activation(flat[:, c0:c0 + n], k.ps[:, b, 0:n], ACT.Copy).then_inc(s_a, 1)

        @block.vector
        def _(eng):
            for b, c0, n, _, _ in banks():
                if not b % 2:
                    eng.tensor_copy(flat[:, c0:c0 + n], k.ps[:, b, 0:n]).then_inc(s_v, 1)
            if column is not None:
                eng.tensor_copy(column, k.psf[:, COL:COL + NW]).then_inc(s_v, 1)
    k.end_phase()


def layer0(k, a):
    nc = k.nc
    own = ExitStack()
    with own:
        sb = lambda name, shape, dt=F32: k.sb(name, shape, dt, own)
        w1 = sb("w1", [P, 4 * D])
        bias1 = sb("bias1", [P, 2 * D])
        w2, b2 = sb("w2", [P, D]), sb("b2", [P, D])
        u1, u2 = sb("u1", [P, 2, D]), sb("u2", [P, D])
        c1, c2 = sb("c1", [P, 1]), sb("c2", [P, D])
        wg, bg = sb("wg", [P, D]), sb("bg", [P, D])
        w_att, b_att = sb("w_att", [P, D]), sb("b_att", [P, 1])
        glob = sb("glob", [P, D])
        here = sb("here", [P, NW, 2 * D])
        mean_wide = sb("mean_wide", [P, P])
        att_sum = sb("att_sum", [P, NW])
        mean = sb("mean", [P, 1])
        rows = nc.dram_tensor("rows0", [NP, 2 * D], F32, kind="Internal").ap()
        L = "L0_gnn_"
        wide = lambda v: a[L + v].partition_broadcast(P)
        load_all(k, [(w1[:, 0:D], a[L + "msg_W1"][0:D, :]), (w1[:, D:2 * D], a[L + "att_W1"][0:D, :]),
                     (w1[:, 2 * D:3 * D], a[L + "msg_W1"][D:2 * D, :]), (w1[:, 3 * D:4 * D], a[L + "att_W1"][D:2 * D, :]),
                     (bias1[:, 0:D], wide("msg_b1")), (bias1[:, D:2 * D], wide("att_b1")),
                     (w2[:, :], a[L + "msg_W2"]), (b2[:, :], wide("msg_b2")),
                     (u1[:, :, :], a[L + "upd_W1"].rearrange("(s p) d -> p s d", p=P)), (u2[:, :], a[L + "upd_W2"]),
                     (c1[:, :], a[L + "upd_b1"]), (c2[:, :], wide("upd_b2")),
                     (wg[:, :], a[L + "glb_W"]), (bg[:, :], wide("glb_b")),
                     (w_att[:, :], a[L + "att_W2"].partition_broadcast(P)), (b_att[:, :], wide("att_b2"))], "w0")
        s_dve, s_mean, s_g = k.sem("s_dve"), k.sem("s_mean"), k.sem("s_g")
        with nc.Block() as block:
            @block.vector
            def _(eng):
                c = Count(eng, s_dve)
                c.step(eng.tensor_reduce(mean[:, :], k.hT[:, 0:N], AX.X, ALU.add))
                c.step(eng.tensor_scalar(mean[:, :], mean[:, :], 1.0 / N, None, ALU.mult))
                eng.tensor_scalar(mean_wide[:, :], k.ones[:, 0:P], mean[:, 0:1], None, ALU.mult).then_inc(s_mean, 1)
                eng.wait_ge(s_g, 1)
                c.step(eng.tensor_tensor(glob[:, :], k.ps[:, 0, 0:D], bg[:, :], ALU.add))
                c.step(eng.scalar_tensor_tensor(glob[:, :], glob[:, :], 0.0, c2[:, :], ALU.max, ALU.add))

            @block.tensor
            def _(eng):
                eng.wait_ge(s_mean, 1)
                eng.matmul(k.ps[:, 0, 0:D], mean_wide[:, :], wg[:, :], start=True, stop=True).then_inc(s_g, 1)
        k.end_phase()

        with nc.Fori(0, 2) as _step:
            with ExitStack() as inner:
                table(k, inner, w1, 4 * D, lambda w0, n, st: [(rows[w0 * P:(w0 + n) * P, :].rearrange("(w p) d -> p w d", p=P), st)],
                      bias=bias1, keep=here, shared=2 * D)
            with ExitStack() as inner:
                attention_pass(k, inner, rows, here.rearrange("p w d -> p (w d)"), w_att, b_att)
            with ExitStack() as inner:
                agg = k.sb("agg", [P, NW, D], F32, inner)
                aggT, zT = k.sb("aggT", [P, NP], F32, inner), k.sb("zT", [P, NP], F32, inner)
                accumulated(k, agg, att_sum[:, :])
                update0(k, agg, aggT, zT, att_sum, w2, b2, u1, c1, u2, glob)
        s_x = k.sem("s_x")
        with nc.Block() as block:
            @block.vector
            def _(eng):
                eng.tensor_tensor(k.x[:, :, :], k.x[:, :, :], k.h[:, :, :], ALU.add).then_inc(s_x, 1)
        k.end_phase()


def update0(k, agg, aggT, zT, att_sum, w2, b2, u1, c1, u2, glob):
    S = {n: (k.sem(f"s_pe_{n}"), k.sem(f"s_ev_{n}")) for n in "ABCDEF"}
    s_dve = k.sem("s_dve")
    with k.nc.Block() as block:
        @block.tensor
        def _(eng):
            def stage(name, before, product):
                for b, c0, n, w0, wn in banks():
                    if before:
                        eng.wait_ge(S[before][1], b + 1)
                    last = product(b, c0, n, w0, wn)
                    last.then_inc(S[name][0], 1)

            def turned(b, c0, n, w0, wn, rows):
                for j in range(wn):
                    last = eng.transpose(k.ps[:, b, j * P:(j + 1) * P], rows[:, w0 + j, :], k.ident[:, :])
                return last

            def times(b, c0, n, w0, wn, cols, w):
                for j in range(wn):
                    last = eng.matmul(k.ps[:, b, j * P:(j + 1) * P], cols[:, (w0 + j) * P:(w0 + j + 1) * P], w[:, :],
                                      start=True, stop=True)
                return last

            def hidden(b, c0, n, w0, wn):
                eng.matmul(k.ps[:, b, 0:n], u1[:, 0, :], k.hT[:, c0:c0 + n], start=True, stop=False)
                return eng.matmul(k.ps[:, b, 0:n], u1[:, 1, :], aggT[:, c0:c0 + n], start=False, stop=True)

            stage("A", None, lambda *s: turned(*s, agg))
            stage("B", "A", lambda *s: times(*s, aggT, w2))
            stage("C", "B", lambda *s: turned(*s, agg))
            stage("D", "C", hidden)
            stage("E", "D", lambda *s: times(*s, zT, u2))
            stage("F", "E", lambda *s: turned(*s, k.h))

        @block.scalar
        def _(eng):
            for name, out in (("A", aggT), ("C", aggT), ("D", zT), ("F", k.hT)):
                for b, c0, n, _, _ in banks():
                    eng.wait_ge(S[name][0], b + 1)
                    if name == "D":
                        eng.activation(out[:, c0:c0 + n], k.ps[:, b, 0:n], ACT.Relu, bias=c1[:, 0:1]).then_inc(S[name][1], 1)
                    else:
                        eng.activation(out[:, c0:c0 + n], k.ps[:, b, 0:n], ACT.Copy).then_inc(S[name][1], 1)

        @block.vector
        def _(eng):
            c = Count(eng, s_dve)
            for b, c0, n, w0, wn in banks():
                eng.wait_ge(S["B"][0], b + 1)
                for j in range(wn):
                    ins = eng.scalar_tensor_tensor(agg[:, w0 + j, :], b2[:, :], att_sum[:, w0 + j:w0 + j + 1],
                                                   k.ps[:, b, j * P:(j + 1) * P], ALU.mult, ALU.add)
                ins.then_inc(S["B"][1], 1)
            for b, c0, n, w0, wn in banks():
                eng.wait_ge(S["E"][0], b + 1)
                part = k.h[:, w0:w0 + wn, :]
                c.step(eng.tensor_tensor(part, part, glob[:, :].unsqueeze(1).to_broadcast([P, wn, D]), ALU.add))
                eng.tensor_tensor(part, part, k.ps[:, b, 0:n].rearrange("p (w d) -> p w d", d=D), ALU.add)\
                   .then_inc(S["E"][1], 1)
    k.end_phase()


def gru(k, inputs, w_h, b_r, b_z, b_i, b_n, buf):
    r, z, t, n_ = buf
    s_pe, s_rz, s_pre, s_n, s_dve, s_new = (k.sem(x) for x in ("s_pe", "s_rz", "s_pre", "s_n", "s_dve", "s_new"))
    R, Z, I, H = range(4)
    with k.nc.Block() as block:
        @block.tensor
        def _(eng):
            for b, c0, n, _, _ in banks():
                if b >= 2:
                    eng.wait_ge(s_pre, b - 1)
                bank = lambda g: k.ps[:, (b % 2) * 4 + g, 0:n]
                for g in (R, Z, I):
                    for m, (cols, w) in enumerate(inputs):
                        eng.matmul(bank(g), w[:, g * D:(g + 1) * D], cols[:, c0:c0 + n], start=m == 0,
                                   stop=g == I and m + 1 == len(inputs))
                    if g != I:
                        eng.matmul(bank(g), w_h[:, g * D:(g + 1) * D], k.hT[:, c0:c0 + n], start=False, stop=True)
                eng.matmul(bank(H), w_h[:, 2 * D:3 * D], k.hT[:, c0:c0 + n], start=True, stop=True).then_inc(s_pe, 1)

        @block.scalar
        def _(eng):
            def gates(b, n):
                eng.wait_ge(s_pe, b + 1)
                if b >= 2:
                    eng.wait_ge(s_new, b - 1)
                eng.activation(r[:, b % 2, 0:n], k.ps[:, (b % 2) * 4 + R, 0:n], ACT.Sigmoid, bias=b_r).then_inc(s_rz, 1)
                eng.activation(z[:, b % 2, 0:n], k.ps[:, (b % 2) * 4 + Z, 0:n], ACT.Sigmoid, bias=b_z).then_inc(s_rz, 1)
            every = list(banks())
            gates(0, every[0][2])
            for b, c0, n, _, _ in every:
                if b + 1 < NB:
                    gates(b + 1, every[b + 1][2])
                eng.wait_ge(s_pre, b + 1)
                eng.activation(n_[:, b % 2, 0:n], t[:, b % 2, 0:n], ACT.Tanh, bias=b_i).then_inc(s_n, 1)

        @block.vector
        def _(eng):
            c = Count(eng, s_dve)
            for b, c0, n, _, _ in banks():
                p = b % 2
                eng.wait_ge(s_rz, 2 * b + 2)
                c.step(eng.scalar_tensor_tensor(t[:, p, 0:n], k.ps[:, p * 4 + H, 0:n], b_n, r[:, p, 0:n], ALU.add, ALU.mult))
                eng.tensor_tensor(t[:, p, 0:n], t[:, p, 0:n], k.ps[:, p * 4 + I, 0:n], ALU.add).then_inc(s_pre, 1)
                eng.wait_ge(s_n, b + 1)
                h = k.hT[:, c0:c0 + n]
                c.step(eng.tensor_tensor(h, h, n_[:, p, 0:n], ALU.subtract))
                c.step(eng.tensor_tensor(h, h, z[:, p, 0:n], ALU.mult))
                eng.tensor_tensor(h, h, n_[:, p, 0:n], ALU.add).then_inc(s_new, 1)
    k.end_phase()


def gru_weights(k, own, a, name, wide_in, more):
    ih = k.sb("w_ih", [P, wide_in, 3 * D], F32, own)
    hh = k.sb("w_hh", [P, 3 * D], F32, own)
    bi, bh = k.sb("b_ih", [P, 3], F32, own), k.sb("b_hh", [P, 3], F32, own)
    both = k.sb("b_both", [P, 3], F32, own)
    pairs = [(ih[:, :, :], a[name + "ih"].rearrange("(s p) g -> p s g", p=P)), (hh[:, :], a[name + "hh"]),
             (bi[:, :], a[name + "b_ih"]), (bh[:, :], a[name + "b_hh"])] + more
    s_load, s = k.sem("s_load"), k.sem("s_dve")
    with k.nc.Block() as block:
        @block.sync
        def _(eng):
            for dst, src in pairs:
                eng.dma_start(dst, src).then_inc(s_load, 16)
            eng.wait_ge(s_load, 16 * len(pairs))

        @block.vector
        def _(eng):
            eng.wait_ge(s_load, 16 * len(pairs))
            eng.tensor_tensor(both[:, :], bi[:, :], bh[:, :], ALU.add).then_inc(s, 1)
    k.end_phase()
    return ih, hh, both, bi, bh


def add_turned(k):
    s_tr, s_x = k.sem("s_tr"), k.sem("s_x")
    with k.nc.Block() as block:
        @block.tensor
        def _(eng):
            for b, c0, n, w0, wn in banks():
                for j in range(wn):
                    last = eng.transpose(k.ps[:, b, j * P:(j + 1) * P], k.hT[:, c0 + j * P:c0 + (j + 1) * P], k.ident[:, :])
                last.then_inc(s_tr, 1)

        @block.vector
        def _(eng):
            for b, c0, n, w0, wn in banks():
                eng.wait_ge(s_tr, b + 1)
                part = k.x[:, w0:w0 + wn, :]
                eng.tensor_tensor(part, part, k.ps[:, b, 0:n].rearrange("p (w d) -> p w d", d=D), ALU.add).then_inc(s_x, 1)
    k.end_phase()


def layer1(k, a):
    nc = k.nc
    own = ExitStack()
    with own:
        sb = lambda name, shape, dt=F32: k.sb(name, shape, dt, own)
        wn = [sb("wn1", [P, D]), sb("wn2", [P, D])]
        mean = sb("mean", [P, NW, D])
        meanT = sb("meanT", [P, NP])
        mixT = [sb("mix1", [P, NP]), sb("mix2", [P, NP])]
        total, some, safe = sb("total", [P, NW]), sb("some", [P, NW]), sb("safe", [P, NW])
        buf = [sb(f"gru{j}", [P, 2, BANK]) for j in range(4)]
        rows = nc.dram_tensor("rows1", [NP, D], F32, kind="Internal").ap()
        ih, hh, both, bi, bh = gru_weights(k, own, a, "L1_", 2, [
            (rows.rearrange("(w p) d -> p w d", p=P), k.h[:, :, :]), (wn[0][:, :], a["L1_W1T"]), (wn[1][:, :], a["L1_W2T"])])
        for m in range(2):
            if m == 0:
                with ExitStack() as inner:
                    edge_pass(k, inner, rows, k.by_dst, D_LOC, D_SRC, k.where, weight=D_W, column="weight")
                    accumulated(k, mean, total[:, :])
            else:
                with ExitStack() as inner:
                    reverse_pass(k, inner)
                with ExitStack() as inner:
                    sum_copies(k, inner, mean, total[:, :])
            s_dve, s_ready = k.sem("s_dve"), k.sem("s_ready")
            S = {n: (k.sem(f"s_pe_{n}"), k.sem(f"s_ev_{n}")) for n in "AB"}
            with nc.Block() as block:
                @block.vector
                def _(eng):
                    c = Count(eng, s_dve)
                    c.step(eng.tensor_scalar(some[:, :], total[:, :], 0.0, None, ALU.is_gt))
                    c.step(eng.tensor_scalar(safe[:, :], some[:, :], -1.0, 1.0, ALU.mult, ALU.add))
                    c.step(eng.tensor_tensor(total[:, :], total[:, :], some[:, :], ALU.mult))
                    c.step(eng.tensor_tensor(safe[:, :], safe[:, :], total[:, :], ALU.add))
                    c.step(eng.reciprocal(safe[:, :], safe[:, :]))
                    c.step(eng.tensor_tensor(safe[:, :], safe[:, :], some[:, :], ALU.mult))
                    for b, _, _, w0, n in banks():
                        part = mean[:, w0:w0 + n, :]
                        eng.tensor_tensor(part, part, safe[:, w0:w0 + n].unsqueeze(2).to_broadcast([P, n, D]), ALU.mult)\
                           .then_inc(s_ready, 1)

                @block.tensor
                def _(eng):
                    turn(k, eng, mean, s_ready, S["A"][0])
                    for b, c0, n, _, _ in banks():
                        eng.wait_ge(S["A"][1], b + 1)
                        eng.matmul(k.ps[:, b, 0:n], wn[m][:, :], meanT[:, c0:c0 + n], start=True, stop=True)\
                           .then_inc(S["B"][0], 1)

                @block.scalar
                def _(eng):
                    evacuate(k, eng, *S["A"], meanT)
                    evacuate(k, eng, *S["B"], mixT[m])
            k.end_phase()
        gru(k, [(mixT[0], ih[:, 0, :]), (mixT[1], ih[:, 1, :])], hh, both[:, 0:1], both[:, 1:2], bi[:, 2:3], bh[:, 2:3], buf)
        add_turned(k)


def layer2(k, a):
    nc = k.nc
    own = ExitStack()
    with own:
        sb = lambda name, shape, dt=F32: k.sb(name, shape, dt, own)
        we, be = sb("we", [P, T4 * D]), sb("be", [P, T4 * D])
        sumT = sb("sumT", [P, NP])
        buf = [sb(f"gru{j}", [P, 2, BANK]) for j in range(4)]
        rows = nc.dram_tensor("rows2", [T4, NP, D], F32, kind="Internal").ap()
        ih, hh, both, bi, bh = gru_weights(k, own, a, "L2_", 1, [(we[:, :], a["L2_We"]),
                                                                 (be[:, :], a["L2_be"].partition_broadcast(P))])
        with nc.Fori(0, 4) as _step:
            with ExitStack() as inner:
                table(k, inner, we, T4 * D,
                      lambda w0, n, st: [(rows[t, w0 * P:(w0 + n) * P, :].rearrange("(w p) d -> p w d", p=P), st[:, :, t * D:(t + 1) * D])
                                         for t in range(T4)],
                      bias=be)
            with ExitStack() as inner:
                edge_pass(k, inner, rows.rearrange("t n d -> (t n) d"), k.by_dst, D_LOC, D_T4, k.where, flipped=True)
            accumulated(k, sumT)
            gru(k, [(sumT, ih[:, 0, :])], hh, both[:, 0:1], both[:, 1:2], bi[:, 2:3], bh[:, 2:3], buf)
        add_turned(k)


def layer3(k, a, out):
    nc = k.nc
    own = ExitStack()
    with own:
        sb = lambda name, shape, dt=F32: k.sb(name, shape, dt, own)
        coef = sb("coef", [P, T16, 8])
        bases = sb("bases", [P, 8, D])
        loop = sb("loop", [P, D])
        agg = sb("agg", [P, NW, D])
        deg = sb("deg", [P, NW])
        rows = nc.dram_tensor("rows3", [T16, NP, D], F32, kind="Internal").ap()
        load_all(k, [(coef[:, :, :].rearrange("p r b -> p (r b)"), a["L3_gnn_coefficients"].partition_broadcast(P)),
                     (bases[:, :, :], a["L3_bases"]), (loop[:, :], a["L3_gnn_self_loop"])], "w3")
        s_dve = k.sem("s_dve")
        early = ExitStack()
        with early:
            rel = k.sb("rel", [P, T16, D], F32, early)
            part = k.sb("part3", [P, T16, D], F32, early)
            with nc.Block() as block:
                @block.vector
                def _(eng):
                    c = Count(eng, s_dve)
                    for b in range(8):
                        out_ = rel if b == 0 else part
                        c.step(eng.tensor_tensor(out_[:, :, :], bases[:, b, :].unsqueeze(1).to_broadcast([P, T16, D]),
                                                 coef[:, :, b].unsqueeze(2).to_broadcast([P, T16, D]), ALU.mult))
                        if b:
                            c.step(eng.tensor_tensor(rel[:, :, :], rel[:, :, :], part[:, :, :], ALU.add))
            k.end_phase()
            table(k, early, rel.rearrange("p r d -> p (r d)"), T16 * D,
                  lambda w0, n, st: [(rows[:, w0 * P:(w0 + 1) * P, :].rearrange("r p d -> p r d"),
                                      st[:, 0, :].rearrange("p (r d) -> p r d", d=D))])
        late = ExitStack()
        with late:
            edge_pass(k, late, rows.rearrange("r n d -> (r n) d"), k.by_dst, D_LOC, D_T16, k.where, column="one")
            accumulated(k, agg, deg[:, :])
        s_mm, s_out, s_x = k.sem("s_mm"), k.sem("s_out"), k.sem("s_x")
        with nc.Block() as block:
            @block.tensor
            def _(eng):
                for b, c0, n, w0, wn in banks():
                    for j in range(wn):
                        last = eng.matmul(k.ps[:, b, j * P:(j + 1) * P], k.hT[:, c0 + j * P:c0 + (j + 1) * P], loop[:, :],
                                          start=True, stop=True)
                    last.then_inc(s_mm, 1)

            @block.vector
            def _(eng):
                c = Count(eng, s_dve)
                c.step(eng.tensor_scalar(deg[:, :], deg[:, :], 1.0, None, ALU.max))
                c.step(eng.reciprocal(deg[:, :], deg[:, :]))
                for b, c0, n, w0, wn in banks():
                    part, x = agg[:, w0:w0 + wn, :], k.x[:, w0:w0 + wn, :]
                    c.step(eng.tensor_tensor(part, part, deg[:, w0:w0 + wn].unsqueeze(2).to_broadcast([P, wn, D]), ALU.mult))
                    eng.wait_ge(s_mm, b + 1)
                    c.step(eng.tensor_tensor(part, part, k.ps[:, b, 0:n].rearrange("p (w d) -> p w d", d=D), ALU.add))
                    eng.tensor_tensor(x, x, part, ALU.add).then_inc(s_x, 1)

            @block.sync
            def _(eng):
                eng.wait_ge(s_x, NB)
                eng.dma_start(out[0:(NW - 1) * P, :].rearrange("(w p) d -> p w d", p=P), k.x[:, 0:NW - 1, :]).then_inc(s_out, 16)
                eng.dma_start(out[(NW - 1) * P:N, :], k.x[0:TAIL, NW - 1, :]).then_inc(s_out, 16)
                eng.wait_ge(s_out, 32)


def build(nc, a, out):
    with ExitStack() as ctx:
        k = Program(nc, ctx)
        constants(k)
        k.psf = k.ps[:, :, :].rearrange("p b c -> p (b c)")
        route(k, a)
        layer0(k, a)
        normalise(k)
        layer1(k, a)
        normalise(k)
        layer2(k, a)
        normalise(k)
        layer3(k, a, out)


def kernel(**inputs):
    import concourse.bacc as bacc
    from concourse.bass_utils import run_bass_kernel_spmd as run
    nc = bacc.Bacc("TRN2", target_bir_lowering=False, num_devices=1)
    v = {n: np.asarray(x) for n, x in inputs.items()}
    laid = {n: v[n] for n in ("x", "src", "dst", "edge_attr_4", "edge_type_16", "edge_weight", "L3_gnn_self_loop")}
    laid.update({n: v[n] for n in v if n.startswith("L0_")})
    laid["L0_gnn_upd_b1"] = v["L0_gnn_upd_b1"].reshape(D, 1)
    laid["L0_gnn_att_W2"] = v["L0_gnn_att_W2"].reshape(D)
    laid["L1_W1T"], laid["L1_W2T"] = v["L1_gnn_W1"].T, v["L1_gnn_W2"].T
    laid["L2_We"] = v["L2_gnn_W_edge"].transpose(2, 0, 1).reshape(D, T4 * D)
    laid["L2_be"] = v["L2_gnn_b_edge"].reshape(T4 * D)
    for l, ih, hh in (("L1_", "L1_gnn_w_ih", "L1_gnn_w_hh"), ("L2_", "L2_gnn_W_ih", "L2_gnn_W_hh")):
        laid[l + "ih"], laid[l + "hh"] = v[ih].T, v[hh].T
        for b in ("b_ih", "b_hh"):
            laid[l + b] = v[l + "gnn_" + b].reshape(3, D).T
    laid["L3_bases"] = v["L3_gnn_bases"].transpose(1, 0, 2)
    laid["L3_gnn_coefficients"] = v["L3_gnn_coefficients"].reshape(-1)
    arrays, aps = {}, {}
    for n, x in laid.items():
        x = np.ascontiguousarray(x)
        arrays[n + "_dram"] = x
        aps[n] = nc.dram_tensor(n + "_dram", x.shape, mybir.dt.from_np(x.dtype), kind="ExternalInput").ap()
    out = nc.dram_tensor("out_dram", (N, D), F32, kind="ExternalOutput").ap()
    build(nc, aps, out)
    r = run(nc, [arrays], core_ids=[0])
    return r.results[0]["out_dram"]
```
